# Optimizing a Trainium2 kernel written in Bass

```python
import numpy as np
import jax
import jax.numpy as jnp

def _softmax(x, axis=-1):
    return jax.nn.softmax(x, axis=axis)
def _gelu(x):
    return jax.nn.gelu(x, approximate=True)
def _silu(x):
    return jax.nn.silu(x)
def _sigmoid(x):
    return jax.nn.sigmoid(x)
def _layernorm(x, axis=-1, eps=1e-5):
    m = jnp.mean(x, axis=axis, keepdims=True)
    v = jnp.var(x, axis=axis, keepdims=True)
    return (x - m) / jnp.sqrt(v + eps)
def _scatter_add(tgt, idx, src, axis=0):
    return tgt.at[idx].add(src)
def _segment_sum(src, seg, n):
    return jax.ops.segment_sum(src, seg, n)

kernel_name = 'mk_conv_preact_d4_conv_nchw512_e7838a'

def setup_inputs(seed: int = 0):
    np.random.seed(seed)
    _w = jnp.asarray
    def _rec_inputs():
        import jax
        import jax.numpy as jnp
        _gk = jax.random.key(seed)
        x = -0.0002928 + 1 * jax.random.normal(jax.random.fold_in(_gk, 1), (8, 512, 32, 32), jnp.float32)
        return x
    x = _rec_inputs()
    def _L0_conv_setup():
        import jax, jax.numpy as jnp
        from jax import lax
        import numpy as np
        D_IN = 512
        HID = 128
        D_INNER = 2 * HID
        D_PROJ = 2 * D_INNER
        N_STATE = 16
        R_DT = 8
        B, H, W = (8, 32, 32)

        def _layernorm(y, g, b):
            mu = y.mean(-1, keepdims=True)
            var = ((y - mu) ** 2).mean(-1, keepdims=True)
            return (y - mu) / jnp.sqrt(var + 1e-05) * g + b

        def _ssm(x, xw, dtw, dtb, Al, Dv, g, be):
            Bb, D, L = x.shape
            n = Al.shape[1]
            xd = jnp.einsum('bdl,kd->blk', x, xw)
            dts = xd[..., :R_DT]
            Bs = xd[..., R_DT:R_DT + n]
            Cs = xd[..., R_DT + n:]
            delta = jax.nn.softplus(jnp.einsum('blr,dr->bld', dts, dtw) + dtb)
            A = -jnp.exp(Al)
            xt = x.transpose(0, 2, 1)
            dA = jnp.exp(delta[..., None] * A)
            dBx = delta[..., None] * Bs[:, :, None, :] * xt[..., None]

            def step(h, inp):
                da, dbx, c = inp
                h = h * da + dbx
                return (h, jnp.einsum('bdn,bn->bd', h, c))
            h0 = jnp.zeros((Bb, D, n), x.dtype)
            _, ys = lax.scan(step, h0, (dA.transpose(1, 0, 2, 3), dBx.transpose(1, 0, 2, 3), Cs.transpose(1, 0, 2)))
            y = ys.transpose(1, 0, 2) + xt * Dv
            return _layernorm(y, g, be)

        def _up2(y, h, w):
            Bb, L, C = y.shape
            img = y.transpose(0, 2, 1).reshape(Bb, C, h, w)
            img = jnp.repeat(jnp.repeat(img, 2, axis=2), 2, axis=3)
            return img.reshape(Bb, C, 4 * L).transpose(0, 2, 1)

        def _conv1x1(x, w, b):
            return jnp.einsum('bchw,oc->bohw', x, w) + b[None, :, None, None]

        def _conv2s2(x, w, b):
            out = lax.conv_general_dilated(x, w, (2, 2), 'VALID', dimension_numbers=('NCHW', 'OIHW', 'NCHW'))
            return out + b[None, :, None, None]

        def _forward(input_f, in_w, in_b, c1_w, c1_b, c2_w, c2_b, c3_w, c3_b, out_w, out_b, xw1, dtw1, dtb1, Al1, Dv1, g1, be1, xw2, dtw2, dtb2, Al2, Dv2, g2, be2, xw3, dtw3, dtb3, Al3, Dv3, g3, be3):
            xz = _conv1x1(input_f, in_w, in_b)
            x, z = jnp.split(xz, 2, axis=1)
            f1 = _conv1x1(x, c1_w, c1_b)
            f2 = _conv2s2(f1, c2_w, c2_b)
            f3 = _conv2s2(f2, c3_w, c3_b)
            Bb, C, h3, w3 = f3.shape
            fx3 = f3.reshape(Bb, C, h3 * w3)
            y3 = _ssm(fx3, xw3, dtw3, dtb3, Al3, Dv3, g3, be3) + jnp.flip(_ssm(jnp.flip(fx3, -1), xw3, dtw3, dtb3, Al3, Dv3, g3, be3), 1)
            y2_ = _up2(y3, h3, w3)
            _, _, h2, w2 = f2.shape
            fx2 = f2.reshape(Bb, C, h2 * w2)
            y2 = _ssm(fx2, xw2, dtw2, dtb2, Al2, Dv2, g2, be2) + jnp.flip(_ssm(jnp.flip(fx2, -1), xw2, dtw2, dtb2, Al2, Dv2, g2, be2), 1) + y2_
            y1_ = _up2(y2, h2, w2)
            _, _, h1, w1 = f1.shape
            fx1 = f1.reshape(Bb, C, h1 * w1)
            y1 = _ssm(fx1, xw1, dtw1, dtb1, Al1, Dv1, g1, be1) + jnp.flip(_ssm(jnp.flip(fx1, -1), xw2, dtw2, dtb2, Al2, Dv2, g2, be2), 1) + y1_
            out1 = y1.transpose(0, 2, 1).reshape(Bb, C, h1, w1)
            out = out1 * jax.nn.silu(z)
            return _conv1x1(out, out_w, out_b)
        key = jax.random.key(seed)
        ks = iter(jax.random.split(key, 64))

        def nrm(shape, s=0.05):
            return jax.random.normal(next(ks), shape, dtype=jnp.float32) * s
        inp = {'input_f': jax.random.normal(next(ks), (B, D_IN, H, W), dtype=jnp.float32), 'in_w': nrm((D_PROJ, D_IN)), 'in_b': nrm((D_PROJ,)), 'c1_w': nrm((D_INNER, D_INNER)), 'c1_b': nrm((D_INNER,)), 'c2_w': nrm((D_INNER, D_INNER, 2, 2)), 'c2_b': nrm((D_INNER,)), 'c3_w': nrm((D_INNER, D_INNER, 2, 2)), 'c3_b': nrm((D_INNER,)), 'out_w': nrm((D_IN, D_INNER)), 'out_b': nrm((D_IN,))}
        Al = jnp.log(jnp.tile(jnp.arange(1, N_STATE + 1, dtype=jnp.float32), (D_INNER, 1)))
        for i in (1, 2, 3):
            inp[f'xw{i}'] = nrm((R_DT + 2 * N_STATE, D_INNER))
            inp[f'dtw{i}'] = nrm((D_INNER, R_DT), s=R_DT ** (-0.5))
            inp[f'dtb{i}'] = nrm((D_INNER,)) - 4.0
            inp[f'Al{i}'] = Al
            inp[f'Dv{i}'] = jnp.ones((D_INNER,), jnp.float32)
            inp[f'g{i}'] = jnp.ones((D_INNER,), jnp.float32)
            inp[f'be{i}'] = jnp.zeros((D_INNER,), jnp.float32)
        return inp
    _L0_conv_all = _L0_conv_setup()
    _L0_conv_in = {k: v for k, v in _L0_conv_all.items() if k in ('in_w', 'in_b', 'c1_w', 'c1_b', 'c2_w', 'c2_b', 'c3_w', 'c3_b', 'out_w', 'out_b', 'xw1', 'dtw1', 'dtb1', 'Al1', 'Dv1', 'g1', 'be1', 'xw2', 'dtw2', 'dtb2', 'Al2', 'Dv2', 'g2', 'be2', 'xw3', 'dtw3', 'dtb3', 'Al3', 'Dv3', 'g3', 'be3', )}
    del _L0_conv_all

    def _L1_conv_setup():
        import jax, jax.numpy as jnp
        import numpy as np
        PAD0, PAD1 = (2, 1)

        def make_kernel(k1d):
            k = jnp.asarray(k1d, dtype=jnp.float32)
            k = k[None, :] * k[:, None]
            return k / k.sum()
        key = jax.random.key(seed)
        x = jax.random.normal(key, (16, 512, 64, 64), dtype=jnp.float32)
        kernel = make_kernel([1.0, 3.0, 3.0, 1.0])
        return {'x': x, 'kernel': kernel}
    _L1_conv_all = _L1_conv_setup()
    _L1_conv_in = {k: v for k, v in _L1_conv_all.items() if k in ('kernel', )}
    del _L1_conv_all

    def _L2_conv_setup():
        import jax, jax.numpy as jnp
        from jax import lax
        import numpy as np
        D_IN = 512
        HID = 128
        D_INNER = 2 * HID
        D_PROJ = 2 * D_INNER
        N_STATE = 16
        R_DT = 8
        B, H, W = (8, 32, 32)

        def _layernorm(y, g, b):
            mu = y.mean(-1, keepdims=True)
            var = ((y - mu) ** 2).mean(-1, keepdims=True)
            return (y - mu) / jnp.sqrt(var + 1e-05) * g + b

        def _ssm(x, xw, dtw, dtb, Al, Dv, g, be):
            Bb, D, L = x.shape
            n = Al.shape[1]
            xd = jnp.einsum('bdl,kd->blk', x, xw)
            dts = xd[..., :R_DT]
            Bs = xd[..., R_DT:R_DT + n]
            Cs = xd[..., R_DT + n:]
            delta = jax.nn.softplus(jnp.einsum('blr,dr->bld', dts, dtw) + dtb)
            A = -jnp.exp(Al)
            xt = x.transpose(0, 2, 1)
            dA = jnp.exp(delta[..., None] * A)
            dBx = delta[..., None] * Bs[:, :, None, :] * xt[..., None]

            def step(h, inp):
                da, dbx, c = inp
                h = h * da + dbx
                return (h, jnp.einsum('bdn,bn->bd', h, c))
            h0 = jnp.zeros((Bb, D, n), x.dtype)
            _, ys = lax.scan(step, h0, (dA.transpose(1, 0, 2, 3), dBx.transpose(1, 0, 2, 3), Cs.transpose(1, 0, 2)))
            y = ys.transpose(1, 0, 2) + xt * Dv
            return _layernorm(y, g, be)

        def _up2(y, h, w):
            Bb, L, C = y.shape
            img = y.transpose(0, 2, 1).reshape(Bb, C, h, w)
            img = jnp.repeat(jnp.repeat(img, 2, axis=2), 2, axis=3)
            return img.reshape(Bb, C, 4 * L).transpose(0, 2, 1)

        def _conv1x1(x, w, b):
            return jnp.einsum('bchw,oc->bohw', x, w) + b[None, :, None, None]

        def _conv2s2(x, w, b):
            out = lax.conv_general_dilated(x, w, (2, 2), 'VALID', dimension_numbers=('NCHW', 'OIHW', 'NCHW'))
            return out + b[None, :, None, None]

        def _forward(input_f, in_w, in_b, c1_w, c1_b, c2_w, c2_b, c3_w, c3_b, out_w, out_b, xw1, dtw1, dtb1, Al1, Dv1, g1, be1, xw2, dtw2, dtb2, Al2, Dv2, g2, be2, xw3, dtw3, dtb3, Al3, Dv3, g3, be3):
            xz = _conv1x1(input_f, in_w, in_b)
            x, z = jnp.split(xz, 2, axis=1)
            f1 = _conv1x1(x, c1_w, c1_b)
            f2 = _conv2s2(f1, c2_w, c2_b)
            f3 = _conv2s2(f2, c3_w, c3_b)
            Bb, C, h3, w3 = f3.shape
            fx3 = f3.reshape(Bb, C, h3 * w3)
            y3 = _ssm(fx3, xw3, dtw3, dtb3, Al3, Dv3, g3, be3) + jnp.flip(_ssm(jnp.flip(fx3, -1), xw3, dtw3, dtb3, Al3, Dv3, g3, be3), 1)
            y2_ = _up2(y3, h3, w3)
            _, _, h2, w2 = f2.shape
            fx2 = f2.reshape(Bb, C, h2 * w2)
            y2 = _ssm(fx2, xw2, dtw2, dtb2, Al2, Dv2, g2, be2) + jnp.flip(_ssm(jnp.flip(fx2, -1), xw2, dtw2, dtb2, Al2, Dv2, g2, be2), 1) + y2_
            y1_ = _up2(y2, h2, w2)
            _, _, h1, w1 = f1.shape
            fx1 = f1.reshape(Bb, C, h1 * w1)
            y1 = _ssm(fx1, xw1, dtw1, dtb1, Al1, Dv1, g1, be1) + jnp.flip(_ssm(jnp.flip(fx1, -1), xw2, dtw2, dtb2, Al2, Dv2, g2, be2), 1) + y1_
            out1 = y1.transpose(0, 2, 1).reshape(Bb, C, h1, w1)
            out = out1 * jax.nn.silu(z)
            return _conv1x1(out, out_w, out_b)
        key = jax.random.key(seed)
        ks = iter(jax.random.split(key, 64))

        def nrm(shape, s=0.05):
            return jax.random.normal(next(ks), shape, dtype=jnp.float32) * s
        inp = {'input_f': jax.random.normal(next(ks), (B, D_IN, H, W), dtype=jnp.float32), 'in_w': nrm((D_PROJ, D_IN)), 'in_b': nrm((D_PROJ,)), 'c1_w': nrm((D_INNER, D_INNER)), 'c1_b': nrm((D_INNER,)), 'c2_w': nrm((D_INNER, D_INNER, 2, 2)), 'c2_b': nrm((D_INNER,)), 'c3_w': nrm((D_INNER, D_INNER, 2, 2)), 'c3_b': nrm((D_INNER,)), 'out_w': nrm((D_IN, D_INNER)), 'out_b': nrm((D_IN,))}
        Al = jnp.log(jnp.tile(jnp.arange(1, N_STATE + 1, dtype=jnp.float32), (D_INNER, 1)))
        for i in (1, 2, 3):
            inp[f'xw{i}'] = nrm((R_DT + 2 * N_STATE, D_INNER))
            inp[f'dtw{i}'] = nrm((D_INNER, R_DT), s=R_DT ** (-0.5))
            inp[f'dtb{i}'] = nrm((D_INNER,)) - 4.0
            inp[f'Al{i}'] = Al
            inp[f'Dv{i}'] = jnp.ones((D_INNER,), jnp.float32)
            inp[f'g{i}'] = jnp.ones((D_INNER,), jnp.float32)
            inp[f'be{i}'] = jnp.zeros((D_INNER,), jnp.float32)
        return inp
    _L2_conv_all = _L2_conv_setup()
    _L2_conv_in = {k: v for k, v in _L2_conv_all.items() if k in ('in_w', 'in_b', 'c1_w', 'c1_b', 'c2_w', 'c2_b', 'c3_w', 'c3_b', 'out_w', 'out_b', 'xw1', 'dtw1', 'dtb1', 'Al1', 'Dv1', 'g1', 'be1', 'xw2', 'dtw2', 'dtb2', 'Al2', 'Dv2', 'g2', 'be2', 'xw3', 'dtw3', 'dtb3', 'Al3', 'Dv3', 'g3', 'be3', )}
    del _L2_conv_all

    def _L3_conv_setup():
        import jax, jax.numpy as jnp
        import numpy as np
        B, C, H, W = (8, 512, 32, 32)
        HEADS = 8
        DIM = C // HEADS
        EPS = 1e-05
        key = jax.random.key(seed)
        ks = jax.random.split(key, 7)
        scale = 1.0 / np.sqrt(C)
        return {'x': jax.random.normal(ks[0], (B, C, H, W), dtype=jnp.float32), 'gn_gamma': jnp.ones((C,), dtype=jnp.float32), 'gn_beta': jnp.zeros((C,), dtype=jnp.float32), 'w_qkv': jax.random.normal(ks[1], (3 * HEADS * DIM, C), dtype=jnp.float32) * scale, 'b_qkv': jax.random.normal(ks[2], (3 * HEADS * DIM,), dtype=jnp.float32) * 0.01, 'w_proj': jax.random.normal(ks[3], (C, HEADS * DIM), dtype=jnp.float32) * scale, 'b_proj': jax.random.normal(ks[4], (C,), dtype=jnp.float32) * 0.01}
    _L3_conv_all = _L3_conv_setup()
    _L3_conv_in = {k: v for k, v in _L3_conv_all.items() if k in ('gn_gamma', 'gn_beta', 'w_qkv', 'b_qkv', 'w_proj', 'b_proj', )}
    del _L3_conv_all

    return {
        "x": x,
        "L0_conv_in_w": _L0_conv_in["in_w"],
        "L0_conv_in_b": _L0_conv_in["in_b"],
        "L0_conv_c1_w": _L0_conv_in["c1_w"],
        "L0_conv_c1_b": _L0_conv_in["c1_b"],
        "L0_conv_c2_w": _L0_conv_in["c2_w"],
        "L0_conv_c2_b": _L0_conv_in["c2_b"],
        "L0_conv_c3_w": _L0_conv_in["c3_w"],
        "L0_conv_c3_b": _L0_conv_in["c3_b"],
        "L0_conv_out_w": _L0_conv_in["out_w"],
        "L0_conv_out_b": _L0_conv_in["out_b"],
        "L0_conv_xw1": _L0_conv_in["xw1"],
        "L0_conv_dtw1": _L0_conv_in["dtw1"],
        "L0_conv_dtb1": _L0_conv_in["dtb1"],
        "L0_conv_Al1": _L0_conv_in["Al1"],
        "L0_conv_Dv1": _L0_conv_in["Dv1"],
        "L0_conv_g1": _L0_conv_in["g1"],
        "L0_conv_be1": _L0_conv_in["be1"],
        "L0_conv_xw2": _L0_conv_in["xw2"],
        "L0_conv_dtw2": _L0_conv_in["dtw2"],
        "L0_conv_dtb2": _L0_conv_in["dtb2"],
        "L0_conv_Al2": _L0_conv_in["Al2"],
        "L0_conv_Dv2": _L0_conv_in["Dv2"],
        "L0_conv_g2": _L0_conv_in["g2"],
        "L0_conv_be2": _L0_conv_in["be2"],
        "L0_conv_xw3": _L0_conv_in["xw3"],
        "L0_conv_dtw3": _L0_conv_in["dtw3"],
        "L0_conv_dtb3": _L0_conv_in["dtb3"],
        "L0_conv_Al3": _L0_conv_in["Al3"],
        "L0_conv_Dv3": _L0_conv_in["Dv3"],
        "L0_conv_g3": _L0_conv_in["g3"],
        "L0_conv_be3": _L0_conv_in["be3"],
        "L1_conv_kernel": _L1_conv_in["kernel"],
        "L2_conv_in_w": _L2_conv_in["in_w"],
        "L2_conv_in_b": _L2_conv_in["in_b"],
        "L2_conv_c1_w": _L2_conv_in["c1_w"],
        "L2_conv_c1_b": _L2_conv_in["c1_b"],
        "L2_conv_c2_w": _L2_conv_in["c2_w"],
        "L2_conv_c2_b": _L2_conv_in["c2_b"],
        "L2_conv_c3_w": _L2_conv_in["c3_w"],
        "L2_conv_c3_b": _L2_conv_in["c3_b"],
        "L2_conv_out_w": _L2_conv_in["out_w"],
        "L2_conv_out_b": _L2_conv_in["out_b"],
        "L2_conv_xw1": _L2_conv_in["xw1"],
        "L2_conv_dtw1": _L2_conv_in["dtw1"],
        "L2_conv_dtb1": _L2_conv_in["dtb1"],
        "L2_conv_Al1": _L2_conv_in["Al1"],
        "L2_conv_Dv1": _L2_conv_in["Dv1"],
        "L2_conv_g1": _L2_conv_in["g1"],
        "L2_conv_be1": _L2_conv_in["be1"],
        "L2_conv_xw2": _L2_conv_in["xw2"],
        "L2_conv_dtw2": _L2_conv_in["dtw2"],
        "L2_conv_dtb2": _L2_conv_in["dtb2"],
        "L2_conv_Al2": _L2_conv_in["Al2"],
        "L2_conv_Dv2": _L2_conv_in["Dv2"],
        "L2_conv_g2": _L2_conv_in["g2"],
        "L2_conv_be2": _L2_conv_in["be2"],
        "L2_conv_xw3": _L2_conv_in["xw3"],
        "L2_conv_dtw3": _L2_conv_in["dtw3"],
        "L2_conv_dtb3": _L2_conv_in["dtb3"],
        "L2_conv_Al3": _L2_conv_in["Al3"],
        "L2_conv_Dv3": _L2_conv_in["Dv3"],
        "L2_conv_g3": _L2_conv_in["g3"],
        "L2_conv_be3": _L2_conv_in["be3"],
        "L3_conv_gn_gamma": _L3_conv_in["gn_gamma"],
        "L3_conv_gn_beta": _L3_conv_in["gn_beta"],
        "L3_conv_w_qkv": _L3_conv_in["w_qkv"],
        "L3_conv_b_qkv": _L3_conv_in["b_qkv"],
        "L3_conv_w_proj": _L3_conv_in["w_proj"],
        "L3_conv_b_proj": _L3_conv_in["b_proj"],
    }

def reference(x, L0_conv_in_w, L0_conv_in_b, L0_conv_c1_w, L0_conv_c1_b, L0_conv_c2_w, L0_conv_c2_b, L0_conv_c3_w, L0_conv_c3_b, L0_conv_out_w, L0_conv_out_b, L0_conv_xw1, L0_conv_dtw1, L0_conv_dtb1, L0_conv_Al1, L0_conv_Dv1, L0_conv_g1, L0_conv_be1, L0_conv_xw2, L0_conv_dtw2, L0_conv_dtb2, L0_conv_Al2, L0_conv_Dv2, L0_conv_g2, L0_conv_be2, L0_conv_xw3, L0_conv_dtw3, L0_conv_dtb3, L0_conv_Al3, L0_conv_Dv3, L0_conv_g3, L0_conv_be3, L1_conv_kernel, L2_conv_in_w, L2_conv_in_b, L2_conv_c1_w, L2_conv_c1_b, L2_conv_c2_w, L2_conv_c2_b, L2_conv_c3_w, L2_conv_c3_b, L2_conv_out_w, L2_conv_out_b, L2_conv_xw1, L2_conv_dtw1, L2_conv_dtb1, L2_conv_Al1, L2_conv_Dv1, L2_conv_g1, L2_conv_be1, L2_conv_xw2, L2_conv_dtw2, L2_conv_dtb2, L2_conv_Al2, L2_conv_Dv2, L2_conv_g2, L2_conv_be2, L2_conv_xw3, L2_conv_dtw3, L2_conv_dtb3, L2_conv_Al3, L2_conv_Dv3, L2_conv_g3, L2_conv_be3, L3_conv_gn_gamma, L3_conv_gn_beta, L3_conv_w_qkv, L3_conv_b_qkv, L3_conv_w_proj, L3_conv_b_proj):
    import jax
    import jax.numpy as jnp
    def _L0_conv_ref(input_f, in_w, in_b, c1_w, c1_b, c2_w, c2_b, c3_w, c3_b, out_w, out_b, xw1, dtw1, dtb1, Al1, Dv1, g1, be1, xw2, dtw2, dtb2, Al2, Dv2, g2, be2, xw3, dtw3, dtb3, Al3, Dv3, g3, be3):
        import jax, jax.numpy as jnp
        from jax import lax
        import numpy as np
        D_IN = 512
        HID = 128
        D_INNER = 2 * HID
        D_PROJ = 2 * D_INNER
        N_STATE = 16
        R_DT = 8
        B, H, W = (8, 32, 32)

        def _layernorm(y, g, b):
            mu = y.mean(-1, keepdims=True)
            var = ((y - mu) ** 2).mean(-1, keepdims=True)
            return (y - mu) / jnp.sqrt(var + 1e-05) * g + b

        def _ssm(x, xw, dtw, dtb, Al, Dv, g, be):
            Bb, D, L = x.shape
            n = Al.shape[1]
            xd = jnp.einsum('bdl,kd->blk', x, xw)
            dts = xd[..., :R_DT]
            Bs = xd[..., R_DT:R_DT + n]
            Cs = xd[..., R_DT + n:]
            delta = jax.nn.softplus(jnp.einsum('blr,dr->bld', dts, dtw) + dtb)
            A = -jnp.exp(Al)
            xt = x.transpose(0, 2, 1)
            dA = jnp.exp(delta[..., None] * A)
            dBx = delta[..., None] * Bs[:, :, None, :] * xt[..., None]

            def step(h, inp):
                da, dbx, c = inp
                h = h * da + dbx
                return (h, jnp.einsum('bdn,bn->bd', h, c))
            h0 = jnp.zeros((Bb, D, n), x.dtype)
            _, ys = lax.scan(step, h0, (dA.transpose(1, 0, 2, 3), dBx.transpose(1, 0, 2, 3), Cs.transpose(1, 0, 2)))
            y = ys.transpose(1, 0, 2) + xt * Dv
            return _layernorm(y, g, be)

        def _up2(y, h, w):
            Bb, L, C = y.shape
            img = y.transpose(0, 2, 1).reshape(Bb, C, h, w)
            img = jnp.repeat(jnp.repeat(img, 2, axis=2), 2, axis=3)
            return img.reshape(Bb, C, 4 * L).transpose(0, 2, 1)

        def _conv1x1(x, w, b):
            return jnp.einsum('bchw,oc->bohw', x, w) + b[None, :, None, None]

        def _conv2s2(x, w, b):
            out = lax.conv_general_dilated(x, w, (2, 2), 'VALID', dimension_numbers=('NCHW', 'OIHW', 'NCHW'))
            return out + b[None, :, None, None]

        def _forward(input_f, in_w, in_b, c1_w, c1_b, c2_w, c2_b, c3_w, c3_b, out_w, out_b, xw1, dtw1, dtb1, Al1, Dv1, g1, be1, xw2, dtw2, dtb2, Al2, Dv2, g2, be2, xw3, dtw3, dtb3, Al3, Dv3, g3, be3):
            xz = _conv1x1(input_f, in_w, in_b)
            x, z = jnp.split(xz, 2, axis=1)
            f1 = _conv1x1(x, c1_w, c1_b)
            f2 = _conv2s2(f1, c2_w, c2_b)
            f3 = _conv2s2(f2, c3_w, c3_b)
            Bb, C, h3, w3 = f3.shape
            fx3 = f3.reshape(Bb, C, h3 * w3)
            y3 = _ssm(fx3, xw3, dtw3, dtb3, Al3, Dv3, g3, be3) + jnp.flip(_ssm(jnp.flip(fx3, -1), xw3, dtw3, dtb3, Al3, Dv3, g3, be3), 1)
            y2_ = _up2(y3, h3, w3)
            _, _, h2, w2 = f2.shape
            fx2 = f2.reshape(Bb, C, h2 * w2)
            y2 = _ssm(fx2, xw2, dtw2, dtb2, Al2, Dv2, g2, be2) + jnp.flip(_ssm(jnp.flip(fx2, -1), xw2, dtw2, dtb2, Al2, Dv2, g2, be2), 1) + y2_
            y1_ = _up2(y2, h2, w2)
            _, _, h1, w1 = f1.shape
            fx1 = f1.reshape(Bb, C, h1 * w1)
            y1 = _ssm(fx1, xw1, dtw1, dtb1, Al1, Dv1, g1, be1) + jnp.flip(_ssm(jnp.flip(fx1, -1), xw2, dtw2, dtb2, Al2, Dv2, g2, be2), 1) + y1_
            out1 = y1.transpose(0, 2, 1).reshape(Bb, C, h1, w1)
            out = out1 * jax.nn.silu(z)
            return _conv1x1(out, out_w, out_b)
        return _forward(input_f, in_w, in_b, c1_w, c1_b, c2_w, c2_b, c3_w, c3_b, out_w, out_b, xw1, dtw1, dtb1, Al1, Dv1, g1, be1, xw2, dtw2, dtb2, Al2, Dv2, g2, be2, xw3, dtw3, dtb3, Al3, Dv3, g3, be3)

    def _L1_conv_ref(x, kernel):
        import jax, jax.numpy as jnp
        import numpy as np
        PAD0, PAD1 = (2, 1)

        def make_kernel(k1d):
            k = jnp.asarray(k1d, dtype=jnp.float32)
            k = k[None, :] * k[:, None]
            return k / k.sum()
        N, C, H, W = x.shape
        kh, kw = kernel.shape
        w = jnp.flip(kernel, (0, 1))[None, None]
        xr = x.reshape(N * C, 1, H, W)
        out = jax.lax.conv_general_dilated(xr, w, window_strides=(1, 1), padding=((PAD0, PAD1), (PAD0, PAD1)), dimension_numbers=('NCHW', 'OIHW', 'NCHW'))
        Ho = H + PAD0 + PAD1 - kh + 1
        Wo = W + PAD0 + PAD1 - kw + 1
        return out.reshape(N, C, Ho, Wo)

    def _L2_conv_ref(input_f, in_w, in_b, c1_w, c1_b, c2_w, c2_b, c3_w, c3_b, out_w, out_b, xw1, dtw1, dtb1, Al1, Dv1, g1, be1, xw2, dtw2, dtb2, Al2, Dv2, g2, be2, xw3, dtw3, dtb3, Al3, Dv3, g3, be3):
        import jax, jax.numpy as jnp
        from jax import lax
        import numpy as np
        D_IN = 512
        HID = 128
        D_INNER = 2 * HID
        D_PROJ = 2 * D_INNER
        N_STATE = 16
        R_DT = 8
        B, H, W = (8, 32, 32)

        def _layernorm(y, g, b):
            mu = y.mean(-1, keepdims=True)
            var = ((y - mu) ** 2).mean(-1, keepdims=True)
            return (y - mu) / jnp.sqrt(var + 1e-05) * g + b

        def _ssm(x, xw, dtw, dtb, Al, Dv, g, be):
            Bb, D, L = x.shape
            n = Al.shape[1]
            xd = jnp.einsum('bdl,kd->blk', x, xw)
            dts = xd[..., :R_DT]
            Bs = xd[..., R_DT:R_DT + n]
            Cs = xd[..., R_DT + n:]
            delta = jax.nn.softplus(jnp.einsum('blr,dr->bld', dts, dtw) + dtb)
            A = -jnp.exp(Al)
            xt = x.transpose(0, 2, 1)
            dA = jnp.exp(delta[..., None] * A)
            dBx = delta[..., None] * Bs[:, :, None, :] * xt[..., None]

            def step(h, inp):
                da, dbx, c = inp
                h = h * da + dbx
                return (h, jnp.einsum('bdn,bn->bd', h, c))
            h0 = jnp.zeros((Bb, D, n), x.dtype)
            _, ys = lax.scan(step, h0, (dA.transpose(1, 0, 2, 3), dBx.transpose(1, 0, 2, 3), Cs.transpose(1, 0, 2)))
            y = ys.transpose(1, 0, 2) + xt * Dv
            return _layernorm(y, g, be)

        def _up2(y, h, w):
            Bb, L, C = y.shape
            img = y.transpose(0, 2, 1).reshape(Bb, C, h, w)
            img = jnp.repeat(jnp.repeat(img, 2, axis=2), 2, axis=3)
            return img.reshape(Bb, C, 4 * L).transpose(0, 2, 1)

        def _conv1x1(x, w, b):
            return jnp.einsum('bchw,oc->bohw', x, w) + b[None, :, None, None]

        def _conv2s2(x, w, b):
            out = lax.conv_general_dilated(x, w, (2, 2), 'VALID', dimension_numbers=('NCHW', 'OIHW', 'NCHW'))
            return out + b[None, :, None, None]

        def _forward(input_f, in_w, in_b, c1_w, c1_b, c2_w, c2_b, c3_w, c3_b, out_w, out_b, xw1, dtw1, dtb1, Al1, Dv1, g1, be1, xw2, dtw2, dtb2, Al2, Dv2, g2, be2, xw3, dtw3, dtb3, Al3, Dv3, g3, be3):
            xz = _conv1x1(input_f, in_w, in_b)
            x, z = jnp.split(xz, 2, axis=1)
            f1 = _conv1x1(x, c1_w, c1_b)
            f2 = _conv2s2(f1, c2_w, c2_b)
            f3 = _conv2s2(f2, c3_w, c3_b)
            Bb, C, h3, w3 = f3.shape
            fx3 = f3.reshape(Bb, C, h3 * w3)
            y3 = _ssm(fx3, xw3, dtw3, dtb3, Al3, Dv3, g3, be3) + jnp.flip(_ssm(jnp.flip(fx3, -1), xw3, dtw3, dtb3, Al3, Dv3, g3, be3), 1)
            y2_ = _up2(y3, h3, w3)
            _, _, h2, w2 = f2.shape
            fx2 = f2.reshape(Bb, C, h2 * w2)
            y2 = _ssm(fx2, xw2, dtw2, dtb2, Al2, Dv2, g2, be2) + jnp.flip(_ssm(jnp.flip(fx2, -1), xw2, dtw2, dtb2, Al2, Dv2, g2, be2), 1) + y2_
            y1_ = _up2(y2, h2, w2)
            _, _, h1, w1 = f1.shape
            fx1 = f1.reshape(Bb, C, h1 * w1)
            y1 = _ssm(fx1, xw1, dtw1, dtb1, Al1, Dv1, g1, be1) + jnp.flip(_ssm(jnp.flip(fx1, -1), xw2, dtw2, dtb2, Al2, Dv2, g2, be2), 1) + y1_
            out1 = y1.transpose(0, 2, 1).reshape(Bb, C, h1, w1)
            out = out1 * jax.nn.silu(z)
            return _conv1x1(out, out_w, out_b)
        return _forward(input_f, in_w, in_b, c1_w, c1_b, c2_w, c2_b, c3_w, c3_b, out_w, out_b, xw1, dtw1, dtb1, Al1, Dv1, g1, be1, xw2, dtw2, dtb2, Al2, Dv2, g2, be2, xw3, dtw3, dtb3, Al3, Dv3, g3, be3)

    def _L3_conv_ref(x, gn_gamma, gn_beta, w_qkv, b_qkv, w_proj, b_proj):
        import jax, jax.numpy as jnp
        import numpy as np
        B, C, H, W = (8, 512, 32, 32)
        HEADS = 8
        DIM = C // HEADS
        EPS = 1e-05
        b, c, h, w = x.shape
        n = h * w
        mu = jnp.mean(x, axis=(1, 2, 3), keepdims=True)
        var = jnp.var(x, axis=(1, 2, 3), keepdims=True)
        xn = (x - mu) * jax.lax.rsqrt(var + EPS)
        xn = xn * gn_gamma[None, :, None, None] + gn_beta[None, :, None, None]
        qkv = jnp.einsum('bchw,oc->bohw', xn, w_qkv) + b_qkv[None, :, None, None]
        qkv = qkv.reshape(b, 3, HEADS, DIM, n)
        q, k, v = (qkv[:, 0], qkv[:, 1], qkv[:, 2])
        dot = jnp.einsum('bhdn,bhdm->bhnm', q, k) * c ** (-0.5)
        attn = jax.nn.softmax(dot, axis=-1)
        vals = jnp.einsum('bhnm,bhdm->bhdn', attn, v)
        vals = vals.reshape(b, HEADS * DIM, h, w)
        return jnp.einsum('bchw,oc->bohw', vals, w_proj) + b_proj[None, :, None, None]

    def _gn(v, G=32, eps=1e-5):
        B_, C_, H_, W_ = v.shape
        g = v.reshape(B_, G, C_ // G, H_, W_)
        m = jnp.mean(g, axis=(2, 3, 4), keepdims=True)
        s = jnp.var(g, axis=(2, 3, 4), keepdims=True)
        return ((g - m) / jnp.sqrt(s + eps)).reshape(v.shape)

    def _ln_c(v, eps=1e-6):
        m = jnp.mean(v, axis=1, keepdims=True)
        s = jnp.var(v, axis=1, keepdims=True)
        return (v - m) / jnp.sqrt(s + eps)

    def _ln_t(v, eps=1e-5):
        m = jnp.mean(v, axis=-1, keepdims=True)
        s = jnp.var(v, axis=-1, keepdims=True)
        return (v - m) / jnp.sqrt(s + eps)

    def _to_tokens(v):
        B_, C_, H_, W_ = v.shape
        return v.reshape(B_, C_, H_ * W_).transpose(0, 2, 1)
    def _from_tokens(t, like):
        B_, C_, H_, W_ = like.shape
        return t.transpose(0, 2, 1).reshape(B_, C_, H_, W_)

    x = x + _L0_conv_ref(_gn(x), L0_conv_in_w, L0_conv_in_b, L0_conv_c1_w, L0_conv_c1_b, L0_conv_c2_w, L0_conv_c2_b, L0_conv_c3_w, L0_conv_c3_b, L0_conv_out_w, L0_conv_out_b, L0_conv_xw1, L0_conv_dtw1, L0_conv_dtb1, L0_conv_Al1, L0_conv_Dv1, L0_conv_g1, L0_conv_be1, L0_conv_xw2, L0_conv_dtw2, L0_conv_dtb2, L0_conv_Al2, L0_conv_Dv2, L0_conv_g2, L0_conv_be2, L0_conv_xw3, L0_conv_dtw3, L0_conv_dtb3, L0_conv_Al3, L0_conv_Dv3, L0_conv_g3, L0_conv_be3)
    x = x + _L1_conv_ref(_gn(x), L1_conv_kernel)
    x = x + _L2_conv_ref(_gn(x), L2_conv_in_w, L2_conv_in_b, L2_conv_c1_w, L2_conv_c1_b, L2_conv_c2_w, L2_conv_c2_b, L2_conv_c3_w, L2_conv_c3_b, L2_conv_out_w, L2_conv_out_b, L2_conv_xw1, L2_conv_dtw1, L2_conv_dtb1, L2_conv_Al1, L2_conv_Dv1, L2_conv_g1, L2_conv_be1, L2_conv_xw2, L2_conv_dtw2, L2_conv_dtb2, L2_conv_Al2, L2_conv_Dv2, L2_conv_g2, L2_conv_be2, L2_conv_xw3, L2_conv_dtw3, L2_conv_dtb3, L2_conv_Al3, L2_conv_Dv3, L2_conv_g3, L2_conv_be3)
    x = x + _L3_conv_ref(_gn(x), L3_conv_gn_gamma, L3_conv_gn_beta, L3_conv_w_qkv, L3_conv_b_qkv, L3_conv_w_proj, L3_conv_b_proj)
    return x


_drawn_inputs = setup_inputs


def setup_inputs(seed=0):
    import zlib

    import numpy as np

    out = dict(_drawn_inputs(seed))
    spreads = {'L0_conv_Dv1': (1.0, 0.2),
     'L0_conv_g1': (1.0, 0.2),
     'L0_conv_be1': (0.0, 0.278),
     'L0_conv_Dv2': (1.0, 0.2),
     'L0_conv_g2': (1.0, 0.2),
     'L0_conv_be2': (0.0, 0.1),
     'L0_conv_Dv3': (1.0, 0.2),
     'L0_conv_g3': (1.0, 0.2),
     'L0_conv_be3': (0.0, 0.1),
     'L2_conv_Dv1': (1.0, 0.6),
     'L2_conv_g1': (1.0, 0.2),
     'L2_conv_be1': (0.0, 0.469),
     'L2_conv_Dv2': (1.0, 0.6),
     'L2_conv_g2': (1.0, 0.2),
     'L2_conv_be2': (0.0, 0.1),
     'L2_conv_Dv3': (1.0, 0.6),
     'L2_conv_g3': (1.0, 0.2),
     'L2_conv_be3': (0.0, 0.1),
     'L3_conv_gn_gamma': (1.0, 0.6),
     'L3_conv_gn_beta': (0.0, 0.1)}
    factors = {'L0_conv_dtb1': 64.0,
     'L0_conv_dtb2': 41.64,
     'L0_conv_dtb3': 26.92,
     'L2_conv_c3_b': 4.779,
     'L2_conv_out_b': 3.239,
     'L2_conv_dtb1': 64.0,
     'L2_conv_dtb2': 64.0,
     'L2_conv_dtb3': 56.224,
     'L3_conv_b_qkv': 8.0,
     'L3_conv_b_proj': 8.0,
     'L0_conv_c3_b': 4.817,
     'L0_conv_xw1': 8.0,
     'L0_conv_dtw1': 8.0,
     'L0_conv_xw2': 8.0,
     'L0_conv_dtw2': 8.0,
     'L0_conv_Al2': 8.0,
     'L0_conv_xw3': 4.694,
     'L0_conv_dtw3': 3.566,
     'L0_conv_Al3': 8.0,
     'L2_conv_c2_b': 3.082,
     'L2_conv_xw1': 8.0,
     'L2_conv_dtw1': 8.0,
     'L2_conv_xw2': 8.0,
     'L2_conv_dtw2': 8.0,
     'L2_conv_xw3': 8.0,
     'L2_conv_dtw3': 8.0,
     'L0_conv_Al1': 8.0,
     'L2_conv_Al3': 3.836}
    for name, (base, spread) in spreads.items():
        noise = np.random.default_rng([zlib.crc32(name.encode()), seed]).standard_normal(out[name].shape)
        drawn = base * np.exp(spread * noise) if base else spread * noise
        out[name] = jnp.asarray(drawn.astype(out[name].dtype))
    for name, factor in factors.items():
        out[name] = (out[name] * factor).astype(out[name].dtype)
    return out
```

```python
import concourse.bass as bass
import numpy as np
from concourse import mybir
from contextlib import ExitStack

F32 = mybir.dt.float32
ALU = mybir.AluOpType
ACT = mybir.ActivationFunctionType
AX = mybir.AxisListType

P = 128
C = 512
KC = C // P
L1, L2, L3 = 1024, 256, 64
D = 256
NH = D // P
N = 16
R = 8
BANK = 512
EPS = 1e-5
TAPS, ROWS, WIDTH = 16, 7, 32
HEADS, DH = 8, 64
NB = L1 // P
SCALE = float(C) ** -0.5

W_COLS = {}
_at = 0
for _name, _n in (("in", KC * 512), ("c1", NH * D), ("c2", NH * 4 * D), ("c3", NH * 4 * D),
                  ("out", NH * 512), ("xw1", NH * 40), ("xw2", NH * 40), ("xw3", NH * 40),
                  ("Al1", NH * N), ("Al2", NH * N), ("Al3", NH * N),
                  ("in_b", 4), ("c1_b", NH), ("c2_b", NH), ("c3_b", NH), ("out_b", 4),
                  ("dtb1", NH), ("dtb2", NH), ("dtb3", NH), ("Dv1", NH), ("Dv2", NH), ("Dv3", NH),
                  ("g1", NH), ("g2", NH), ("g3", NH), ("be1", NH), ("be2", NH), ("be3", NH)):
    W_COLS[_name] = (_at, _n)
    _at += _n
W_TOTAL = _at


def ssm_layer(nc, tag, x_in, x_out, w_dram, dtw_dram, ident_dram, group_dram, batches):
    ctx = ExitStack()
    with ctx:
        def sb(name, shape):
            return ctx.enter_context(nc.sbuf_tensor(f"{tag}_{name}", shape, F32))

        def sem(name):
            return ctx.enter_context(nc.semaphore(f"{tag}_{name}"))

        PITCH = NH * (L1 + 1)
        PITCH = max(PITCH, 4 * NH * (L2 + 1), N * NH * (L3 + 1))
        NA, NU = 3, 4
        W = sb("W", [P, W_TOTAL])
        dtw = sb("dtw", [R, 3, D])
        ident = sb("ident", [P, P])
        group = sb("group", [P, P])
        xin = sb("xin", [P, KC, L1])
        xn = sb("xn", [P, KC, L1])
        z = sb("z", [P, NH, L1])
        f1 = sb("f1", [P, NH, L1])
        f2 = sb("f2", [P, NH, L2])
        f3 = sb("f3", [P, NH, L3])
        dA_ring = sb("dA", [P, NA, PITCH])
        u_ring = sb("u", [P, NU, PITCH])
        b_sb = sb("b_sb", [P, 2, 1024])
        delta = {"3": sb("dl3", [P, NH, L3]), "2": sb("dl2", [P, NH, L2]),
                 "1f": sb("dl1f", [P, NH, L1]), "1b": sb("dl1b", [P, NH, L1])}
        dx = {"3": sb("dx3", [P, NH, L3]), "2": sb("dx2", [P, NH, L2]),
              "1f": sb("dx1f", [P, NH, L1]), "1b": sb("dx1b", [P, NH, L1])}
        bct = {"3": sb("bct3", [P, 1, 32]), "2": sb("bct2", [P, 2, 32]),
               "1f": sb("bct1f", [P, 8, 32]), "1b": sb("bct1b", [P, 8, 32])}
        hn = {"3": sb("hn3", [P, 2, D]), "2": sb("hn2", [P, 4, D]),
              "1f": xn[:, 0:2, :].rearrange("p a (k d) -> p (a k) d", d=D),
              "1b": xn[:, 2:4, :].rearrange("p a (k d) -> p (a k) d", d=D)}
        y3s = sb("y3s", [P, NH, L3])
        y2s = sb("y2s", [P, NH, L2])
        negA = sb("negA", [P, 3 * NH * N])
        bt = sb("bt", [P, 4 * NH])
        gst = sb("gst", [P, KC, 6 * 2])
        gmv = sb("gmv", [P, KC, 2])
        ggm = sb("ggm", [P, KC, 2])
        gd = sb("gd", [P, KC])
        gd2 = sb("gd2", [P, KC])
        gve = sb("gve", [P, KC])
        gr = sb("gr", [P, KC])
        lst = sb("lst", [P, 8, 6])
        lmv = sb("lmv", [P, 8, 2])
        lve = sb("lve", [P, 8])
        lr = sb("lr", [P, 8])
        mhalf = sb("mhalf", [P, 8])
        zero = sb("zero", [P, 32])
        f0 = dA_ring[:, 0, 0:NH * L1].rearrange("p (h l) -> p h l", h=NH)
        out1 = dA_ring[:, 1, 0:NH * L1].rearrange("p (h l) -> p h l", h=NH)
        dts = b_sb[0:R, 0, :]
        T0, T1, T2, T3 = (u_ring[:, i, 0:NH * L1] for i in range(4))
        xres = dx["1f"]
        bank = [ctx.enter_context(nc.psum_tensor(f"{tag}_bank{i}", [P, 8 * BANK], F32)) for i in range(1)][0]

        def bk(i, n=BANK):
            return bank[:, i * BANK:i * BANK + n]

        def w(name):
            a, n = W_COLS[name]
            return W[:, a:a + n]

        inT = w("in").rearrange("p (k o) -> p k o", k=KC)
        c1T = w("c1").rearrange("p (k o) -> p k o", k=NH)
        c2T = w("c2").rearrange("p (k t o) -> p k t o", k=NH, t=4)
        c3T = w("c3").rearrange("p (k t o) -> p k t o", k=NH, t=4)
        outT = w("out").rearrange("p (k o) -> p k o", k=NH)
        xwT = {s: w(f"xw{s}").rearrange("p (k o) -> p k o", k=NH) for s in "123"}

        T_GM, T_GD = 0, 1
        T_INX, T_INZ, T_C1, T_C2, T_C3 = 2, 6, 10, 14, 16
        SETS = [("3", f3, "3", L3), ("2", f2, "2", L2), ("1f", f1, "1", L1), ("1b", f1, "2", L1)]
        T_XD = [18, 21, 24, 31]
        T_N3, T_N2, T_NF, T_NB, T_OUT = 38, 39, 40, 44, 48
        TILES = 56
        BY_DVE = {0, 1, 18, 19, 21, 22, 24, 25, 26, 31, 32, 33} | set(range(40, 44)) | set(range(48, 56))
        PER_D = len(BY_DVE)
        PER_A = TILES - PER_D

        def left(t):
            same = t in BY_DVE
            return sum((i in BY_DVE) == same for i in range(t + 1))

        PASSES = [("3", L3, "fb", "3"), ("2", L2, "fb", "2"), ("1f", L1, "f", "1"), ("1b", L1, "b", "2")]
        CH, FIRST, VITEM, END = [], [], [], []
        item = 0
        for pi, (key, L, dirs, s) in enumerate(PASSES):
            ns = 1024 // L
            FIRST.append(len(CH))
            VITEM.append(item)
            item += 1
            for n0 in range(0, N, ns):
                CH.append(dict(key=key, L=L, dirs=dirs, n0=n0, ns=ns, pi=pi, item=item, wset=s))
                item += len(dirs)
            END.append(item)
        ITEMS, NCH = item, len(CH)
        SCANS = sum(len(c["dirs"]) for c in CH)
        for i, c in enumerate(CH):
            c["scan0"] = sum(len(q["dirs"]) for q in CH[:i])
            c["pad_a"] = i - FIRST[c["pi"]] < NA and (c["pi"] != 3)
            c["in_item"] = c["item"] + len(c["dirs"]) - 1
            c["pad_u"] = c["pi"] != 3 and (c["in_item"] - VITEM[c["pi"]]) <= NU
        for i, c in enumerate(CH):
            c["a_done"] = sum(q["pad_a"] + q["ns"] * NH for q in CH[:i + 1])
            c["u_done"] = sum(q["pad_u"] + 1 for q in CH[:i + 1])
        PER_DA, PER_DBX = CH[-1]["a_done"], CH[-1]["u_done"]

        def seg(buf, c):
            n = c["ns"] * NH * (c["L"] + 1)
            return buf[:, 0:n].rearrange("p (n h l) -> p n h l", h=NH, l=c["L"] + 1)

        def xd_tile(si):
            return T_XD[si], [T_XD[si] + 1 + i for i in range(max(1, SETS[si][3] // BANK))]

        def pre_tiles(si):
            n = max(1, SETS[si][3] * NH // BANK)
            return [xd_tile(si)[1][-1] + 1 + i for i in range(n)]

        LN_BLOCKS = [2, 4, 8, 8]

        const_in = sem("const_in")
        const_set = sem("const_set")
        expA = sem("expA")
        held = {e: sem(f"held_{e}") for e in ("pe", "dve", "pool", "sp")}
        bias_step = sem("bias_step")
        x_arrived = sem("x_arrived")
        res_in = [sem(f"res_in{i}") for i in range(2)]
        stored = sem("stored")
        gn_step = sem("gn_step")
        gn_rstd = sem("gn_rstd")
        xn_done = sem("xn_done")
        tile_full = sem("tile_full")
        tile_act = sem("tile_act")
        tile_dve = sem("tile_dve")
        sp_exp = sem("sp_exp")
        sp_ln = sem("sp_ln")
        sp_w = sem("sp_w")
        sp_c = sem("sp_c")
        sp_s = sem("sp_s")
        delta_done = sem("delta_done")
        dx_done = sem("dx_done")
        bb_full = sem("bb_full")
        bsb_full = sem("bsb_full")
        cb_full = sem("cb_full")
        da_full = sem("da_full")
        dbx_full = sem("dbx_full")
        xdv_full = sem("xdv_full")
        scan_done = sem("scan_done")
        hc_full = sem("hc_full")
        tr_done = sem("tr_done")
        ln_st = sem("ln_st")
        ln_mv = sem("ln_mv")
        ln_ve = sem("ln_ve")
        ln_r = sem("ln_r")
        ln_done = sem("ln_done")
        up2_done = sem("up2_done")
        up1_done = sem("up1_done")
        gate_done = sem("gate_done")

        def hold(engine, name):
            engine.sem_inc(held[name], 1)

        block = ctx.enter_context(nc.Block())

        @block.sync
        def _(sp):
            sp.sem_inc(stored, 1)
            for dst, src in ((W[:], w_dram), (dtw[:], dtw_dram), (ident[:], ident_dram), (group[:], group_dram)):
                sp.dma_start(dst, src).then_inc(const_in, 16)

            def load_x(b):
                src = x_in[bass.ds(b, 1)].rearrange("a (k p) l -> p (a k) l", p=P)
                sp.dma_start(xin[:], src).then_inc(x_arrived, 16)

            def residual(b):
                for m in range(4):
                    if m < 2:
                        sp.wait_ge(dbx_full, b * PER_DBX + PER_DBX)
                    else:
                        sp.wait_ge(stored, b * 64 + 16 * (m - 1) + 1)
                    sp.dma_start(xres[:, m % 2, :],
                                 x_in[bass.ds(b, 1), m * P:(m + 1) * P, :].rearrange("a p l -> (a p) l")).then_inc(res_in[m % 2], 16)
                    if m >= 1:
                        store(b, m - 1)
                store(b, 3)

            def store(b, m):
                sp.wait_ge(tile_dve, b * PER_D + left(T_OUT + 2 * m + 1) + 1)
                sp.dma_start(x_out[bass.ds(b, 1), m * P:(m + 1) * P, :].rearrange("a p l -> (a p) l"),
                             xres[:, m % 2, :]).then_inc(stored, 16)

            load_x(0)

            def body(b, last):
                if not last:
                    sp.wait_ge(xn_done, b * 4 + 4)
                    load_x(b + 1)
                residual(b)

            if batches > 1:
                with sp.Fori(0, batches - 1) as b:
                    body(b, False)
            body(batches - 1, True)
            sp.wait_ge(stored, batches * 64 + 1)

        @block.tensor
        def _(pe):
            mm = nc.tensor.matmul
            pe.wait_ge(const_in, 64)

            def tile_wait(b, t):
                if t < 8:
                    pe.wait_ge(tile_dve, b * PER_D + 1)
                elif t - 8 in BY_DVE:
                    pe.wait_ge(tile_dve, b * PER_D + left(t - 8) + 1)
                else:
                    pe.wait_ge(tile_act, b * PER_A + left(t - 8))

            def projections(b, si):
                key, f, s, L = SETS[si]
                txd, tdts = xd_tile(si)
                tile_wait(b, txd)
                nlb = max(1, L // P)
                rows = min(L, P)
                for lb in range(nlb):
                    for k in range(NH):
                        last = mm(bk(txd % 8)[0:rows, lb * 32:lb * 32 + 32], f[:, k, lb * rows:(lb + 1) * rows],
                                  xwT[s][:, k, R:40], start=(k == 0), stop=(k == NH - 1))
                last.then_inc(tile_full, 1)
                for i, t in enumerate(tdts):
                    tile_wait(b, t)
                    n = min(L, BANK)
                    for k in range(NH):
                        last = mm(bk(t % 8)[0:R, 0:n], xwT[s][:, k, 0:R], f[:, k, i * n:(i + 1) * n],
                                  start=(k == 0), stop=(k == NH - 1))
                    last.then_inc(tile_full, 1)
                pe.wait_ge(tile_dve, b * PER_D + left(tdts[-1]) + 1)
                for i, t in enumerate(pre_tiles(si)):
                    tile_wait(b, t)
                    if L == L1:
                        h, q = i // 2, i % 2
                        last = mm(bk(t % 8), dtw[:, int(s) - 1, h * P:(h + 1) * P], dts[:, q * BANK:(q + 1) * BANK],
                                  start=True, stop=True)
                    else:
                        for h in range(NH):
                            last = mm(bk(t % 8)[:, h * L:(h + 1) * L], dtw[:, int(s) - 1, h * P:(h + 1) * P],
                                      dts[:, 0:L], start=True, stop=True)
                    last.then_inc(tile_full, 1)

            def conv_s2(b, t0, wT, src, width):
                half = width // 2
                for m in range(NH):
                    tile_wait(b, t0 + m)
                    i = 0
                    for k in range(NH):
                        v = src[:, k, :].rearrange("p (h y w x) -> p y x h w", y=2, x=2, w=half)
                        for t in range(4):
                            last = mm(bk((t0 + m) % 8)[:, 0:half * half].rearrange("p (h w) -> p h w", w=half),
                                      wT[:, k, t, m * P:(m + 1) * P], v[:, t // 2, t % 2],
                                      start=(i == 0), stop=(i == 7))
                            i += 1
                    last.then_inc(tile_full, 1)

            def broadcast(c, what, col):
                key, L = c["key"], c["L"]
                rows, nlb = min(L, P), max(1, L // P)
                for i in range(c["ns"]):
                    for lb in range(nlb):
                        o = i * L + lb * rows
                        src = bct[key][0:rows, lb, col + c["n0"] + i:col + c["n0"] + i + 1].broadcast_to([rows, P])
                        last = mm(bank[:, what * BANK + o:what * BANK + o + rows], src, ident[0:rows, 0:rows],
                                  start=(o % BANK == 0), stop=(o % BANK == BANK - rows), is_transpose=True)
                return last

            def y_bank(pi, d, lb):
                key, L, dirs, _ = PASSES[pi]
                if L == L1:
                    return lb // 2, (lb % 2) * D
                return (2 if L == L3 else 0) + (d == "b"), lb * D

            def add_item(src, pi, dirs, first, final, n0ns=(1,)):
                key, L, _, _ = PASSES[pi]
                rows, nlb = min(L, P), max(1, L // P)
                for d in dirs:
                    for i in range(src.shape[1]):
                        for h in range(NH):
                            for lb in range(nlb):
                                bi, col = y_bank(pi, d, lb)
                                st = first and i == 0 and h == 0 and col == 0
                                en = final and i == src.shape[1] - 1 and h == NH - 1 and (
                                    lb == nlb - 1 or (L == L1 and lb % 2 == 1))
                                last = mm(bank[0:rows, bi * BANK + col + h * P:bi * BANK + col + h * P + P],
                                          src[:, i, h, 1 + lb * rows:1 + (lb + 1) * rows], ident[:, :],
                                          start=st, stop=en, is_transpose=True)
                return last

            def scans(b):
                pending = []

                def flush():
                    for fn in pending:
                        fn()
                    pending.clear()

                for ci, c in enumerate(CH):
                    pe.wait_ge(bsb_full, b * NCH + ci + 1)
                    if c["L"] == L3:
                        hold(pe, "pe")
                    broadcast(c, 4, 0).then_inc(bb_full, 1)
                    pe.wait_ge(hc_full, b * SCANS + c["scan0"] + 1)
                    if c["L"] == L3:
                        hold(pe, "pe")
                    broadcast(c, 6, N).then_inc(cb_full, 1)
                    flush()
                    if ci == FIRST[c["pi"]]:
                        pi = c["pi"]
                        pe.wait_ge(xdv_full, b * 8 + 2 * (pi + 1))
                        if pi >= 2:
                            pe.wait_ge(ln_done, b * 4 + pi)
                        if pi == 0:
                            hold(pe, "pe")
                        slot = u_ring[:, VITEM[pi] % NU, :]
                        v = dict(ns=1, L=c["L"])
                        add_item(seg(slot, v), pi, c["dirs"], True, False).then_inc(tr_done, 1)

                    def later(c=c):
                        for j, d in enumerate(c["dirs"]):
                            pe.wait_ge(hc_full, b * SCANS + c["scan0"] + j + 1 + 1)
                            it = c["item"] + j
                            if c["L"] == L3:
                                hold(pe, "pe")
                            add_item(seg(u_ring[:, it % NU, :], c), c["pi"], d, False,
                                     c["n0"] + c["ns"] == N).then_inc(tr_done, 1)
                    pending.append(later)
                flush()

            with pe.Fori(0, batches) as b:
                tile_wait(b, T_GM)
                pe.wait_ge(gn_step, b * 15 + 12)
                mm(bk(0)[:, 0:2 * KC], group[:], gmv[:].rearrange("p k s -> p (k s)"), start=True, stop=True).then_inc(tile_full, 1)
                pe.wait_ge(gn_step, b * 15 + 14)
                mm(bk(1)[:, 0:KC], group[:], gd2[:], start=True, stop=True).then_inc(tile_full, 1)
                pe.wait_ge(xn_done, b * 4 + 4)
                for m in range(4):
                    for q in range(2):
                        t = T_INX + 2 * m + q
                        tile_wait(b, t)
                        for k in range(KC):
                            last = mm(bk(t % 8), inT[:, k, m * P:(m + 1) * P], xn[:, k, q * BANK:(q + 1) * BANK],
                                      start=(k == 0), stop=(k == KC - 1))
                        last.then_inc(tile_full, 1)
                pe.wait_ge(tile_act, b * PER_A + left(T_INX + 3))
                for m in range(NH):
                    for q in range(2):
                        t = T_C1 + 2 * m + q
                        tile_wait(b, t)
                        for k in range(NH):
                            last = mm(bk(t % 8), c1T[:, k, m * P:(m + 1) * P], f0[:, k, q * BANK:(q + 1) * BANK],
                                      start=(k == 0), stop=(k == NH - 1))
                        last.then_inc(tile_full, 1)
                pe.wait_ge(tile_act, b * PER_A + left(T_C1 + 3))
                conv_s2(b, T_C2, c2T, f1, 32)
                pe.wait_ge(tile_act, b * PER_A + left(T_C2 + 1))
                conv_s2(b, T_C3, c3T, f2, 16)
                pe.wait_ge(tile_act, b * PER_A + left(T_C3 + 1))
                for si in range(4):
                    projections(b, si)
                pe.wait_ge(tile_act, b * PER_A + left(37))
                pe.wait_ge(tile_dve, b * PER_D + left(33) + 1)
                scans(b)
                pe.wait_ge(ln_done, b * 4 + 4)
                for t, key, L in ((T_N3, "3", L3), (T_N2, "2", L2)):
                    rows, nlb = min(L, P), max(1, L // P)
                    pe.wait_ge(hc_full, b * SCANS + SCANS + 1)
                    if L == L3:
                        hold(pe, "pe")
                    for h in range(NH):
                        for lb in range(nlb):
                            for d in range(2):
                                last = mm(bk(t % 8)[:, h * L + lb * rows:h * L + (lb + 1) * rows],
                                          hn[key][0:rows, d * nlb + lb, h * P:(h + 1) * P], ident[0:rows, 0:rows],
                                          start=(h == 0 and lb == 0 and d == 0),
                                          stop=(h == NH - 1 and lb == nlb - 1 and d == 1), is_transpose=True)
                    last.then_inc(tile_full, 1)
                for t0, key in ((T_NF, "1f"), (T_NB, "1b")):
                    for h in range(NH):
                        for q in range(2):
                            t = t0 + 2 * h + q
                            if t in (T_NB, T_NB + 1):
                                pe.wait_ge(bsb_full, b * NCH + NCH + 1)
                            if t >= T_NB + 2:
                                tile_wait(b, t)
                            for j in range(4):
                                last = mm(bk(t % 8)[:, j * P:(j + 1) * P], hn[key][:, 4 * q + j, h * P:(h + 1) * P],
                                          ident[:], start=(j == 0), stop=(j == 3), is_transpose=True)
                            last.then_inc(tile_full, 1)
                pe.wait_ge(gate_done, b * 4 + 4)
                for m in range(4):
                    for q in range(2):
                        t = T_OUT + 2 * m + q
                        tile_wait(b, t)
                        for k in range(NH):
                            last = mm(bk(t % 8), outT[:, k, m * P:(m + 1) * P], out1[:, k, q * BANK:(q + 1) * BANK],
                                      start=(k == 0), stop=(k == NH - 1))
                        last.then_inc(tile_full, 1)

        @block.scalar
        def _(act):
            act.sem_inc(bsb_full, 1)
            A = nc.scalar.activation
            act.wait_ge(const_in, 64)
            a0 = W_COLS["Al1"][0]
            A(negA[:], W[:, a0:a0 + 3 * NH * N], ACT.Exp).then_inc(expA, 1)
            act.wait_ge(const_set, 3)

            def full(b, t):
                act.wait_ge(tile_full, b * TILES + t + 1)

            def softplus(b, si):
                key, f, s, L = SETS[si]
                if si > 0:
                    act.wait_ge(delta_done, b * 4 + si)
                for i, t in enumerate(pre_tiles(si)):
                    full(b, t)
                    for j in range(1 if L == L1 else NH):
                        h, n = (i // 2, BANK) if L == L1 else (j, L)
                        o = i * BANK if L == L1 else j * L
                        src = bk(t % 8)[:, 0 if L == L1 else j * L:][:, 0:n]
                        bias = w(f"dtb{s}")[:, h:h + 1]
                        A(T0[:, o:o + n], src, ACT.Abs, bias=bias)
                        last = A(T2[:, o:o + n], src, ACT.Relu, bias=bias)
                    last.then_inc(tile_act, 1)
                n = NH * L
                act.wait_ge(tile_act, b * PER_A + left(pre_tiles(si)[-1]))
                A(T0[:, 0:n], T0[:, 0:n], ACT.Exp, scale=-1.0).then_inc(sp_exp, 1)
                act.wait_ge(sp_exp, b * 4 + si + 1)
                A(T1[:, 0:n], T0[:, 0:n], ACT.Ln, bias=1.0).then_inc(sp_ln, 1)

            with act.Fori(0, batches) as b:
                for m in range(4):
                    for q in range(2):
                        t = T_INX + 2 * m + q
                        full(b, t)
                        dst, fn = (f0, ACT.Identity) if m < 2 else (z, ACT.Silu)
                        A(dst[:, m % 2, q * BANK:(q + 1) * BANK], bk(t % 8), fn,
                          bias=w("in_b")[:, m:m + 1]).then_inc(tile_act, 1)
                for t0, dst, n, bias in ((T_C1, f1, BANK, "c1_b"), (T_C2, f2, L2, "c2_b"), (T_C3, f3, L3, "c3_b")):
                    per = dst.shape[2] // n
                    for m in range(NH):
                        for q in range(per):
                            t = t0 + per * m + q
                            full(b, t)
                            A(dst[:, m, q * n:(q + 1) * n], bk(t % 8)[:, 0:n], ACT.Identity,
                              bias=w(bias)[:, m:m + 1]).then_inc(tile_act, 1)
                for si in range(4):
                    softplus(b, si)
                for ci, c in enumerate(CH):
                    key, f, s, L = SETS[c["pi"]]
                    if ci == FIRST[c["pi"]]:
                        it = VITEM[c["pi"]]
                        if it < NU:
                            act.wait_ge(delta_done, b * 4 + 4)
                        else:
                            act.wait_ge(tr_done, b * ITEMS + it - NU + 1)
                        for h in range(NH):
                            A(seg(u_ring[:, it % NU, :], dict(ns=1, L=L))[:, 0, h, 1:], f[:, h, :], ACT.Copy,
                              scale=w(f"Dv{s}")[:, h:h + 1]).then_inc(xdv_full, 1)
                    act.wait_ge(bb_full, b * NCH + ci + 1)
                    if ci >= 2:
                        act.wait_ge(dbx_full, b * PER_DBX + CH[ci - 2]["u_done"])
                    A(b_sb[:, ci % 2, :], bank[:, 4 * BANK:6 * BANK], ACT.Copy).then_inc(bsb_full, 1)
                    if ci >= NA:
                        act.wait_ge(scan_done, b * SCANS + CH[ci - NA]["scan0"] + len(CH[ci - NA]["dirs"]))
                    slot = seg(dA_ring[:, ci % NA, :], c)
                    if c["pad_a"]:
                        A(slot[:, :, :, 0], zero[:, 0:c["ns"] * NH].rearrange("p (n h) -> p n h", h=NH), ACT.Copy).then_inc(da_full, 1)
                    for i in range(c["ns"]):
                        for h in range(NH):
                            col = (int(s) - 1) * NH * N + h * N + c["n0"] + i
                            A(slot[:, i, h, 1:], delta[key][:, h, :], ACT.Exp,
                              scale=negA[:, col:col + 1]).then_inc(da_full, 1)
                for t, dst, g, L in ((T_N3, y3s, "g3", L3), (T_N2, y2s, "g2", L2)):
                    full(b, t)
                    for h in range(NH):
                        if t == T_N3:
                            last = A(dst[:, h, :], bk(t % 8)[:, h * L:(h + 1) * L], ACT.Identity,
                                     scale=w(g)[:, h:h + 1], bias=bt[:, h:h + 1])
                        else:
                            last = A(dst[:, h, :], bk(t % 8)[:, h * L:(h + 1) * L], ACT.Copy, scale=w(g)[:, h:h + 1])
                    last.then_inc(tile_act, 1)
                for h in range(NH):
                    for q in range(2):
                        t = T_NB + 2 * h + q
                        full(b, t)
                        A(out1[:, h, q * BANK:(q + 1) * BANK], bk(t % 8), ACT.Copy,
                          scale=w("g2")[:, h:h + 1]).then_inc(tile_act, 1)

        @block.gpsimd
        def _(pool):
            G = nc.gpsimd
            G.memset(mhalf[:], -0.5).then_inc(const_set, 1)
            pool.wait_ge(const_set, 3)

            def norm_rstd(b, pi):
                pool.wait_ge(ln_ve, b * 4 + pi + 1)
                rows, nb = min(PASSES[pi][1], P), LN_BLOCKS[pi]
                G.tensor_tensor(lr[0:rows, 0:nb], lve[0:rows, 0:nb], mhalf[0:rows, 0:nb], ALU.pow).then_inc(ln_r, 1)

            with pool.Fori(0, batches) as b:
                pool.wait_ge(gn_step, b * 15 + 15)
                G.tensor_tensor(gr[:], gve[:], mhalf[:, 0:KC], ALU.pow).then_inc(gn_rstd, 1)
                for si, (key, f, s, L) in enumerate(SETS):
                    n = NH * L
                    pool.wait_ge(sp_w, b * 4 + si + 1)
                    G.tensor_tensor(T3[:, 0:n], T0[:, 0:n], T3[:, 0:n], ALU.subtract).then_inc(sp_c, 1)
                    pool.wait_ge(delta_done, b * 4 + si + 1)
                    if key == "1f":
                        pool.wait_ge(stored, b * 64 + 1)
                    G.tensor_tensor(dx[key][:], delta[key][:], f[:], ALU.mult).then_inc(dx_done, 1)
                for ci, c in enumerate(CH):
                    key, L, ns = c["key"], c["L"], c["ns"]
                    if ci == 0:
                        pool.wait_ge(dx_done, b * 4 + 4)
                        pool.wait_ge(delta_done, b * 4 + 4)
                    else:
                        if c["in_item"] >= NU:
                            pool.wait_ge(tr_done, b * ITEMS + c["in_item"] - NU + 1)
                    slot = seg(u_ring[:, c["in_item"] % NU, :], c)
                    if c["pad_u"]:
                        hold(pool, "pool")
                        G.memset(slot[:, :, :, 0], 0.0).then_inc(dbx_full, 1)
                    pool.wait_ge(bsb_full, b * NCH + ci + 1 + 1)
                    shape = [P, ns, NH, L]
                    a = dx[key][:].unsqueeze(1).broadcast_to(shape)
                    bb = b_sb[:, ci % 2, 0:ns * L].rearrange("p (n l) -> p n l", l=L).unsqueeze(2).broadcast_to(shape)
                    G.tensor_tensor(slot[:, :, :, 1:], a, bb, ALU.mult).then_inc(dbx_full, 1)
                    if ci in FIRST[1:]:
                        norm_rstd(b, c["pi"] - 1)
                norm_rstd(b, 3)

                def enlarge(dst, src, width, y0, y1):
                    for dy in range(2):
                        v = dst.rearrange("p (h y w x) -> p h y w x", y=2, x=2, w=width)[:, y0:y1, dy]
                        s_ = src.rearrange("p (h w) -> p h w", w=width)[:, y0:y1]
                        last = G.tensor_tensor(v, v, s_.unsqueeze(3).broadcast_to([P, y1 - y0, width, 2]), ALU.add)
                    return last

                pool.wait_ge(tile_act, b * PER_A + left(T_N2))
                for h in range(NH):
                    last = enlarge(y2s[:, h, :], y3s[:, h, :], 8, 0, 8)
                last.then_inc(up2_done, 1)
                pool.wait_ge(up2_done, b + 1)
                for h in range(NH):
                    for q in range(2):
                        pool.wait_ge(tile_act, b * PER_A + left(T_NB + 2 * h + q))
                        enlarge(out1[:, h, :], y2s[:, h, :], 16, 8 * q, 8 * q + 8).then_inc(up1_done, 1)
                for h in range(NH):
                    for q in range(2):
                        pool.wait_ge(tile_dve, b * PER_D + left(T_NF + 2 * h + q) + 1)
                        o = out1[:, h, q * BANK:(q + 1) * BANK]
                        G.tensor_tensor(o, o, z[:, h, q * BANK:(q + 1) * BANK], ALU.mult).then_inc(gate_done, 1)

        @block.vector
        def _(dve):
            dve.sem_inc(tile_dve, 1)
            dve.sem_inc(hc_full, 1)
            V = nc.vector
            V.memset(zero[:], 0.0).then_inc(const_set, 1)
            dve.wait_ge(const_in, 64)
            dve.wait_ge(expA, 1)
            V.tensor_scalar(negA[:], negA[:], -1.0, None, ALU.mult)
            t = [bt[:, NH * i:NH * i + NH] for i in range(4)]
            V.tensor_scalar(t[1], w("be2"), 3.0, None, ALU.mult).then_inc(bias_step, 1)
            V.tensor_scalar(t[2], w("be3"), 2.0, None, ALU.mult).then_inc(bias_step, 1)
            dve.wait_ge(bias_step, 2)
            V.tensor_tensor(t[3], t[1], t[2], ALU.add).then_inc(bias_step, 1)
            dve.wait_ge(bias_step, 3)
            V.tensor_tensor(t[0], t[3], w("be1"), ALU.add).then_inc(const_set, 1)
            dve.wait_ge(const_set, 3)

            def full(b, t):
                dve.wait_ge(tile_full, b * TILES + t + 1)

            def softplus(b, si):
                key, f, s, L = SETS[si]
                txd, tdts = xd_tile(si)
                rows, nlb = min(L, P), max(1, L // P)
                full(b, txd)
                V.tensor_copy(bct[key][0:rows].rearrange("p a n -> p (a n)"),
                              bk(txd % 8)[0:rows, 0:nlb * 32]).then_inc(tile_dve, 1)
                for i, t_ in enumerate(tdts):
                    n = min(L, BANK)
                    full(b, t_)
                    V.tensor_copy(dts[:, i * n:(i + 1) * n], bk(t_ % 8)[0:R, 0:n]).then_inc(tile_dve, 1)
                n = NH * L
                dve.wait_ge(sp_exp, b * 4 + si + 1)
                V.tensor_scalar(T3[:, 0:n], T0[:, 0:n], 1.0, 1.0, ALU.add, ALU.subtract).then_inc(sp_w, 1)
                dve.wait_ge(sp_ln, b * 4 + si + 1)
                dve.wait_ge(sp_c, b * 4 + si + 1)
                V.tensor_tensor(T3[:, 0:n], T3[:, 0:n], T1[:, 0:n], ALU.add).then_inc(sp_s, 1)
                dve.wait_ge(sp_s, b * 8 + 2 * si + 1)
                V.tensor_tensor(T3[:, 0:n], T3[:, 0:n], T0[:, 0:n], ALU.min).then_inc(sp_s, 1)
                dve.wait_ge(sp_s, b * 8 + 2 * si + 2)
                V.tensor_tensor(delta[key][:].rearrange("p h l -> p (h l)"), T3[:, 0:n], T2[:, 0:n], ALU.add).then_inc(delta_done, 1)

            def layer_norm(b, pi):
                key, L, dirs, _ = PASSES[pi]
                rows = min(L, P)
                nb, before = LN_BLOCKS[pi], sum(LN_BLOCKS[:pi])
                blocks = []
                for j in range(nb):
                    if L == L1:
                        blocks.append(bank[:, j * D:(j + 1) * D])
                    elif L == L2:
                        blocks.append(bank[:, (j // 2) * BANK + (j % 2) * D:][:, 0:D])
                    else:
                        blocks.append(bank[0:rows, (2 + j) * BANK:(2 + j) * BANK + D])
                dve.wait_ge(tr_done, b * ITEMS + END[pi])
                for j in range(nb):
                    V.bn_stats(lst[0:rows, j, :], blocks[j]).then_inc(ln_st, 1)
                for j in range(nb):
                    dve.wait_ge(ln_st, b * 22 + before + j + 1)
                    hold(dve, "dve")
                    V.bn_aggr(lmv[0:rows, j, :], lst[0:rows, j, :]).then_inc(ln_mv, 1)
                dve.wait_ge(ln_mv, b * 22 + before + nb)
                V.tensor_scalar(lve[0:rows, 0:nb], lmv[0:rows, 0:nb, 1], EPS, None, ALU.add).then_inc(ln_ve, 1)
                dve.wait_ge(ln_r, b * 4 + pi + 1)
                for j in range(nb):
                    last = V.tensor_scalar(hn[key][0:rows, j, :], blocks[j], lmv[0:rows, j, 0:1], lr[0:rows, j:j + 1],
                                           ALU.subtract, ALU.mult)
                last.then_inc(ln_done, 1)

            with dve.Fori(0, batches) as b:
                dve.wait_ge(x_arrived, b * 16 + 16)
                g0 = b * 15
                for k in range(KC):
                    for q in range(2):
                        V.bn_stats(gst[:, k, 6 * q:6 * q + 6], xin[:, k, q * BANK:(q + 1) * BANK]).then_inc(gn_step, 1)
                for k in range(KC):
                    dve.wait_ge(gn_step, g0 + 2 * k + 2)
                    hold(dve, "dve")
                    V.bn_aggr(gmv[:, k, :], gst[:, k, :]).then_inc(gn_step, 1)
                full(b, T_GM)
                V.tensor_copy(ggm[:].rearrange("p k s -> p (k s)"), bk(0)[:, 0:2 * KC]).then_inc(tile_dve, 1)
                dve.wait_ge(tile_dve, b * PER_D + 1 + 1)
                V.tensor_tensor(gd[:], gmv[:, :, 0], ggm[:, :, 0], ALU.subtract).then_inc(gn_step, 1)
                dve.wait_ge(gn_step, g0 + 13)
                V.tensor_tensor(gd2[:], gd[:], gd[:], ALU.mult).then_inc(gn_step, 1)
                full(b, T_GD)
                V.tensor_tensor(gve[:], bk(1)[:, 0:KC], ggm[:, :, 1], ALU.add).then_inc(tile_dve, 1)
                dve.wait_ge(tile_dve, b * PER_D + 2 + 1)
                V.tensor_scalar(gve[:], gve[:], EPS, None, ALU.add).then_inc(gn_step, 1)
                dve.wait_ge(gn_rstd, b + 1)
                for k in range(KC):
                    last = V.tensor_scalar(xn[:, k, :], xin[:, k, :], ggm[:, k, 0:1], gr[:, k:k + 1],
                                           ALU.subtract, ALU.mult).then_inc(xn_done, 1)
                for si in range(4):
                    softplus(b, si)
                for ci, c in enumerate(CH):
                    a = seg(dA_ring[:, ci % NA, :], c)
                    n = c["ns"] * NH * (c["L"] + 1)
                    a2 = dA_ring[:, ci % NA, 0:n]
                    src = u_ring[:, c["in_item"] % NU, 0:n]
                    dve.wait_ge(da_full, b * PER_DA + c["a_done"])
                    dve.wait_ge(dbx_full, b * PER_DBX + c["u_done"])
                    two = len(c["dirs"]) == 2
                    outs = []
                    for j, d in enumerate(c["dirs"]):
                        it = c["item"] + j
                        dst = u_ring[:, it % NU, 0:n]
                        if two and j == 0:
                            if it >= NU:
                                dve.wait_ge(tr_done, b * ITEMS + it - NU + 1)
                        if two and j == 1:
                            dve.wait_ge(scan_done, b * SCANS + c["scan0"] + 1)
                        if d == "f":
                            V.tensor_tensor_scan(dst, a2, src, 0.0, ALU.mult, ALU.add).then_inc(scan_done, 1)
                        else:
                            V.tensor_tensor_scan(dst[:, ::-1], a2[:, ::-1], src[:, ::-1], 0.0, ALU.mult, ALU.add).then_inc(scan_done, 1)
                        outs.append(it)
                    dve.wait_ge(cb_full, b * NCH + ci + 1)
                    for j, it in enumerate(outs):
                        dve.wait_ge(scan_done, b * SCANS + c["scan0"] + j + 1)
                        v = seg(u_ring[:, it % NU, :], c)[:, :, :, 1:]
                        cc = bank[:, 6 * BANK:8 * BANK].rearrange("p (n l) -> p n l", l=c["L"]).unsqueeze(2).broadcast_to([P, c["ns"], NH, c["L"]])
                        V.tensor_tensor(v, v, cc, ALU.mult).then_inc(hc_full, 1)
                    if c["n0"] + c["ns"] == N:
                        layer_norm(b, c["pi"])
                for h in range(NH):
                    for q in range(2):
                        full(b, T_NF + 2 * h + q)
                        dve.wait_ge(up1_done, b * 4 + 2 * h + q + 1)
                        o = out1[:, h, q * BANK:(q + 1) * BANK]
                        V.scalar_tensor_tensor(o, bk((T_NF + 2 * h + q) % 8), w("g1")[:, h:h + 1], o, ALU.mult, ALU.add).then_inc(tile_dve, 1)
                for m in range(4):
                    for q in range(2):
                        full(b, T_OUT + 2 * m + q)
                        dve.wait_ge(res_in[m % 2], b * 32 + 16 * (m // 2) + 16)
                        o = xres[:, m % 2, q * BANK:(q + 1) * BANK]
                        V.scalar_tensor_tensor(o, bk((T_OUT + 2 * m + q) % 8), w("out_b")[:, m:m + 1], o, ALU.add, ALU.add).then_inc(tile_dve, 1)


def conv_layer(nc, tag, x_in, x_out, taps_dram, masks_dram, ident_dram, group_dram, batches):
    ctx = ExitStack()
    with ctx:
        def sb(name, shape):
            return ctx.enter_context(nc.sbuf_tensor(f"{tag}_{name}", shape, F32))

        def sem(name):
            return ctx.enter_context(nc.semaphore(f"{tag}_{name}"))

        ident = sb("ident", [P, P])
        group = sb("group", [P, P])
        taps = sb("taps", [P, TAPS])
        masks = sb("masks", [P, TAPS, ROWS * WIDTH])
        band = sb("band", [P, ROWS * WIDTH])
        xin = sb("xin", [P, 2, KC, L1])
        xn = sb("xn", [P, KC, L1])
        xt = sb("xt", [P, 8, C])
        y = sb("y", [P, 2, L1])
        gst = sb("gst", [P, KC, 12])
        gmv = sb("gmv", [P, KC, 2])
        ggm = sb("ggm", [P, KC, 2])
        gd = sb("gd", [P, KC])
        gd2 = sb("gd2", [P, KC])
        gve = sb("gve", [P, KC])
        gr = sb("gr", [P, KC])
        mhalf = sb("mhalf", [P, KC])
        bank = ctx.enter_context(nc.psum_tensor(f"{tag}_bank", [P, 8 * BANK], F32))

        const_in = sem("const_in")
        band_step = sem("band_step")
        mhalf_set = sem("mhalf_set")
        x_arrived = [sem(f"x_arrived{i}") for i in range(2)]
        gn_step = sem("gn_step")
        gm_full = sem("gm_full")
        gm_read = sem("gm_read")
        gn_rstd = sem("gn_rstd")
        xn_done = sem("xn_done")
        xt_full = sem("xt_full")
        xt_done = sem("xt_done")
        y_full = sem("y_full")
        y_done = sem("y_done")
        stored = [sem(f"stored{i}") for i in range(2)]
        held = sem("held")

        def hold(engine):
            engine.sem_inc(held, 1)

        block = ctx.enter_context(nc.Block())

        @block.sync
        def _(sp):
            sp.sem_inc(stored[0], 1)
            sp.sem_inc(stored[1], 1)
            for dst, src in ((ident[:], ident_dram), (group[:], group_dram), (masks[:], masks_dram),
                             (taps[:], taps_dram.partition_broadcast(P))):
                sp.dma_start(dst, src).then_inc(const_in, 16)

            def load(b, j):
                src = x_in[bass.ds(b, 1)].rearrange("a (k p) l -> p (a k) l", p=P)
                sp.dma_start(xin[:, j], src).then_inc(x_arrived[j], 16)

            def stores(b, bb, j):
                for k in range(KC):
                    sp.wait_ge(y_done, (b + j) * KC + k + 1 + 1)
                    sp.dma_start(x_out[bass.ds(b + j, 1), k * P:(k + 1) * P, :].rearrange("a p l -> (a p) l"),
                                 y[:, k % 2, :]).then_inc(stored[k % 2], 16)

            load(0, 0)

            def pair(b, last):
                load(b + 1, 1)
                stores(b, None, 0)
                if not last:
                    load(b + 2, 0)
                stores(b, None, 1)

            if batches > 2:
                with sp.Fori(0, batches - 2, 2) as b:
                    pair(b, False)
            pair(batches - 2, True)
            for i in range(2):
                sp.wait_ge(stored[i], batches * 32 + 1)

        @block.tensor
        def _(pe):
            pe.sem_inc(y_full, 1)
            mm = nc.tensor.matmul
            pe.wait_ge(const_in, 64)
            pe.wait_ge(band_step, TAPS)
            with pe.Fori(0, batches) as b:
                pe.wait_ge(gn_step, b * 15 + 12)
                mm(bank[:, 0:2 * KC], group[:], gmv[:].rearrange("p k s -> p (k s)"), start=True, stop=True).then_inc(gm_full, 1)
                pe.wait_ge(gn_step, b * 15 + 14)
                mm(bank[:, BANK:BANK + KC], group[:], gd2[:], start=True, stop=True).then_inc(gm_full, 1)
                pe.wait_ge(xn_done, b * KC + KC)
                for lb in range(8):
                    if lb >= 2:
                        pe.wait_ge(xt_done, b * 8 + lb - 1)
                    for k in range(KC):
                        o = (2 + lb % 2) * BANK + k * P
                        last = mm(bank[:, o:o + P], xn[:, k, lb * P:(lb + 1) * P], ident[:],
                                  start=(k == 0), stop=(k == KC - 1), is_transpose=True)
                    last.then_inc(xt_full, 1)
                pe.wait_ge(xt_done, b * 8 + 8)
                for k in range(KC):
                    if k < 2:
                        pe.wait_ge(y_done, b * KC + 1)
                    else:
                        pe.wait_ge(y_done, b * KC + k - 1 + 1)
                    started = set()
                    for j in range(8):
                        lo, hi = max(0, (4 * j - 1) * WIDTH), min(L1, (4 * j + 6) * WIDTH)
                        for q in range(2):
                            a, e = max(lo, q * BANK), min(hi, (q + 1) * BANK)
                            if a >= e:
                                continue
                            base = (4 + 2 * (k % 2)) * BANK
                            off = (4 * j - 1) * WIDTH
                            last = mm(bank[:, base + a:base + e], xt[:, j, k * P:(k + 1) * P], band[:, a - off:e - off],
                                      start=q not in started, stop=(j == (4 if q == 0 else 7)), skip_group_check=True)
                            started.add(q)
                    last.then_inc(y_full, 1)

        @block.scalar
        def _(act):
            with act.Fori(0, batches) as b:
                for lb in range(8):
                    act.wait_ge(xt_full, b * 8 + lb + 1)
                    act.wait_ge(y_full, b * KC + 1)
                    nc.scalar.activation(xt[:, lb, :], bank[:, (2 + lb % 2) * BANK:(3 + lb % 2) * BANK],
                                         ACT.Copy).then_inc(xt_done, 1)

        @block.gpsimd
        def _(pool):
            nc.gpsimd.memset(mhalf[:], -0.5).then_inc(mhalf_set, 1)
            pool.wait_ge(mhalf_set, 1)
            with pool.Fori(0, batches) as b:
                pool.wait_ge(gn_step, b * 15 + 15)
                nc.gpsimd.tensor_tensor(gr[:], gve[:], mhalf[:], ALU.pow).then_inc(gn_rstd, 1)

        @block.vector
        def _(dve):
            dve.sem_inc(y_done, 1)
            V = nc.vector
            dve.wait_ge(const_in, 64)
            V.tensor_scalar(band[:], masks[:, 0, :], taps[:, 0:1], None, ALU.mult).then_inc(band_step, 1)
            for t in range(1, TAPS):
                dve.wait_ge(band_step, t)
                V.scalar_tensor_tensor(band[:], masks[:, t, :], taps[:, t:t + 1], band[:], ALU.mult, ALU.add).then_inc(band_step, 1)

            def batch(b, bj, j, half):
                dve.wait_ge(x_arrived[j], half * 16 + 16)
                g0 = b * 15
                for k in range(KC):
                    for q in range(2):
                        V.bn_stats(gst[:, k, 6 * q:6 * q + 6], xin[:, j, k, q * BANK:(q + 1) * BANK]).then_inc(gn_step, 1)
                for k in range(KC):
                    dve.wait_ge(gn_step, g0 + 2 * k + 2)
                    hold(dve)
                    V.bn_aggr(gmv[:, k, :], gst[:, k, :]).then_inc(gn_step, 1)
                dve.wait_ge(gm_full, b * 2 + 1)
                V.tensor_copy(ggm[:].rearrange("p k s -> p (k s)"), bank[:, 0:2 * KC]).then_inc(gm_read, 1)
                dve.wait_ge(gm_read, b * 2 + 1)
                V.tensor_tensor(gd[:], gmv[:, :, 0], ggm[:, :, 0], ALU.subtract).then_inc(gn_step, 1)
                dve.wait_ge(gn_step, g0 + 13)
                V.tensor_tensor(gd2[:], gd[:], gd[:], ALU.mult).then_inc(gn_step, 1)
                dve.wait_ge(gm_full, b * 2 + 2)
                V.tensor_tensor(gve[:], bank[:, BANK:BANK + KC], ggm[:, :, 1], ALU.add).then_inc(gm_read, 1)
                dve.wait_ge(gm_read, b * 2 + 2)
                V.tensor_scalar(gve[:], gve[:], EPS, None, ALU.add).then_inc(gn_step, 1)
                dve.wait_ge(gn_rstd, b + 1)
                for k in range(KC):
                    V.tensor_scalar(xn[:, k, :], xin[:, j, k, :], ggm[:, k, 0:1], gr[:, k:k + 1],
                                    ALU.subtract, ALU.mult).then_inc(xn_done, 1)
                for k in range(KC):
                    dve.wait_ge(y_full, b * KC + k + 1 + 1)
                    if k >= 2:
                        dve.wait_ge(stored[k % 2], b * 32 + 16 + 1)
                    else:
                        dve.wait_ge(stored[k % 2], b * 32 + 1)
                    base = (4 + 2 * (k % 2)) * BANK
                    V.tensor_tensor(y[:, k % 2, :], bank[:, base:base + L1], xin[:, j, k, :], ALU.add).then_inc(y_done, 1)

            with dve.Fori(0, batches // 2) as pair:
                for j in range(2):
                    batch(pair * 2 + j, None, j, pair)


def attention_layer(nc, tag, x_in, x_out, wqkv_dram, wproj_dram, vec_dram, ident_dram, group_dram, mean_dram, batches):
    ctx = ExitStack()
    with ctx:
        def sb(name, shape):
            return ctx.enter_context(nc.sbuf_tensor(f"{tag}_{name}", shape, F32))

        def sem(name):
            return ctx.enter_context(nc.semaphore(f"{tag}_{name}"))

        ident = sb("ident", [P, P])
        group = sb("group", [P, P])
        mean = sb("mean", [P, P])
        wqkv = sb("wqkv", [P, KC, 3 * C])
        wproj = sb("wproj", [P, KC, C])
        vec = sb("vec", [P, 24])
        gamma, beta, bq, bv, bo = vec[:, 0:4], vec[:, 4:8], vec[:, 8:16], vec[:, 16:20], vec[:, 20:24]
        xin = sb("xin", [P, KC, L1])
        xf = sb("xf", [P, KC, L1])
        qk = sb("qk", [P, 8, L1])
        vt = sb("vt", [P, NB, C])
        vals = sb("vals", [P, KC, L1])
        prob = sb("prob", [P, 2, L1])
        pt = sb("pt", [P, 2, L1])
        vn = sb("vn", [P, C])
        y = sb("y", [P, 2, L1])
        mx = sb("mx", [P, 2])
        nbias = sb("nbias", [P, 2])
        rs = sb("rs", [P, 2, HEADS])
        rr = sb("rr", [P, HEADS])
        gst = sb("gst", [P, KC, 12])
        gmv = sb("gmv", [P, KC, 2])
        ggm = sb("ggm", [P, KC, 2])
        gd = sb("gd", [P, KC])
        gd2 = sb("gd2", [P, KC])
        gve = sb("gve", [P, KC])
        gr = sb("gr", [P, KC])
        st = sb("st", [P, KC, 2])
        st2 = sb("st2", [P, KC])
        lm = sb("lm", [P, 2])
        ld = sb("ld", [P, KC])
        ld2 = sb("ld2", [P, KC])
        lve = sb("lve", [P, 1])
        lr = sb("lr", [P, 1])
        sc = sb("sc", [P, KC])
        aa = sb("aa", [P, KC])
        bb = sb("bb", [P, KC])
        cc = sb("cc", [P, KC])
        mhalf = sb("mhalf", [P, KC])
        bank = ctx.enter_context(nc.psum_tensor(f"{tag}_bank", [P, 8 * BANK], F32))

        def bk(i, n=BANK):
            return bank[:, i * BANK:i * BANK + n]

        T_QK, T_V, T_O, TILES = 4, 20, 28, 36
        BY_ACT = {t for t in range(T_QK, T_O) if t % 2 == 0}
        PER_A, PER_D = len(BY_ACT), TILES - len(BY_ACT)

        def left(t):
            return sum((i in BY_ACT) == (t in BY_ACT) for i in range(t + 1))

        UNITS = NB * HEADS
        STEPS = 8 + 4 + 2 + 1 + 3 + 2 + 1 + 5

        const_in = sem("const_in")
        mhalf_set = sem("mhalf_set")
        x_arrived = sem("x_arrived")
        gn_step = sem("gn_step")
        rstd = sem("rstd")
        xf_done = sem("xf_done")
        tile_full = sem("tile_full")
        tile_act = sem("tile_act")
        tile_dve = sem("tile_dve")
        s_full = sem("s_full")
        max_done = sem("max_done")
        bias_done = sem("bias_done")
        p_full = sem("p_full")
        pt_full = sem("pt_full")
        pt_dve = sem("pt_dve")
        pt_act = sem("pt_act")
        o_full = sem("o_full")
        rr_done = sem("rr_done")
        vn_done = sem("vn_done")
        vtr_full = sem("vtr_full")
        vals_done = sem("vals_done")
        stored = [sem(f"stored{i}") for i in range(2)]
        held = sem("held")

        def hold(engine):
            engine.sem_inc(held, 1)

        block = ctx.enter_context(nc.Block())

        @block.sync
        def _(sp):
            sp.sem_inc(stored[0], 1)
            sp.sem_inc(stored[1], 1)
            for dst, src in ((wqkv[:], wqkv_dram), (wproj[:], wproj_dram), (vec[:], vec_dram),
                             (ident[:], ident_dram), (group[:], group_dram), (mean[:], mean_dram)):
                sp.dma_start(dst, src).then_inc(const_in, 16)
            with sp.Fori(0, batches) as b:
                sp.wait_ge(tile_dve, b * PER_D + 1)
                sp.dma_start(xin[:], x_in[bass.ds(b, 1)].rearrange("a (k p) l -> p (a k) l", p=P)).then_inc(x_arrived, 16)
                for m in range(KC):
                    sp.wait_ge(tile_dve, b * PER_D + left(T_O + 2 * m + 1) + 1)
                    sp.dma_start(x_out[bass.ds(b, 1), m * P:(m + 1) * P, :].rearrange("a p l -> (a p) l"),
                                 y[:, m % 2, :]).then_inc(stored[m % 2], 16)
            for i in range(2):
                sp.wait_ge(stored[i], batches * 32 + 1)

        @block.tensor
        def _(pe):
            mm = nc.tensor.matmul
            pe.wait_ge(const_in, 96)

            def tile_wait(b, t):
                if t < 8:
                    pe.wait_ge(tile_dve, b * PER_D + 1)
                elif t - 8 in BY_ACT:
                    pe.wait_ge(tile_act, b * PER_A + left(t - 8))
                else:
                    pe.wait_ge(tile_dve, b * PER_D + left(t - 8) + 1)

            def scores(b, u):
                i, h = u // HEADS, u % HEADS
                if u >= 2:
                    pe.wait_ge(p_full, b * UNITS + u - 1)
                r0 = (h % 2) * DH
                for q in range(2):
                    o = (u % 2) * 2 * BANK + q * BANK
                    last = mm(bank[:, o:o + BANK], qk[r0:r0 + DH, h // 2, i * P:(i + 1) * P],
                              qk[r0:r0 + DH, 4 + h // 2, q * BANK:(q + 1) * BANK], start=True, stop=True)
                last.then_inc(s_full, 1)

            def turn(b, u):
                pe.wait_ge(p_full, b * UNITS + u + 1)
                if u >= 1:
                    pe.wait_ge(pt_dve, b * UNITS + u)
                    pe.wait_ge(pt_act, b * UNITS + u)
                for m in range(NB):
                    last = mm(bank[:, 4 * BANK + m * P:4 * BANK + (m + 1) * P], prob[:, u % 2, m * P:(m + 1) * P],
                              ident[:], start=(m % 4 == 0), stop=(m % 4 == 3), is_transpose=True)
                last.then_inc(pt_full, 1)

            def weigh(b, u):
                i, h = u // HEADS, u % HEADS
                pe.wait_ge(pt_dve, b * UNITS + u + 1)
                pe.wait_ge(pt_act, b * UNITS + u + 1)
                if h == 0 and i > 0:
                    pe.wait_ge(vn_done, b * NB + i)
                for m in range(NB):
                    last = mm(bank[:, 6 * BANK + h * DH:6 * BANK + (h + 1) * DH], pt[:, u % 2, m * P:(m + 1) * P],
                              vt[:, m, h * DH:(h + 1) * DH], start=(m == 0), stop=(m == NB - 1))
                last.then_inc(o_full, 1)

            def back(b, i):
                pe.wait_ge(vn_done, b * NB + i + 1)
                if i > 0:
                    pe.wait_ge(vals_done, b * NB + i)
                for k in range(KC):
                    last = mm(bank[:, 7 * BANK + k * P:7 * BANK + (k + 1) * P], vn[:, k * P:(k + 1) * P], ident[:],
                              start=(k == 0), stop=(k == KC - 1), is_transpose=True)
                last.then_inc(vtr_full, 1)

            with pe.Fori(0, batches) as b:
                g0 = b * STEPS
                tile_wait(b, 0)
                pe.wait_ge(gn_step, g0 + 12)
                mm(bk(0)[:, 0:2 * KC], group[:], gmv[:].rearrange("p k s -> p (k s)"), start=True, stop=True).then_inc(tile_full, 1)
                pe.wait_ge(gn_step, g0 + 14)
                mm(bk(1)[:, 0:KC], group[:], gd2[:], start=True, stop=True).then_inc(tile_full, 1)
                pe.wait_ge(gn_step, g0 + 18)
                for k in range(KC):
                    last = mm(bk(2)[:, 0:2], mean[:], st[:, k, :], start=(k == 0), stop=(k == KC - 1))
                last.then_inc(tile_full, 1)
                pe.wait_ge(gn_step, g0 + 20)
                for k in range(KC):
                    last = mm(bk(3)[:, 0:1], mean[:], ld2[:, k:k + 1], start=(k == 0), stop=(k == KC - 1))
                last.then_inc(tile_full, 1)
                pe.wait_ge(xf_done, b * KC + KC)
                for m in range(8):
                    for q in range(2):
                        t = T_QK + 2 * m + q
                        tile_wait(b, t)
                        for k in range(KC):
                            last = mm(bk(t % 8), wqkv[:, k, m * P:(m + 1) * P], xf[:, k, q * BANK:(q + 1) * BANK],
                                      start=(k == 0), stop=(k == KC - 1))
                        last.then_inc(tile_full, 1)
                for i in range(NB):
                    t = T_V + i
                    tile_wait(b, t)
                    for k in range(KC):
                        last = mm(bk(t % 8), xf[:, k, i * P:(i + 1) * P], wqkv[:, k, 2 * C:3 * C],
                                  start=(k == 0), stop=(k == KC - 1))
                    last.then_inc(tile_full, 1)
                pe.wait_ge(tile_act, b * PER_A + PER_A)
                pe.wait_ge(tile_dve, b * PER_D + left(T_V + 7) + 1)
                for u in range(UNITS + 2):
                    if u < UNITS:
                        scores(b, u)
                    if 1 <= u <= UNITS:
                        turn(b, u - 1)
                    if u >= 2:
                        weigh(b, u - 2)
                        if u - 2 > 7 and (u - 2) % HEADS == 1:
                            back(b, (u - 2) // HEADS - 1)
                back(b, NB - 1)
                pe.wait_ge(vals_done, b * NB + NB)
                for m in range(KC):
                    for q in range(2):
                        t = T_O + 2 * m + q
                        if t >= T_O + 8:
                            tile_wait(b, t)
                        for k in range(KC):
                            last = mm(bk(t % 8), wproj[:, k, m * P:(m + 1) * P], vals[:, k, q * BANK:(q + 1) * BANK],
                                      start=(k == 0), stop=(k == KC - 1))
                        last.then_inc(tile_full, 1)

        @block.scalar
        def _(act):
            A = nc.scalar.activation
            act.wait_ge(const_in, 96)

            def exps(b, u):
                act.wait_ge(bias_done, b * UNITS + u + 1)
                i, h = u // HEADS, u % HEADS
                if u >= 2:
                    act.wait_ge(pt_full, b * UNITS + u - 1)
                if h == 0 and i >= 2:
                    act.wait_ge(rr_done, b * NB + i - 1)
                A(prob[:, u % 2, :], bank[:, (u % 2) * 2 * BANK:(u % 2) * 2 * BANK + L1], ACT.Exp,
                  bias=nbias[:, u % 2:u % 2 + 1], scale=SCALE, accum_out=rs[:, i % 2, h:h + 1]).then_inc(p_full, 1)

            def half(b, u):
                act.wait_ge(pt_full, b * UNITS + u + 1)
                if u >= 2:
                    act.wait_ge(o_full, b * UNITS + u - 1)
                A(pt[:, u % 2, BANK:], bank[:, 5 * BANK:6 * BANK], ACT.Copy).then_inc(pt_act, 1)

            def values(b, i):
                act.wait_ge(vtr_full, b * NB + i + 1)
                for k in range(KC):
                    last = A(vals[:, k, i * P:(i + 1) * P], bank[:, 7 * BANK + k * P:7 * BANK + (k + 1) * P],
                             ACT.Identity, bias=bv[:, k:k + 1])
                last.then_inc(vals_done, 1)

            with act.Fori(0, batches) as b:
                for t in sorted(BY_ACT):
                    act.wait_ge(tile_full, b * TILES + t + 1)
                    if t < T_V:
                        m, q = (t - T_QK) // 2, (t - T_QK) % 2
                        A(qk[:, m, q * BANK:(q + 1) * BANK], bk(t % 8), ACT.Identity, bias=bq[:, m:m + 1]).then_inc(tile_act, 1)
                    else:
                        A(vt[:, t - T_V, :], bk(t % 8), ACT.Copy).then_inc(tile_act, 1)
                for u in range(UNITS + 1):
                    if u < UNITS:
                        exps(b, u)
                    if u >= 1:
                        half(b, u - 1)
                        if u - 1 > 10 and (u - 1) % HEADS == 3:
                            values(b, (u - 1) // HEADS - 1)
                values(b, NB - 1)

        @block.gpsimd
        def _(pool):
            nc.gpsimd.memset(mhalf[:], -0.5).then_inc(mhalf_set, 1)
            pool.wait_ge(mhalf_set, 1)
            with pool.Fori(0, batches) as b:
                g0 = b * STEPS
                pool.wait_ge(gn_step, g0 + 15)
                nc.gpsimd.tensor_tensor(gr[:], gve[:], mhalf[:], ALU.pow).then_inc(rstd, 1)
                pool.wait_ge(gn_step, g0 + 21)
                nc.gpsimd.tensor_tensor(lr[:], lve[:], mhalf[:, 0:1], ALU.pow).then_inc(rstd, 1)

        @block.vector
        def _(dve):
            dve.sem_inc(tile_dve, 1)
            V = nc.vector
            dve.wait_ge(const_in, 96)

            def maximum(b, u):
                dve.wait_ge(s_full, b * UNITS + u + 1)
                if u >= 2:
                    dve.wait_ge(p_full, b * UNITS + u - 1)
                V.reduce_max(mx[:, u % 2:u % 2 + 1], bank[:, (u % 2) * 2 * BANK:(u % 2) * 2 * BANK + L1], AX.X).then_inc(max_done, 1)
                dve.wait_ge(max_done, b * UNITS + u + 1)
                V.tensor_scalar(nbias[:, u % 2:u % 2 + 1], mx[:, u % 2:u % 2 + 1], -SCALE, None, ALU.mult).then_inc(bias_done, 1)

            def half(b, u):
                dve.wait_ge(pt_full, b * UNITS + u + 1)
                if u >= 2:
                    dve.wait_ge(o_full, b * UNITS + u - 1)
                V.tensor_copy(pt[:, u % 2, 0:BANK], bank[:, 4 * BANK:5 * BANK]).then_inc(pt_dve, 1)

            def normalise(b, i):
                dve.wait_ge(p_full, b * UNITS + (i + 1) * HEADS)
                V.reciprocal(rr[:], rs[:, i % 2, :]).then_inc(rr_done, 1)
                dve.wait_ge(rr_done, b * NB + i + 1)
                dve.wait_ge(o_full, b * UNITS + (i + 1) * HEADS)
                if i > 0:
                    dve.wait_ge(vtr_full, b * NB + i)
                V.tensor_tensor(vn[:].rearrange("p (h d) -> p h d", d=DH),
                                bk(6).rearrange("p (h d) -> p h d", d=DH),
                                rr[:].unsqueeze(2).broadcast_to([P, HEADS, DH]), ALU.mult).then_inc(vn_done, 1)

            with dve.Fori(0, batches) as b:
                n = [0]
                g0 = b * STEPS

                def step(ins, wait=True):
                    n[0] += 1
                    ins.then_inc(gn_step, 1)
                    if wait:
                        dve.wait_ge(gn_step, g0 + n[0])

                dve.wait_ge(x_arrived, b * 16 + 16)
                for k in range(KC):
                    for q in range(2):
                        step(V.bn_stats(gst[:, k, 6 * q:6 * q + 6], xin[:, k, q * BANK:(q + 1) * BANK]), False)
                dve.wait_ge(gn_step, g0 + 8)
                hold(dve)
                for k in range(KC):
                    step(V.bn_aggr(gmv[:, k, :], gst[:, k, :]), False)
                dve.wait_ge(tile_full, b * TILES + 1)
                V.tensor_copy(ggm[:].rearrange("p k s -> p (k s)"), bk(0)[:, 0:2 * KC]).then_inc(tile_dve, 1)
                dve.wait_ge(tile_dve, b * PER_D + 1 + 1)
                step(V.tensor_tensor(gd[:], gmv[:, :, 0], ggm[:, :, 0], ALU.subtract))
                step(V.tensor_tensor(gd2[:], gd[:], gd[:], ALU.mult))
                dve.wait_ge(tile_full, b * TILES + 2)
                V.tensor_tensor(gve[:], bk(1)[:, 0:KC], ggm[:, :, 1], ALU.add).then_inc(tile_dve, 1)
                dve.wait_ge(tile_dve, b * PER_D + 2 + 1)
                step(V.tensor_scalar(gve[:], gve[:], EPS, None, ALU.add))
                dve.wait_ge(rstd, b * 2 + 1)
                step(V.tensor_tensor(st2[:], gmv[:, :, 1], gr[:], ALU.mult))
                step(V.tensor_tensor(st[:, :, 0], gd[:], gr[:], ALU.mult))
                step(V.tensor_tensor(st[:, :, 1], st2[:], gr[:], ALU.mult))
                dve.wait_ge(tile_full, b * TILES + 3)
                V.tensor_copy(lm[:], bk(2)[:, 0:2]).then_inc(tile_dve, 1)
                dve.wait_ge(tile_dve, b * PER_D + 3 + 1)
                step(V.tensor_scalar(ld[:], st[:, :, 0], lm[:, 0:1], None, ALU.subtract))
                step(V.tensor_tensor(ld2[:], ld[:], ld[:], ALU.mult))
                dve.wait_ge(tile_full, b * TILES + 4)
                V.tensor_tensor(lve[:], bk(3)[:, 0:1], lm[:, 1:2], ALU.add).then_inc(tile_dve, 1)
                dve.wait_ge(tile_dve, b * PER_D + 4 + 1)
                step(V.tensor_scalar(lve[:], lve[:], EPS, None, ALU.add))
                dve.wait_ge(rstd, b * 2 + 2)
                step(V.tensor_scalar(sc[:], gamma, lr[:, 0:1], None, ALU.mult))
                step(V.tensor_tensor(aa[:], sc[:], gr[:], ALU.mult))
                step(V.tensor_tensor(bb[:], ggm[:, :, 0], gr[:], ALU.mult))
                step(V.scalar_tensor_tensor(cc[:], bb[:], lm[:, 0:1], sc[:], ALU.add, ALU.mult))
                step(V.tensor_tensor(bb[:], beta, cc[:], ALU.subtract))
                assert n[0] == STEPS
                for k in range(KC):
                    V.tensor_scalar(xf[:, k, :], xin[:, k, :], aa[:, k:k + 1], bb[:, k:k + 1], ALU.mult, ALU.add).then_inc(xf_done, 1)
                for t in range(T_QK, T_O):
                    if t in BY_ACT:
                        continue
                    dve.wait_ge(tile_full, b * TILES + t + 1)
                    if t < T_V:
                        m, q = (t - T_QK) // 2, (t - T_QK) % 2
                        V.tensor_scalar(qk[:, m, q * BANK:(q + 1) * BANK], bk(t % 8), bq[:, m:m + 1], None, ALU.add).then_inc(tile_dve, 1)
                    else:
                        V.tensor_copy(vt[:, t - T_V, :], bk(t % 8)).then_inc(tile_dve, 1)
                for u in range(UNITS + 2):
                    if u < UNITS:
                        maximum(b, u)
                    if 1 <= u <= UNITS:
                        half(b, u - 1)
                    if u >= 2 and (u - 2) % HEADS == HEADS - 1:
                        normalise(b, (u - 2) // HEADS)
                for m in range(KC):
                    for q in range(2):
                        t = T_O + 2 * m + q
                        dve.wait_ge(tile_full, b * TILES + t + 1)
                        dve.wait_ge(stored[m % 2], b * 32 + 16 * (m // 2) + 1)
                        V.scalar_tensor_tensor(y[:, m % 2, q * BANK:(q + 1) * BANK], bk(t % 8), bo[:, m:m + 1],
                                               xin[:, m, q * BANK:(q + 1) * BANK], ALU.add, ALU.add).then_inc(tile_dve, 1)


def build_program(nc, a, batches):
    shape = (batches, C, L1)
    between = [nc.dram_tensor(f"x_after_{i}", shape, F32, kind="Internal").ap() for i in range(3)]
    ssm_layer(nc, "l0", a["x"], between[0], a["w0"], a["dtw0"], a["ident"], a["group"], batches)
    conv_layer(nc, "l1", between[0], between[1], a["taps"], a["masks"], a["ident"], a["group"], batches)
    ssm_layer(nc, "l2", between[1], between[2], a["w2"], a["dtw2"], a["ident"], a["group"], batches)
    attention_layer(nc, "l3", between[2], a["out"], a["wqkv"], a["wproj"], a["vec"], a["ident"], a["group"],
                    a["mean"], batches)


def chunks(m):
    return np.ascontiguousarray(m.reshape(m.shape[0] // P, P, -1).transpose(1, 0, 2))


def ssm_weights(g):
    parts = [g("in_w").T, g("c1_w").T]
    parts += [g(n).transpose(1, 2, 3, 0).reshape(D, 4 * D) for n in ("c2_w", "c3_w")]
    parts += [g("out_w").T] + [g(f"xw{i}").T for i in (1, 2, 3)] + [g(f"Al{i}") for i in (1, 2, 3)]
    parts += [g(n)[:, None] for n in ("in_b", "c1_b", "c2_b", "c3_b", "out_b")]
    parts += [g(f"{n}{i}")[:, None] for n in ("dtb", "Dv", "g", "be") for i in (1, 2, 3)]
    w = np.concatenate([chunks(m).reshape(P, -1) for m in parts], axis=1)
    assert w.shape[1] == W_TOTAL
    return np.ascontiguousarray(w), np.ascontiguousarray(np.stack([g(f"dtw{i}").T for i in (1, 2, 3)], axis=1))


def band_masks():
    m = np.zeros((4, WIDTH, TAPS, ROWS, WIDTH), np.float32)
    for a in range(4):
        for b in range(4):
            for s in range(4):
                for w in range(WIDTH):
                    if 0 <= w + b - 1 < WIDTH:
                        m[s, w, 4 * a + b, s + a, w + b - 1] = 1.0
    return m.reshape(P, TAPS, ROWS * WIDTH)


def kernel(**inputs):
    import concourse.bacc as bacc
    from concourse.bass_utils import run_bass_kernel_spmd

    def layer(i):
        return lambda name: np.asarray(inputs[f"L{i}_conv_{name}"])

    x = np.asarray(inputs["x"])
    batches = x.shape[0]
    same_group = np.arange(P)[:, None] // 16 == np.arange(P)[None, :] // 16
    arrays = {"x": np.ascontiguousarray(x.reshape(batches, C, L1)),
              "ident": np.eye(P, dtype=np.float32),
              "group": np.where(same_group, np.float32(1 / 16), np.float32(0)),
              "mean": np.full((P, P), 1 / C, np.float32),
              "masks": band_masks(),
              "taps": np.ascontiguousarray(np.asarray(inputs["L1_conv_kernel"]).reshape(TAPS)),
              "wqkv": chunks(layer(3)("w_qkv").T), "wproj": chunks(layer(3)("w_proj").T),
              "vec": np.concatenate([chunks(layer(3)(n)[:, None])[:, :, 0]
                                     for n in ("gn_gamma", "gn_beta", "b_qkv", "b_proj")], axis=1)}
    for i in (0, 2):
        arrays[f"w{i}"], arrays[f"dtw{i}"] = ssm_weights(layer(i))

    nc = bacc.Bacc("TRN2", target_bir_lowering=False, num_devices=1)
    aps = {n: nc.dram_tensor(f"in_{n}", a.shape, mybir.dt.from_np(a.dtype), kind="ExternalInput").ap()
           for n, a in arrays.items()}
    aps["out"] = nc.dram_tensor("out", arrays["x"].shape, F32, kind="ExternalOutput").ap()
    build_program(nc, aps, batches)
    r = run_bass_kernel_spmd(nc, [{f"in_{n}": np.ascontiguousarray(a) for n, a in arrays.items()}], core_ids=[0])
    return r.results[0]["out"].reshape(x.shape)
```

```python
import concourse.bass as bass
import numpy as np
from concourse import mybir
from contextlib import ExitStack

F32 = mybir.dt.float32
ALU = mybir.AluOpType
ACT = mybir.ActivationFunctionType
AX = mybir.AxisListType

P = 128
C = 512
KC = C // P
L1, L2, L3 = 1024, 256, 64
D = 256
NH = D // P
N = 16
R = 8
BANK = 512
EPS = 1e-5
TAPS, ROWS, WIDTH = 16, 7, 32
HEADS, DH = 8, 64
NB = L1 // P
SCALE = float(C) ** -0.5

W_COLS = {}
_at = 0
for _name, _n in (("inz", KC * D), ("c2", NH * 4 * D), ("c3", NH * 4 * D), ("out", NH * C),
                  ("xw1", NH * 2 * N), ("xw2", NH * 2 * N), ("xw3", NH * 2 * N),
                  ("Al1", NH * N), ("Al2", NH * N), ("Al3", NH * N),
                  ("in_b", KC), ("c1_b", NH), ("c2_b", NH), ("c3_b", NH), ("out_b", KC),
                  ("dtb1", NH), ("dtb2", NH), ("dtb3", NH), ("Dv1", NH), ("Dv2", NH), ("Dv3", NH),
                  ("g1", NH), ("g2", NH), ("g3", NH), ("be1", NH), ("be2", NH), ("be3", NH)):
    W_COLS[_name] = (_at, _n)
    _at += _n
W_TOTAL = _at


def ssm_layer(nc, tag, x_in, x_out, w_dram, nat_dram, low_dram, ident_dram, group_dram, batches):
    ctx = ExitStack()
    with ctx:
        def sb(name, shape):
            return ctx.enter_context(nc.sbuf_tensor(f"{tag}_{name}", shape, F32))

        def sem(name):
            return ctx.enter_context(nc.semaphore(f"{tag}_{name}"))

        PITCH = max(NH * (L1 + 1), 4 * NH * (L2 + 1), N * NH * (L3 + 1))
        NA, NU = 2, 4
        W = sb("W", [P, W_TOTAL])
        wc = sb("wc", [P, KC, D])
        wd = sb("wd", [P, 3, NH, D])
        f1_b = sb("f1_b", [P, NH])
        ident = sb("ident", [P, P])
        group = sb("group", [P, P])
        xin = sb("xin", [P, KC, L1])
        z = sb("z", [P, NH, L1])
        f1 = sb("f1", [P, NH, L1])
        f2 = sb("f2", [P, NH, L2])
        f3 = sb("f3", [P, NH, L3])
        dA_ring = sb("dA", [P, NA, PITCH])
        u_ring = sb("u", [P, NU, PITCH])
        b_sb = sb("b_sb", [P, 2, 1024])
        delta = {"3": sb("dl3", [P, NH, L3]), "2": sb("dl2", [P, NH, L2]),
                 "1f": sb("dl1f", [P, NH, L1]), "1b": sb("dl1b", [P, NH, L1])}
        dx = {"3": sb("dx3", [P, NH, L3]), "2": sb("dx2", [P, NH, L2]),
              "1f": sb("dx1f", [P, NH, L1]), "1b": sb("dx1b", [P, NH, L1])}
        bct = {"3": sb("bct3", [P, 1, 2 * N]), "2": sb("bct2", [P, 2, 2 * N]),
               "1f": sb("bct1f", [P, NB, 2 * N]), "1b": sb("bct1b", [P, NB, 2 * N])}
        hn_buf = sb("hn", [P, 8, D])
        hn = {"3": hn_buf[:, 0:2, :], "2": hn_buf[:, 2:6, :], "1f": hn_buf[:], "1b": hn_buf[:]}
        out1 = sb("out1", [P, NH, L1])
        xres = sb("xres", [P, 2, BANK])
        y3s = sb("y3s", [P, NH, L3])
        y2s = sb("y2s", [P, NH, L2])
        T_u = sb("T_u", [P, 2, BANK])
        T_ln = sb("T_ln", [P, 2, BANK])
        T_r = sb("T_r", [P, 2, BANK])
        T_c = sb("T_c", [P, BANK])
        negA = sb("negA", [P, 3 * NH * N])
        bt = sb("bt", [P, 4 * NH])
        gst = sb("gst", [P, KC, 12])
        gmv = sb("gmv", [P, KC, 2])
        ggm = sb("ggm", [P, KC, 2])
        gd = sb("gd", [P, KC])
        gd2 = sb("gd2", [P, KC])
        gve = sb("gve", [P, KC])
        gr = sb("gr", [P, KC])
        lst = sb("lst", [P, 8, 6])
        lmv = sb("lmv", [P, 8, 2])
        lve = sb("lve", [P, 8])
        lr = sb("lr", [P, 8])
        mhalf = sb("mhalf", [P, 8])
        zero = sb("zero", [P, 2 * N])
        nat = u_ring[:, 0, 0:NH * 768].rearrange("p (k o) -> p k o", k=NH)
        low = u_ring[0:R, 1, 0:6 * D].rearrange("p (a s o) -> p a s o", a=2, s=3)
        bank = ctx.enter_context(nc.psum_tensor(f"{tag}_bank", [P, 8 * BANK], F32))
        BANK_B, BANK_T, BANK_C, BANK_X = 4, 5, 6, 3

        def bk(i, n=BANK):
            return bank[:, i * BANK:i * BANK + n]

        def w(name):
            a, n = W_COLS[name]
            return W[:, a:a + n]

        inz = w("inz").rearrange("p (k o) -> p k o", k=KC)
        c2T = w("c2").rearrange("p (k t o) -> p k t o", k=NH, t=4)
        c3T = w("c3").rearrange("p (k t o) -> p k t o", k=NH, t=4)
        outT = w("out").rearrange("p (k o) -> p k o", k=NH)
        xwT = {s: w(f"xw{s}").rearrange("p (k o) -> p k o", k=NH) for s in "123"}

        PASSES = [("3", f3, L3, "fb", "3"), ("2", f2, L2, "fb", "2"), ("1f", f1, L1, "f", "1"), ("1b", f1, L1, "b", "2")]
        LN_BLOCKS = [2, 4, 8, 8]
        CH, FIRST, VITEM, END = [], [], [], []
        ITEMS = 0
        for pi, (key, f, L, dirs, s) in enumerate(PASSES):
            FIRST.append(len(CH))
            VITEM.append(ITEMS)
            ITEMS += 1
            for n0 in range(0, N, 1024 // L):
                CH.append(dict(key=key, L=L, dirs=dirs, n0=n0, ns=1024 // L, pi=pi, item=ITEMS, wset=s,
                               in_item=ITEMS + len(dirs) - 1))
                ITEMS += len(dirs)
            END.append(ITEMS)
        NCH = len(CH)
        for i, c in enumerate(CH):
            c["scan0"] = sum(len(q["dirs"]) for q in CH[:i])
            c["pad_a"] = i - FIRST[c["pi"]] < NA and c["pi"] != 3
            c["pad_u"] = c["pi"] != 3 and c["in_item"] - VITEM[c["pi"]] <= NU
        for i, c in enumerate(CH):
            c["a_done"] = sum(q["pad_a"] + q["ns"] * NH for q in CH[:i + 1])
            c["u_done"] = sum(q["pad_u"] + 1 for q in CH[:i + 1])
        SCANS = sum(len(c["dirs"]) for c in CH)
        PER_DA, PER_DBX = CH[-1]["a_done"], CH[-1]["u_done"]

        A_TILES = ["gm", "gd", "f1_0", "f1_1", "f1_2", "f1_3", "f2", "f3", "x23", "p2"]
        P_TILES = ["xd1f", "p1f_0", "p1f_1", "p1f_2", "p1f_3", "z_0", "z_1", "z_2", "z_3",
                   "xd1b", "p1b_0", "p1b_1", "p1b_2", "p1b_3"]
        Z_TILES = ["n3", "n2", "nf_0", "nf_1", "nf_2", "nf_3", "nb_0", "nb_1", "nb_2", "nb_3"] + [f"out_{j}" for j in range(8)]
        PIECES = {"x23": 0, "p2": 1} | {f"p1f_{i}": 2 + i for i in range(4)} | {f"p1b_{i}": 6 + i for i in range(4)}
        NPC = len(PIECES)

        const_in = sem("const_in")
        const_set = sem("const_set")
        expA = sem("expA")
        bias_step = sem("bias_step")
        comp_full = sem("comp_full")
        x_arrived = sem("x_arrived")
        res_in = [sem(f"res_in{i}") for i in range(2)]
        stored = [sem(f"stored{i}") for i in range(2)]
        gn_step = sem("gn_step")
        gn_rstd = sem("gn_rstd")
        xn_done = sem("xn_done")
        a_full, p_full, z_full = sem("a_full"), sem("p_full"), sem("z_full")
        a_act, p_act, z_act = sem("a_act"), sem("p_act"), sem("z_act")
        a_dve, z_dve = sem("a_dve"), sem("z_dve")
        sp_exp = sem("sp_exp")
        sp_ln = sem("sp_ln")
        sp_step = sem("sp_step")
        delta_done = sem("delta_done")
        dx_done = sem("dx_done")
        silu_done = sem("silu_done")
        bb_full = sem("bb_full")
        bsb_full = sem("bsb_full")
        cb_full = sem("cb_full")
        da_full = sem("da_full")
        dbx_full = sem("dbx_full")
        xdv_full = sem("xdv_full")
        scan_done = sem("scan_done")
        hc_full = sem("hc_full")
        tr_done = sem("tr_done")
        ln_st = sem("ln_st")
        ln_mv = sem("ln_mv")
        ln_ve = sem("ln_ve")
        ln_r = sem("ln_r")
        ln_done = sem("ln_done")
        up2_done = sem("up2_done")
        up1_done = sem("up1_done")
        gate_done = sem("gate_done")
        held = {e: sem(f"held_{e}") for e in ("pe", "dve", "pool", "act")}

        def hold(engine, name):
            engine.sem_inc(held[name], 1)

        def wait(engine, s, per, b, k):
            if isinstance(b, int):
                if b * per + k > 0:
                    engine.wait_ge(s, b * per + k)
            else:
                engine.wait_ge(s, b * per + k)

        FAM = {"a": (A_TILES, a_full, {"gm": "dve", "gd": "dve"}, a_act, a_dve),
               "p": (P_TILES, p_full, {}, p_act, None),
               "z": (Z_TILES, z_full, {t: "dve" for t in Z_TILES[6:]}, z_act, z_dve)}

        def family(t):
            return next(v for v in FAM.values() if t in v[0])

        def wait_full(engine, b, t):
            tiles, full, _, _, _ = family(t)
            wait(engine, full, len(tiles), b, tiles.index(t) + 1)

        def wait_empty(engine, b, t):
            tiles, _, by, s_act, s_dve = family(t)
            who = by.get(t, "act")
            mine = [q for q in tiles if by.get(q, "act") == who]
            wait(engine, s_act if who == "act" else s_dve, len(mine), b, mine.index(t) + 1)

        def full_sem(t):
            return family(t)[1]

        def empty_sem(t):
            _, _, by, s_act, s_dve = family(t)
            return s_act if by.get(t, "act") == "act" else s_dve

        def wait_slot(engine, b, it):
            if it >= NU:
                wait(engine, tr_done, ITEMS, b, it - NU + 1)
            else:
                before = max(j for j in range(ITEMS) if j % NU == it)
                wait(engine, tr_done, ITEMS, b, before + 1 - ITEMS)

        def seg(buf, ns, L):
            return buf[:, 0:ns * NH * (L + 1)].rearrange("p (n h l) -> p n h l", h=NH, l=L + 1)

        def piece(t):
            if t == "x23":
                return "3", [(3 * 2 * N + h * L3, h, 0, L3) for h in range(NH)]
            if t == "p2":
                return "2", [(h * L2, h, 0, L2) for h in range(NH)]
            i = int(t[-1])
            return t[1:3], [(0, i // 2, (i % 2) * BANK, BANK)]

        def fillers(z_before, a_next):
            at = {c: [] for c in range(NCH)}
            if z_before:
                at[0] += ["nb_0", "nb_1", "nb_2", "nb_3"]
                at[3] += ["out_0", "out_1", "out_2", "out_3"]
                at[4] += ["out_4", "out_5", "out_6", "out_7"]
            at[1] += ["xd1f", "p1f_0", "p1f_1"]
            at[2] += ["p1f_2", "p1f_3"]
            at[5] += ["n3", "n2"]
            for i in range(4):
                at[6 + i] += [f"z_{i}"]
                at[11 + i] += [f"p1b_{i}"]
            at[10] += ["xd1b"]
            if a_next:
                at[15] += ["gm"]
                at[16] += ["gd"]
                for i in range(4):
                    at[21 + 2 * i] += [f"f1_{i}/0"]
                    at[22 + 2 * i] += [f"f1_{i}/1"]
                at[29] += ["f2/0"]
                at[30] += ["f2/1"]
                at[31] += ["f3"]
                at[32] += ["x23"]
                at[33] += ["p2"]
            for i in range(4):
                at[(22, 24, 26, 28)[i]] += [f"nf_{i}"]
            return at

        OFFSET = {t: 1 for t in A_TILES} | {t: 0 for t in P_TILES} | {t: 0 for t in Z_TILES[:6]} | {t: -1 for t in Z_TILES[6:]}

        def emptied_by(who, at, c):
            out = []
            for t in at.get(c, []):
                name, _, part = t.partition("/")
                if part != "0" and (family(name)[2].get(name, "act") == who):
                    out.append(name)
            return out

        def program(engine, prologue, body, epilogue):
            prologue()
            body(0, False, batches > 1)
            if batches > 2:
                with engine.Fori(1, batches - 1) as b:
                    body(b, True, True)
            if batches > 1:
                body(batches - 1, True, False)
            epilogue()

        block = ctx.enter_context(nc.Block())

        @block.sync
        def _(sp):
            for dst, src in ((nat, nat_dram), (low, low_dram), (W[:], w_dram), (ident[:], ident_dram), (group[:], group_dram)):
                sp.dma_start(dst, src).then_inc(const_in, 16)

            def load_x(b):
                sp.dma_start(xin[:], x_in[bass.ds(b, 1)].rearrange("a (k p) l -> p (a k) l", p=P)).then_inc(x_arrived, 16)

            def tile_of(x, b, j):
                return x[bass.ds(b, 1), (j // 2) * P:(j // 2 + 1) * P, (j % 2) * BANK:(j % 2 + 1) * BANK].rearrange("a p l -> (a p) l")

            def load_res(b, j):
                wait(sp, stored[j % 2], 64, b, 16 * (j // 2))
                sp.dma_start(xres[:, j % 2, :], tile_of(x_in, b, j)).then_inc(res_in[j % 2], 16)

            def results(b):
                load_res(b, 0)
                load_res(b, 1)
                for j in range(8):
                    wait_empty(sp, b, f"out_{j}")
                    sp.dma_start(tile_of(x_out, b, j), xres[:, j % 2, :]).then_inc(stored[j % 2], 16)
                    if j < 6:
                        load_res(b, j + 2)

            def body(b, z_before, a_next):
                if z_before:
                    results(b - 1)
                if a_next:
                    wait_full(sp, b, "z_3")
                    load_x(b + 1)

            program(sp, lambda: load_x(0), body, lambda: results(batches - 1))
            for i in range(2):
                sp.wait_ge(stored[i], batches * 64)

        @block.tensor
        def _(pe):
            mm = nc.tensor.matmul
            pe.wait_ge(const_in, 80)
            for ic in range(KC):
                for k in range(NH):
                    mm(bk(ic, D), nat[:, k, ic * P:(ic + 1) * P], nat[:, k, C:C + D], start=(k == 0), stop=(k == NH - 1))
            for s in range(3):
                for k in range(NH):
                    mm(bk(4 + s)[:, k * D:(k + 1) * D], low[:, 0, s, k * P:(k + 1) * P], low[:, 1, s, :], start=True, stop=True)
            for m in range(NH):
                for k in range(NH):
                    last = mm(bk(7)[:, m:m + 1], nat[:, k, C + m * P:C + (m + 1) * P], w("in_b")[:, k:k + 1],
                              start=(k == 0), stop=(k == NH - 1))
            last.then_inc(comp_full, 1)
            pe.wait_ge(const_set, 4)

            before = {}

            def tile(b, t, bi=BANK_T):
                name, _, part = t.partition("/")
                tb = b + OFFSET[name]
                if part in ("", "0"):
                    if before.get(bi) is not None:
                        wait_empty(pe, *before[bi])
                    before[bi] = (tb, name)
                    needs(tb, name)
                ps = bk(bi)
                last = None
                kind = name.split("_")[0]
                i = int(name.split("_")[1]) if "_" in name else 0
                h, q = i // 2, i % 2
                if name == "gm":
                    last = mm(ps[:, 0:2 * KC], group[:], gmv[:].rearrange("p k s -> p (k s)"), start=True, stop=True)
                elif name == "gd":
                    last = mm(ps[:, 0:KC], group[:], gd2[:], start=True, stop=True)
                elif kind in ("f1", "z"):
                    ks = {"": range(KC), "0": range(0, 2), "1": range(2, KC)}[part]
                    wt = wc if kind == "f1" else inz
                    for k in ks:
                        last = mm(ps, wt[:, k, h * P:(h + 1) * P], xin[:, k, q * BANK:(q + 1) * BANK],
                                  start=(k == 0), stop=(k == KC - 1))
                elif kind in ("f2", "f3"):
                    src, wT, width = (f1, c2T, 32) if kind == "f2" else (f2, c3T, 16)
                    half = width // 2
                    for m in {"": range(NH), "0": range(1), "1": range(1, NH)}[part]:
                        j = 0
                        for k in range(NH):
                            v = src[:, k, :].rearrange("p (h y w x) -> p y x h w", y=2, x=2, w=half)
                            for tap in range(4):
                                last = mm(ps[:, m * half * half:(m + 1) * half * half].rearrange("p (h w) -> p h w", w=half),
                                          wT[:, k, tap, m * P:(m + 1) * P], v[:, tap // 2, tap % 2], start=(j == 0), stop=(j == 7))
                                j += 1
                elif name == "x23":
                    for k in range(NH):
                        mm(ps[0:L3, 0:2 * N], f3[:, k, :], xwT["3"][:, k, :], start=(k == 0), stop=(k == NH - 1))
                    for lb in range(2):
                        for k in range(NH):
                            mm(ps[:, (1 + lb) * 2 * N:(2 + lb) * 2 * N], f2[:, k, lb * P:(lb + 1) * P], xwT["2"][:, k, :],
                               start=(k == 0), stop=(k == NH - 1))
                    for m in range(NH):
                        for k in range(NH):
                            last = mm(ps[:, 3 * 2 * N + m * L3:3 * 2 * N + (m + 1) * L3], wd[:, 2, k, m * P:(m + 1) * P], f3[:, k, :],
                                      start=(k == 0), stop=(k == NH - 1))
                elif name == "p2":
                    for m in range(NH):
                        for k in range(NH):
                            last = mm(ps[:, m * L2:(m + 1) * L2], wd[:, 1, k, m * P:(m + 1) * P], f2[:, k, :],
                                      start=(k == 0), stop=(k == NH - 1))
                elif kind in ("xd1f", "xd1b"):
                    s = "1" if kind == "xd1f" else "2"
                    for lb in range(NB):
                        for k in range(NH):
                            last = mm(ps[:, lb * 2 * N:(lb + 1) * 2 * N], f1[:, k, lb * P:(lb + 1) * P], xwT[s][:, k, :],
                                      start=(k == 0), stop=(k == NH - 1))
                elif kind in ("p1f", "p1b"):
                    for k in range(NH):
                        last = mm(ps, wd[:, 0 if kind == "p1f" else 1, k, h * P:(h + 1) * P], f1[:, k, q * BANK:(q + 1) * BANK],
                                  start=(k == 0), stop=(k == NH - 1))
                elif name in ("n3", "n2"):
                    L, key = (L3, "3") if name == "n3" else (L2, "2")
                    rows, nlb = min(L, P), max(1, L // P)
                    if name == "n3":
                        hold(pe, "pe")
                    for m in range(NH):
                        for lb in range(nlb):
                            for d in range(2):
                                last = mm(ps[:, m * L + lb * rows:m * L + (lb + 1) * rows],
                                          hn[key][0:rows, d * nlb + lb, m * P:(m + 1) * P], ident[0:rows, 0:rows],
                                          start=(m == 0 and lb == 0 and d == 0),
                                          stop=(m == NH - 1 and lb == nlb - 1 and d == 1), is_transpose=True)
                elif kind in ("nf", "nb"):
                    for j in range(4):
                        last = mm(ps[:, j * P:(j + 1) * P], hn_buf[:, 4 * q + j, h * P:(h + 1) * P], ident[:],
                                  start=(j == 0), stop=(j == 3), is_transpose=True)
                elif kind == "out":
                    for k in range(NH):
                        last = mm(ps, outT[:, k, h * P:(h + 1) * P], out1[:, k, q * BANK:(q + 1) * BANK],
                                  start=(k == 0), stop=(k == NH - 1))
                if part in ("", "1"):
                    last.then_inc(full_sem(name), 1)

            def needs(tb, name):
                kind = name.split("_")[0]
                if name == "gm":
                    wait(pe, gn_step, 15, tb, 12)
                elif name == "gd":
                    wait(pe, gn_step, 15, tb, 14)
                elif kind == "f1":
                    wait(pe, xn_done, KC, tb, KC)
                elif name == "f2":
                    wait_empty(pe, tb, "f1_3")
                elif name == "f3":
                    wait_empty(pe, tb, "f2")
                elif name == "x23":
                    wait_empty(pe, tb, "f3")
                elif name in ("n3", "n2"):
                    wait(pe, ln_done, 4, tb, 2)
                elif kind == "nf":
                    wait(pe, ln_done, 4, tb, 3)
                elif kind == "nb":
                    wait(pe, ln_done, 4, tb, 4)
                elif kind == "out":
                    wait(pe, gate_done, 4, tb, 3 + int(name[-1]) % 2)

            def broadcast(c, bi, col, halves):
                key, L = c["key"], c["L"]
                rows = min(L, P)
                if rows < P:
                    hold(pe, "pe")
                for hf in halves:
                    for o in range(0, BANK, rows):
                        at = hf * BANK + o
                        i, lb = at // L, (at % L) // rows
                        src = bct[key][0:rows, lb, col + c["n0"] + i:col + c["n0"] + i + 1].broadcast_to([rows, P])
                        oo = bi * BANK + (at if len(halves) == 2 else o)
                        last = mm(bank[:, oo:oo + rows], src, ident[0:rows, 0:rows],
                                  start=(o == 0), stop=(o == BANK - rows), is_transpose=True)
                return last

            def b_half(b, ci, hf):
                c = CH[ci]
                if hf == 0 and ci == FIRST[c["pi"]]:
                    wait_empty(pe, b, {"3": "x23", "2": "x23", "1f": "xd1f", "1b": "xd1b"}[c["key"]])
                wait(pe, bsb_full, 2 * NCH, b, 2 * ci + hf)
                broadcast(c, BANK_B, 0, [hf]).then_inc(bb_full, 1)

            def add_item(src, pi, d, first, final):
                L = PASSES[pi][2]
                rows, nlb = min(L, P), max(1, L // P)
                for i in range(src.shape[1]):
                    for h in range(NH):
                        for lb in range(nlb):
                            if L == L1:
                                bi, col = lb // 2, (lb % 2) * D
                            elif L == L2:
                                bi, col = int(d == "b"), lb * D
                            else:
                                bi, col = 2, int(d == "b") * D
                            one_bank = L == L3
                            st = first and i == 0 and h == 0 and col == 0
                            en = final and i == src.shape[1] - 1 and h == NH - 1 and (
                                (L == L1 and lb % 2 == 1) or (L == L2 and lb == nlb - 1) or (one_bank and d == "b"))
                            o = bi * BANK + col + h * P
                            last = mm(bank[0:rows, o:o + P], src[:, i, h, 1 + lb * rows:1 + (lb + 1) * rows], ident[:, :],
                                      start=st, stop=en, is_transpose=True)
                return last

            def items(b, ci):
                c = CH[ci]
                for j, d in enumerate(c["dirs"]):
                    wait(pe, hc_full, SCANS, b, c["scan0"] + j + 1)
                    if c["L"] == L3:
                        hold(pe, "pe")
                    add_item(seg(u_ring[:, (c["item"] + j) % NU, :], c["ns"], c["L"]), c["pi"], d, False,
                             c["n0"] + c["ns"] == N).then_inc(tr_done, 1)

            def skip_item(b, pi):
                wait(pe, xdv_full, 8, b, 2 * (pi + 1))
                wait(pe, ln_done, 4, b, pi)
                if pi == 2 and before.get(BANK_X) is not None:
                    wait_empty(pe, *before[BANK_X])
                    before[BANK_X] = None
                if pi == 0:
                    hold(pe, "pe")
                L, dirs = PASSES[pi][2], PASSES[pi][3]
                for d in dirs:
                    last = add_item(seg(u_ring[:, VITEM[pi] % NU, :], 1, L), pi, d, d == "f" or L != L3 or len(dirs) == 1, False)
                last.then_inc(tr_done, 1)

            def body(b, z_before, a_next):
                before.clear()
                before[BANK_T] = (b, "p2")
                at = fillers(z_before, a_next)
                for ci in range(2):
                    for hf in range(2):
                        b_half(b, ci, hf)
                for ci in range(NCH):
                    if ci + 2 < NCH:
                        b_half(b, ci + 2, 0)
                    wait(pe, hc_full, SCANS, b, CH[ci]["scan0"])
                    broadcast(CH[ci], BANK_C, N, [0, 1]).then_inc(cb_full, 1)
                    if ci:
                        items(b, ci - 1)
                    if ci in FIRST:
                        skip_item(b, CH[ci]["pi"])
                    if ci + 2 < NCH:
                        b_half(b, ci + 2, 1)
                    for j, t in enumerate(at[ci]):
                        tile(b, t, BANK_X if t[:2] in ("nb", "ou") and j % 2 else BANK_T)
                items(b, NCH - 1)

            def prologue():
                for t in A_TILES:
                    tile(-1, t)

            def epilogue():
                before.clear()
                for t in ["nb_0", "nb_1", "nb_2", "nb_3"] + [f"out_{j}" for j in range(8)]:
                    tile(batches, t, BANK_X if int(t[-1]) % 2 else BANK_T)

            program(pe, prologue, body, epilogue)

        @block.scalar
        def _(act):
            A = nc.scalar.activation
            act.wait_ge(const_in, 80)
            a0 = W_COLS["Al1"][0]
            A(negA[:], W[:, a0:a0 + 3 * NH * N], ACT.Exp).then_inc(expA, 1)
            act.wait_ge(const_set, 4)

            def softplus(b, t):
                key, parts = piece(t)
                s = {"3": "3", "2": "2", "1f": "1", "1b": "2"}[key]
                k = PIECES[t]
                j = k % 2
                wait(act, delta_done, NPC, b, k - 1)
                n = 0
                for col, h, _, m in parts:
                    bias = w(f"dtb{s}")[:, h:h + 1]
                    A(T_u[:, j, n:n + m], bk(BANK_T)[:, col:col + m], ACT.Abs, bias=bias)
                    last = A(T_r[:, j, n:n + m], bk(BANK_T)[:, col:col + m], ACT.Relu, bias=bias)
                    n += m
                last.then_inc(empty_sem(t), 1)
                wait_empty(act, b, t)
                A(T_u[:, j, 0:n], T_u[:, j, 0:n], ACT.Exp, scale=-1.0).then_inc(sp_exp, 1)
                wait(act, sp_exp, NPC, b, k + 1)
                A(T_ln[:, j, 0:n], T_u[:, j, 0:n], ACT.Ln, bias=1.0).then_inc(sp_ln, 1)

            def empty(b, name):
                wait_full(act, b, name)
                kind = name.split("_")[0]
                i = int(name.split("_")[1]) if "_" in name else 0
                h, q = i // 2, i % 2
                ps = bk(BANK_T)
                if name == "f1_0":
                    wait(act, dx_done, NPC, b, 0)
                if name == "z_0":
                    wait(act, gate_done, 4, b, 0)
                if kind == "f1":
                    A(f1[:, h, q * BANK:(q + 1) * BANK], ps, ACT.Identity, bias=f1_b[:, h:h + 1]).then_inc(a_act, 1)
                elif kind == "z":
                    A(z[:, h, q * BANK:(q + 1) * BANK], ps, ACT.Identity, bias=w("in_b")[:, NH + h:NH + h + 1]).then_inc(p_act, 1)
                    if i == 3:
                        wait_empty(act, b, name)
                        A(z[:].rearrange("p h l -> p (h l)"), z[:].rearrange("p h l -> p (h l)"), ACT.Silu).then_inc(silu_done, 1)
                elif kind in ("f2", "f3"):
                    dst, L, bias = (f2, L2, w("c2_b")) if kind == "f2" else (f3, L3, w("c3_b"))
                    for m in range(NH):
                        last = A(dst[:, m, :], ps[:, m * L:(m + 1) * L], ACT.Identity, bias=bias[:, m:m + 1])
                    last.then_inc(a_act, 1)
                elif name == "x23":
                    A(bct["3"][0:L3, 0, :], ps[0:L3, 0:2 * N], ACT.Copy)
                    A(bct["2"][:].rearrange("p a n -> p (a n)"), ps[:, 2 * N:6 * N], ACT.Copy)
                    softplus(b, name)
                elif kind in ("xd1f", "xd1b"):
                    A(bct[kind[2:]][:].rearrange("p a n -> p (a n)"), ps[:, 0:NB * 2 * N], ACT.Copy).then_inc(p_act, 1)
                elif kind in ("p2", "p1f", "p1b"):
                    softplus(b, name)
                elif name == "n3":
                    wait(act, up2_done, 1, b, 0)
                    for m in range(NH):
                        last = A(y3s[:, m, :], ps[:, m * L3:(m + 1) * L3], ACT.Identity, scale=w("g3")[:, m:m + 1], bias=bt[:, m:m + 1])
                    last.then_inc(z_act, 1)
                elif name == "n2":
                    wait(act, up1_done, 4, b, 0)
                    for m in range(NH):
                        last = A(y2s[:, m, :], ps[:, m * L2:(m + 1) * L2], ACT.Copy, scale=w("g2")[:, m:m + 1])
                    last.then_inc(z_act, 1)
                elif kind == "nf":
                    A(out1[:, h, q * BANK:(q + 1) * BANK], ps, ACT.Copy, scale=w("g1")[:, h:h + 1]).then_inc(z_act, 1)

            def copy_b(b, ci):
                for hf in range(2):
                    wait(act, bb_full, 2 * NCH, b, 2 * ci + hf + 1)
                    if hf == 0:
                        wait(act, dbx_full, PER_DBX, b, CH[ci - 2]["u_done"] if ci >= 2 else 0)
                    A(b_sb[:, ci % 2, hf * BANK:(hf + 1) * BANK], bk(BANK_B), ACT.Copy).then_inc(bsb_full, 1)

            def decays(b, ci):
                c = CH[ci]
                wait(act, delta_done, NPC, b, {"3": 1, "2": 2, "1f": 6, "1b": 10}[c["key"]])
                wait(act, scan_done, SCANS, b, CH[ci - NA]["scan0"] + len(CH[ci - NA]["dirs"]) if ci >= NA else 0)
                slot = seg(dA_ring[:, ci % NA, :], c["ns"], c["L"])
                if c["pad_a"]:
                    A(slot[:, :, :, 0], zero[:, 0:c["ns"] * NH].rearrange("p (n h) -> p n h", h=NH), ACT.Copy).then_inc(da_full, 1)
                for i in range(c["ns"]):
                    for h in range(NH):
                        col = (int(c["wset"]) - 1) * NH * N + h * N + c["n0"] + i
                        A(slot[:, i, h, 1:], delta[c["key"]][:, h, :], ACT.Exp, scale=negA[:, col:col + 1]).then_inc(da_full, 1)

            def body(b, z_before, a_next):
                at = fillers(z_before, a_next)
                copy_b(b, 0)
                for ci in range(NCH):
                    if ci in FIRST:
                        pi = CH[ci]["pi"]
                        _, f, L, _, s = PASSES[pi]
                        wait_slot(act, b, VITEM[pi])
                        for h in range(NH):
                            A(seg(u_ring[:, VITEM[pi] % NU, :], 1, L)[:, 0, h, 1:], f[:, h, :], ACT.Copy,
                              scale=w(f"Dv{s}")[:, h:h + 1]).then_inc(xdv_full, 1)
                    decays(b, ci)
                    if ci + 1 < NCH:
                        copy_b(b, ci + 1)
                    for t in emptied_by("act", at, ci - 1):
                        empty(b + OFFSET[t], t)
                for t in emptied_by("act", at, NCH - 1):
                    empty(b + OFFSET[t], t)

            def prologue():
                for t in A_TILES[2:]:
                    empty(0, t)

            program(act, prologue, body, lambda: None)

        @block.gpsimd
        def _(pool):
            G = nc.gpsimd
            G.memset(mhalf[:], -0.5).then_inc(const_set, 1)
            pool.wait_ge(const_set, 4)

            def group_rstd(b):
                wait(pool, gn_step, 15, b, 15)
                G.tensor_tensor(gr[:], gve[:], mhalf[:, 0:KC], ALU.pow).then_inc(gn_rstd, 1)

            def norm_rstd(b, pi):
                wait(pool, ln_ve, 4, b, pi + 1)
                rows, nb = min(PASSES[pi][2], P), LN_BLOCKS[pi]
                G.tensor_tensor(lr[0:rows, 0:nb], lve[0:rows, 0:nb], mhalf[0:rows, 0:nb], ALU.pow).then_inc(ln_r, 1)

            def step_sizes(b, t):
                key, parts = piece(t)
                f = {"3": f3, "2": f2}.get(key, f1)
                k = PIECES[t]
                j = k % 2
                wait(pool, sp_step, 4 * NPC, b, 4 * k + 4)
                h, p0 = parts[0][1], parts[0][2]
                if len(parts) == 2:
                    view = lambda a: a[:]
                    tv = lambda a: a[:, j, 0:NH * parts[0][3]].rearrange("p (h l) -> p h l", h=NH)
                else:
                    view = lambda a: a[:, h, p0:p0 + BANK]
                    tv = lambda a: a[:, j, :]
                G.tensor_tensor(view(delta[key]), tv(T_ln), tv(T_r), ALU.add).then_inc(delta_done, 1)
                wait(pool, delta_done, NPC, b, k + 1)
                G.tensor_tensor(view(dx[key]), view(delta[key]), view(f), ALU.mult).then_inc(dx_done, 1)

            def inputs(b, ci):
                c = CH[ci]
                key, L, ns = c["key"], c["L"], c["ns"]
                wait(pool, dx_done, NPC, b, {"3": 1, "2": 2, "1f": 6, "1b": 10}[key])
                wait_slot(pool, b, c["in_item"])
                slot = seg(u_ring[:, c["in_item"] % NU, :], ns, L)
                if c["pad_u"]:
                    hold(pool, "pool")
                    G.memset(slot[:, :, :, 0], 0.0).then_inc(dbx_full, 1)
                wait(pool, bsb_full, 2 * NCH, b, 2 * ci + 2)
                shape = [P, ns, NH, L]
                G.tensor_tensor(slot[:, :, :, 1:], dx[key][:].unsqueeze(1).broadcast_to(shape),
                                b_sb[:, ci % 2, :].rearrange("p (n l) -> p n l", l=L).unsqueeze(2).broadcast_to(shape),
                                ALU.mult).then_inc(dbx_full, 1)

            def enlarge(dst, src, width, y0, y1):
                for dy in range(2):
                    v = dst.rearrange("p (h y w x) -> p h y w x", y=2, x=2, w=width)[:, y0:y1, dy]
                    s_ = src.rearrange("p (h w) -> p h w", w=width)[:, y0:y1]
                    last = G.tensor_tensor(v, v, s_.unsqueeze(3).broadcast_to([P, y1 - y0, width, 2]), ALU.add)
                return last

            def add_level2(b):
                wait(pool, up2_done, 1, b, 1)
                for i in range(4):
                    h, q = i // 2, i % 2
                    wait_empty(pool, b, f"nb_{i}")
                    enlarge(out1[:, h, :], y2s[:, h, :], 16, 8 * q, 8 * q + 8).then_inc(up1_done, 1)

            def gate(b):
                wait(pool, silu_done, 1, b, 1)
                for j, i in enumerate((0, 2, 1, 3)):
                    h, q = i // 2, i % 2
                    wait(pool, up1_done, 4, b, 4)
                    o = out1[:, h, q * BANK:(q + 1) * BANK]
                    G.tensor_tensor(o, o, z[:, h, q * BANK:(q + 1) * BANK], ALU.mult).then_inc(gate_done, 1)

            def body(b, z_before, a_next):
                for ci in range(NCH):
                    inputs(b, ci)
                    if ci == 0 and z_before:
                        norm_rstd(b - 1, 3)
                    if ci in FIRST[1:]:
                        norm_rstd(b, CH[ci]["pi"] - 1)
                    if ci == 1 and z_before:
                        add_level2(b - 1)
                    if ci == 2 and z_before:
                        gate(b - 1)
                    if ci in (3, 4):
                        for i in range(2):
                            step_sizes(b, f"p1f_{2 * (ci - 3) + i}")
                    if ci == 8:
                        wait_empty(pool, b, "n2")
                        for h in range(NH):
                            last = enlarge(y2s[:, h, :], y3s[:, h, :], 8, 0, 8)
                        last.then_inc(up2_done, 1)
                    if 14 <= ci <= 17:
                        step_sizes(b, f"p1b_{ci - 14}")
                    if a_next:
                        if ci == 18:
                            group_rstd(b + 1)
                        if ci == 35:
                            step_sizes(b + 1, "x23")
                        if ci == 36:
                            step_sizes(b + 1, "p2")

            def prologue():
                group_rstd(0)
                step_sizes(0, "x23")
                step_sizes(0, "p2")

            def epilogue():
                norm_rstd(batches - 1, 3)
                add_level2(batches - 1)
                gate(batches - 1)

            program(pool, prologue, body, epilogue)

        @block.vector
        def _(dve):
            V = nc.vector
            V.memset(zero[:], 0.0).then_inc(const_set, 1)
            dve.wait_ge(const_in, 80)
            dve.wait_ge(comp_full, 1)
            for k in range(KC):
                V.tensor_copy(wc[:, k, :], bk(k, D))
            for s in range(3):
                V.tensor_copy(wd[:, s].rearrange("p k o -> p (k o)"), bk(4 + s))
            V.tensor_tensor(f1_b[:], bk(7)[:, 0:NH], w("c1_b"), ALU.add)
            dve.wait_ge(expA, 1)
            V.tensor_scalar(negA[:], negA[:], -1.0, None, ALU.mult).then_inc(const_set, 1)
            t_ = [bt[:, NH * i:NH * i + NH] for i in range(4)]
            V.tensor_scalar(t_[1], w("be2"), 3.0, None, ALU.mult).then_inc(bias_step, 1)
            V.tensor_scalar(t_[2], w("be3"), 2.0, None, ALU.mult).then_inc(bias_step, 1)
            dve.wait_ge(bias_step, 2)
            V.tensor_tensor(t_[3], t_[1], t_[2], ALU.add).then_inc(bias_step, 1)
            dve.wait_ge(bias_step, 3)
            V.tensor_tensor(t_[0], t_[3], w("be1"), ALU.add).then_inc(const_set, 1)

            def group_stats(b, k):
                wait(dve, x_arrived, 16, b, 16)
                for q in range(2):
                    V.bn_stats(gst[:, k, 6 * q:6 * q + 6], xin[:, k, q * BANK:(q + 1) * BANK]).then_inc(gn_step, 1)

            def group_aggregate(b):
                wait(dve, gn_step, 15, b, 8)
                hold(dve, "dve")
                for k in range(KC):
                    V.bn_aggr(gmv[:, k, :], gst[:, k, :]).then_inc(gn_step, 1)

            def group_mean(b):
                wait_full(dve, b, "gm")
                V.tensor_copy(ggm[:].rearrange("p k s -> p (k s)"), bk(BANK_T)[:, 0:2 * KC]).then_inc(a_dve, 1)
                wait_empty(dve, b, "gm")
                V.tensor_tensor(gd[:], gmv[:, :, 0], ggm[:, :, 0], ALU.subtract).then_inc(gn_step, 1)
                wait(dve, gn_step, 15, b, 13)
                V.tensor_tensor(gd2[:], gd[:], gd[:], ALU.mult).then_inc(gn_step, 1)

            def group_var(b):
                wait_full(dve, b, "gd")
                V.tensor_tensor(gve[:], bk(BANK_T)[:, 0:KC], ggm[:, :, 1], ALU.add).then_inc(a_dve, 1)
                wait_empty(dve, b, "gd")
                V.tensor_scalar(gve[:], gve[:], EPS, None, ALU.add).then_inc(gn_step, 1)

            def normalise(b, k):
                wait(dve, gn_rstd, 1, b, 1)
                V.tensor_scalar(xin[:, k, :], xin[:, k, :], ggm[:, k, 0:1], gr[:, k:k + 1],
                                ALU.subtract, ALU.mult).then_inc(xn_done, 1)

            def log1p(b, t):
                _, parts = piece(t)
                n = sum(p_[3] for p_ in parts)
                k = PIECES[t]
                j = k % 2
                wait(dve, sp_exp, NPC, b, k + 1)
                V.tensor_scalar(T_c[:, 0:n], T_u[:, j, 0:n], 1.0, 1.0, ALU.add, ALU.subtract).then_inc(sp_step, 1)
                wait(dve, sp_step, 4 * NPC, b, 4 * k + 1)
                V.tensor_tensor(T_c[:, 0:n], T_u[:, j, 0:n], T_c[:, 0:n], ALU.subtract).then_inc(sp_step, 1)
                wait(dve, sp_step, 4 * NPC, b, 4 * k + 2)
                wait(dve, sp_ln, NPC, b, k + 1)
                V.tensor_tensor(T_ln[:, j, 0:n], T_ln[:, j, 0:n], T_c[:, 0:n], ALU.add).then_inc(sp_step, 1)
                wait(dve, sp_step, 4 * NPC, b, 4 * k + 3)
                V.tensor_tensor(T_ln[:, j, 0:n], T_ln[:, j, 0:n], T_u[:, j, 0:n], ALU.min).then_inc(sp_step, 1)

            def layer_norm(b, pi):
                key, _, L, dirs, _ = PASSES[pi]
                rows = min(L, P)
                nb, at = LN_BLOCKS[pi], sum(LN_BLOCKS[:pi])
                total = sum(LN_BLOCKS)
                first = 2 * BANK if L == L3 else 0
                blocks = [bank[0:rows, first + j * D:first + (j + 1) * D] for j in range(nb)]
                wait(dve, tr_done, ITEMS, b, END[pi])
                for j in range(nb):
                    V.bn_stats(lst[0:rows, j, :], blocks[j]).then_inc(ln_st, 1)
                wait(dve, ln_st, total, b, at + nb)
                hold(dve, "dve")
                for j in range(nb):
                    V.bn_aggr(lmv[0:rows, j, :], lst[0:rows, j, :]).then_inc(ln_mv, 1)
                wait(dve, ln_mv, total, b, at + nb)
                V.tensor_scalar(lve[0:rows, 0:nb], lmv[0:rows, 0:nb, 1], EPS, None, ALU.add).then_inc(ln_ve, 1)
                wait(dve, ln_r, 4, b, pi + 1)
                if pi == 3:
                    wait_full(dve, b, "nf_3")
                for j in range(nb):
                    last = V.tensor_scalar(hn[key][0:rows, j, :], blocks[j], lmv[0:rows, j, 0:1], lr[0:rows, j:j + 1],
                                           ALU.subtract, ALU.mult)
                last.then_inc(ln_done, 1)

            def empty(b, name, bi):
                wait_full(dve, b, name)
                j = int(name[-1])
                h, q = j // 2, j % 2
                if name == "gm":
                    group_mean(b)
                if name[:2] == "nb":
                    wait_empty(dve, b, "nf_3")
                    o = out1[:, h, q * BANK:(q + 1) * BANK]
                    V.scalar_tensor_tensor(o, bk(bi), w("g2")[:, h:h + 1], o, ALU.mult, ALU.add).then_inc(z_dve, 1)
                else:
                    wait(dve, res_in[j % 2], 64, b, 16 * (j // 2) + 16)
                    o = xres[:, j % 2, :]
                    V.scalar_tensor_tensor(o, bk(bi), w("out_b")[:, h:h + 1], o, ALU.add, ALU.add).then_inc(z_dve, 1)

            def scan(b, ci):
                c = CH[ci]
                n = c["ns"] * NH * (c["L"] + 1)
                a = dA_ring[:, ci % NA, 0:n]
                src = u_ring[:, c["in_item"] % NU, 0:n]
                wait(dve, da_full, PER_DA, b, c["a_done"])
                wait(dve, dbx_full, PER_DBX, b, c["u_done"])
                for j, d in enumerate(c["dirs"]):
                    dst = u_ring[:, (c["item"] + j) % NU, 0:n]
                    if len(c["dirs"]) == 2:
                        if j == 0:
                            wait_slot(dve, b, c["item"])
                        else:
                            wait(dve, scan_done, SCANS, b, c["scan0"] + 1)
                    if d == "f":
                        V.tensor_tensor_scan(dst, a, src, 0.0, ALU.mult, ALU.add).then_inc(scan_done, 1)
                    else:
                        V.tensor_tensor_scan(dst[:, ::-1], a[:, ::-1], src[:, ::-1], 0.0, ALU.mult, ALU.add).then_inc(scan_done, 1)

            def times_c(b, ci):
                c = CH[ci]
                wait(dve, cb_full, NCH, b, ci + 1)
                for j in range(len(c["dirs"])):
                    wait(dve, scan_done, SCANS, b, c["scan0"] + j + 1)
                    v = seg(u_ring[:, (c["item"] + j) % NU, :], c["ns"], c["L"])[:, :, :, 1:]
                    cc = bank[:, BANK_C * BANK:(BANK_C + 2) * BANK].rearrange("p (n l) -> p n l", l=c["L"])
                    V.tensor_tensor(v, v, cc.unsqueeze(2).broadcast_to([P, c["ns"], NH, c["L"]]), ALU.mult).then_inc(hc_full, 1)

            def body(b, z_before, a_next):
                at = fillers(z_before, a_next)
                for ci in range(NCH):
                    mine = [(t, BANK_X if j % 2 else BANK_T) for j, t in enumerate(emptied_by("dve", at, ci)) if t[:2] in ("nb", "ou")]
                    scan(b, ci)
                    for t, bi in (mine[:2] if ci else []):
                        empty(b - 1, t, bi)
                    times_c(b, ci)
                    for t, bi in (mine[2:] if ci else mine):
                        empty(b - 1, t, bi)
                    if ci in (2, 3):
                        for i in range(2):
                            log1p(b, f"p1f_{2 * (ci - 2) + i}")
                    if 12 <= ci <= 15:
                        log1p(b, f"p1b_{ci - 12}")
                    if a_next:
                        if ci in (13, 14):
                            group_stats(b + 1, 2 * (ci - 13))
                            group_stats(b + 1, 2 * (ci - 13) + 1)
                        if ci == 14:
                            group_aggregate(b + 1)
                        if ci == 15:
                            group_mean(b + 1)
                        if ci == 16:
                            group_var(b + 1)
                        if ci in (18, 19):
                            normalise(b + 1, 2 * (ci - 18))
                            normalise(b + 1, 2 * (ci - 18) + 1)
                        if ci == 33:
                            log1p(b + 1, "x23")
                        if ci == 34:
                            log1p(b + 1, "p2")
                    if CH[ci]["n0"] + CH[ci]["ns"] == N:
                        layer_norm(b, CH[ci]["pi"])

            def prologue():
                for k in range(KC):
                    group_stats(0, k)
                group_aggregate(0)
                group_mean(0)
                group_var(0)
                for k in range(KC):
                    normalise(0, k)
                log1p(0, "x23")
                log1p(0, "p2")

            def epilogue():
                for t in ["nb_0", "nb_1", "nb_2", "nb_3"] + [f"out_{j}" for j in range(8)]:
                    empty(batches - 1, t, BANK_X if int(t[-1]) % 2 else BANK_T)

            program(dve, prologue, body, epilogue)


def conv_layer(nc, tag, x_in, x_out, taps_dram, masks_dram, ident_dram, group_dram, batches):
    ctx = ExitStack()
    with ctx:
        def sb(name, shape):
            return ctx.enter_context(nc.sbuf_tensor(f"{tag}_{name}", shape, F32))

        def sem(name):
            return ctx.enter_context(nc.semaphore(f"{tag}_{name}"))

        ident = sb("ident", [P, P])
        group = sb("group", [P, P])
        taps = sb("taps", [P, TAPS])
        masks = sb("masks", [P, TAPS, ROWS * WIDTH])
        band = sb("band", [P, ROWS * WIDTH])
        xin = sb("xin", [P, 2, KC, L1])
        xn = sb("xn", [P, KC, L1])
        xt = sb("xt", [P, 8, C])
        y = sb("y", [P, 2, L1])
        gst = sb("gst", [P, KC, 12])
        gmv = sb("gmv", [P, KC, 2])
        ggm = sb("ggm", [P, KC, 2])
        gd = sb("gd", [P, KC])
        gd2 = sb("gd2", [P, KC])
        gve = sb("gve", [P, KC])
        gr = sb("gr", [P, KC])
        mhalf = sb("mhalf", [P, KC])
        bank = ctx.enter_context(nc.psum_tensor(f"{tag}_bank", [P, 8 * BANK], F32))

        const_in = sem("const_in")
        band_step = sem("band_step")
        mhalf_set = sem("mhalf_set")
        x_arrived = [sem(f"x_arrived{i}") for i in range(2)]
        gn_step = sem("gn_step")
        gm_full = sem("gm_full")
        gm_read = sem("gm_read")
        gn_rstd = sem("gn_rstd")
        xn_done = sem("xn_done")
        xt_full = sem("xt_full")
        xt_done = sem("xt_done")
        y_full = sem("y_full")
        y_done = sem("y_done")
        stored = [sem(f"stored{i}") for i in range(2)]
        held = sem("held")

        def hold(engine):
            engine.sem_inc(held, 1)

        block = ctx.enter_context(nc.Block())

        @block.sync
        def _(sp):
            sp.sem_inc(stored[0], 1)
            sp.sem_inc(stored[1], 1)
            for dst, src in ((ident[:], ident_dram), (group[:], group_dram), (masks[:], masks_dram),
                             (taps[:], taps_dram.partition_broadcast(P))):
                sp.dma_start(dst, src).then_inc(const_in, 16)

            def load(b, j):
                src = x_in[bass.ds(b, 1)].rearrange("a (k p) l -> p (a k) l", p=P)
                sp.dma_start(xin[:, j], src).then_inc(x_arrived[j], 16)

            def stores(b, bb, j):
                for k in range(KC):
                    sp.wait_ge(y_done, (b + j) * KC + k + 1 + 1)
                    sp.dma_start(x_out[bass.ds(b + j, 1), k * P:(k + 1) * P, :].rearrange("a p l -> (a p) l"),
                                 y[:, k % 2, :]).then_inc(stored[k % 2], 16)

            load(0, 0)

            def pair(b, last):
                load(b + 1, 1)
                stores(b, None, 0)
                if not last:
                    load(b + 2, 0)
                stores(b, None, 1)

            if batches > 2:
                with sp.Fori(0, batches - 2, 2) as b:
                    pair(b, False)
            pair(batches - 2, True)
            for i in range(2):
                sp.wait_ge(stored[i], batches * 32 + 1)

        @block.tensor
        def _(pe):
            pe.sem_inc(y_full, 1)
            mm = nc.tensor.matmul
            pe.wait_ge(const_in, 64)
            pe.wait_ge(band_step, TAPS)
            with pe.Fori(0, batches) as b:
                pe.wait_ge(gn_step, b * 15 + 12)
                mm(bank[:, 0:2 * KC], group[:], gmv[:].rearrange("p k s -> p (k s)"), start=True, stop=True).then_inc(gm_full, 1)
                pe.wait_ge(gn_step, b * 15 + 14)
                mm(bank[:, BANK:BANK + KC], group[:], gd2[:], start=True, stop=True).then_inc(gm_full, 1)
                pe.wait_ge(xn_done, b * KC + KC)
                for lb in range(8):
                    if lb >= 2:
                        pe.wait_ge(xt_done, b * 8 + lb - 1)
                    for k in range(KC):
                        o = (2 + lb % 2) * BANK + k * P
                        last = mm(bank[:, o:o + P], xn[:, k, lb * P:(lb + 1) * P], ident[:],
                                  start=(k == 0), stop=(k == KC - 1), is_transpose=True)
                    last.then_inc(xt_full, 1)
                pe.wait_ge(xt_done, b * 8 + 8)
                for k in range(KC):
                    if k < 2:
                        pe.wait_ge(y_done, b * KC + 1)
                    else:
                        pe.wait_ge(y_done, b * KC + k - 1 + 1)
                    started = set()
                    for j in range(8):
                        lo, hi = max(0, (4 * j - 1) * WIDTH), min(L1, (4 * j + 6) * WIDTH)
                        for q in range(2):
                            a, e = max(lo, q * BANK), min(hi, (q + 1) * BANK)
                            if a >= e:
                                continue
                            base = (4 + 2 * (k % 2)) * BANK
                            off = (4 * j - 1) * WIDTH
                            last = mm(bank[:, base + a:base + e], xt[:, j, k * P:(k + 1) * P], band[:, a - off:e - off],
                                      start=q not in started, stop=(j == (4 if q == 0 else 7)), skip_group_check=True)
                            started.add(q)
                    last.then_inc(y_full, 1)

        @block.scalar
        def _(act):
            with act.Fori(0, batches) as b:
                for lb in range(8):
                    act.wait_ge(xt_full, b * 8 + lb + 1)
                    act.wait_ge(y_full, b * KC + 1)
                    nc.scalar.activation(xt[:, lb, :], bank[:, (2 + lb % 2) * BANK:(3 + lb % 2) * BANK],
                                         ACT.Copy).then_inc(xt_done, 1)

        @block.gpsimd
        def _(pool):
            nc.gpsimd.memset(mhalf[:], -0.5).then_inc(mhalf_set, 1)
            pool.wait_ge(mhalf_set, 1)
            with pool.Fori(0, batches) as b:
                pool.wait_ge(gn_step, b * 15 + 15)
                nc.gpsimd.tensor_tensor(gr[:], gve[:], mhalf[:], ALU.pow).then_inc(gn_rstd, 1)

        @block.vector
        def _(dve):
            dve.sem_inc(y_done, 1)
            V = nc.vector
            dve.wait_ge(const_in, 64)
            V.tensor_scalar(band[:], masks[:, 0, :], taps[:, 0:1], None, ALU.mult).then_inc(band_step, 1)
            for t in range(1, TAPS):
                dve.wait_ge(band_step, t)
                V.scalar_tensor_tensor(band[:], masks[:, t, :], taps[:, t:t + 1], band[:], ALU.mult, ALU.add).then_inc(band_step, 1)

            def batch(b, bj, j, half):
                dve.wait_ge(x_arrived[j], half * 16 + 16)
                g0 = b * 15
                for k in range(KC):
                    for q in range(2):
                        V.bn_stats(gst[:, k, 6 * q:6 * q + 6], xin[:, j, k, q * BANK:(q + 1) * BANK]).then_inc(gn_step, 1)
                for k in range(KC):
                    dve.wait_ge(gn_step, g0 + 2 * k + 2)
                    hold(dve)
                    V.bn_aggr(gmv[:, k, :], gst[:, k, :]).then_inc(gn_step, 1)
                dve.wait_ge(gm_full, b * 2 + 1)
                V.tensor_copy(ggm[:].rearrange("p k s -> p (k s)"), bank[:, 0:2 * KC]).then_inc(gm_read, 1)
                dve.wait_ge(gm_read, b * 2 + 1)
                V.tensor_tensor(gd[:], gmv[:, :, 0], ggm[:, :, 0], ALU.subtract).then_inc(gn_step, 1)
                dve.wait_ge(gn_step, g0 + 13)
                V.tensor_tensor(gd2[:], gd[:], gd[:], ALU.mult).then_inc(gn_step, 1)
                dve.wait_ge(gm_full, b * 2 + 2)
                V.tensor_tensor(gve[:], bank[:, BANK:BANK + KC], ggm[:, :, 1], ALU.add).then_inc(gm_read, 1)
                dve.wait_ge(gm_read, b * 2 + 2)
                V.tensor_scalar(gve[:], gve[:], EPS, None, ALU.add).then_inc(gn_step, 1)
                dve.wait_ge(gn_rstd, b + 1)
                for k in range(KC):
                    V.tensor_scalar(xn[:, k, :], xin[:, j, k, :], ggm[:, k, 0:1], gr[:, k:k + 1],
                                    ALU.subtract, ALU.mult).then_inc(xn_done, 1)
                for k in range(KC):
                    dve.wait_ge(y_full, b * KC + k + 1 + 1)
                    if k >= 2:
                        dve.wait_ge(stored[k % 2], b * 32 + 16 + 1)
                    else:
                        dve.wait_ge(stored[k % 2], b * 32 + 1)
                    base = (4 + 2 * (k % 2)) * BANK
                    V.tensor_tensor(y[:, k % 2, :], bank[:, base:base + L1], xin[:, j, k, :], ALU.add).then_inc(y_done, 1)

            with dve.Fori(0, batches // 2) as pair:
                for j in range(2):
                    batch(pair * 2 + j, None, j, pair)


def attention_layer(nc, tag, x_in, x_out, wqkv_dram, wproj_dram, vec_dram, ident_dram, group_dram, mean_dram, batches):
    ctx = ExitStack()
    with ctx:
        def sb(name, shape):
            return ctx.enter_context(nc.sbuf_tensor(f"{tag}_{name}", shape, F32))

        def sem(name):
            return ctx.enter_context(nc.semaphore(f"{tag}_{name}"))

        ident = sb("ident", [P, P])
        group = sb("group", [P, P])
        mean = sb("mean", [P, P])
        wqkv = sb("wqkv", [P, KC, 3 * C])
        wproj = sb("wproj", [P, KC, C])
        vec = sb("vec", [P, 24])
        gamma, beta, bq, bv, bo = vec[:, 0:4], vec[:, 4:8], vec[:, 8:16], vec[:, 16:20], vec[:, 20:24]
        xin = sb("xin", [P, KC, L1])
        xf = sb("xf", [P, KC, L1])
        qk = sb("qk", [P, 8, L1])
        vt = sb("vt", [P, NB, C])
        vals = sb("vals", [P, KC, L1])
        prob = sb("prob", [P, 2, L1])
        pt = sb("pt", [P, 2, L1])
        vn = sb("vn", [P, C])
        y = sb("y", [P, 2, L1])
        mx = sb("mx", [P, 2])
        nbias = sb("nbias", [P, 2])
        rs = sb("rs", [P, 2, HEADS])
        rr = sb("rr", [P, HEADS])
        gst = sb("gst", [P, KC, 12])
        gmv = sb("gmv", [P, KC, 2])
        ggm = sb("ggm", [P, KC, 2])
        gd = sb("gd", [P, KC])
        gd2 = sb("gd2", [P, KC])
        gve = sb("gve", [P, KC])
        gr = sb("gr", [P, KC])
        st = sb("st", [P, KC, 2])
        st2 = sb("st2", [P, KC])
        lm = sb("lm", [P, 2])
        ld = sb("ld", [P, KC])
        ld2 = sb("ld2", [P, KC])
        lve = sb("lve", [P, 1])
        lr = sb("lr", [P, 1])
        sc = sb("sc", [P, KC])
        aa = sb("aa", [P, KC])
        bb = sb("bb", [P, KC])
        cc = sb("cc", [P, KC])
        mhalf = sb("mhalf", [P, KC])
        bank = ctx.enter_context(nc.psum_tensor(f"{tag}_bank", [P, 8 * BANK], F32))

        def bk(i, n=BANK):
            return bank[:, i * BANK:i * BANK + n]

        T_QK, T_V, T_O, TILES = 4, 20, 28, 36
        BY_ACT = {t for t in range(T_QK, T_O) if t % 2 == 0}
        PER_A, PER_D = len(BY_ACT), TILES - len(BY_ACT)

        def left(t):
            return sum((i in BY_ACT) == (t in BY_ACT) for i in range(t + 1))

        UNITS = NB * HEADS
        STEPS = 8 + 4 + 2 + 1 + 3 + 2 + 1 + 5

        const_in = sem("const_in")
        mhalf_set = sem("mhalf_set")
        x_arrived = sem("x_arrived")
        gn_step = sem("gn_step")
        rstd = sem("rstd")
        xf_done = sem("xf_done")
        tile_full = sem("tile_full")
        tile_act = sem("tile_act")
        tile_dve = sem("tile_dve")
        s_full = sem("s_full")
        max_done = sem("max_done")
        bias_done = sem("bias_done")
        p_full = sem("p_full")
        pt_full = sem("pt_full")
        pt_dve = sem("pt_dve")
        pt_act = sem("pt_act")
        o_full = sem("o_full")
        rr_done = sem("rr_done")
        vn_done = sem("vn_done")
        vtr_full = sem("vtr_full")
        vals_done = sem("vals_done")
        stored = [sem(f"stored{i}") for i in range(2)]
        held = sem("held")

        def hold(engine):
            engine.sem_inc(held, 1)

        block = ctx.enter_context(nc.Block())

        @block.sync
        def _(sp):
            sp.sem_inc(stored[0], 1)
            sp.sem_inc(stored[1], 1)
            for dst, src in ((wqkv[:], wqkv_dram), (wproj[:], wproj_dram), (vec[:], vec_dram),
                             (ident[:], ident_dram), (group[:], group_dram), (mean[:], mean_dram)):
                sp.dma_start(dst, src).then_inc(const_in, 16)
            with sp.Fori(0, batches) as b:
                sp.wait_ge(tile_dve, b * PER_D + 1)
                sp.dma_start(xin[:], x_in[bass.ds(b, 1)].rearrange("a (k p) l -> p (a k) l", p=P)).then_inc(x_arrived, 16)
                for m in range(KC):
                    sp.wait_ge(tile_dve, b * PER_D + left(T_O + 2 * m + 1) + 1)
                    sp.dma_start(x_out[bass.ds(b, 1), m * P:(m + 1) * P, :].rearrange("a p l -> (a p) l"),
                                 y[:, m % 2, :]).then_inc(stored[m % 2], 16)
            for i in range(2):
                sp.wait_ge(stored[i], batches * 32 + 1)

        @block.tensor
        def _(pe):
            mm = nc.tensor.matmul
            pe.wait_ge(const_in, 96)

            def tile_wait(b, t):
                if t < 8:
                    pe.wait_ge(tile_dve, b * PER_D + 1)
                elif t - 8 in BY_ACT:
                    pe.wait_ge(tile_act, b * PER_A + left(t - 8))
                else:
                    pe.wait_ge(tile_dve, b * PER_D + left(t - 8) + 1)

            def scores(b, u):
                i, h = u // HEADS, u % HEADS
                if u >= 2:
                    pe.wait_ge(p_full, b * UNITS + u - 1)
                r0 = (h % 2) * DH
                for q in range(2):
                    o = (u % 2) * 2 * BANK + q * BANK
                    last = mm(bank[:, o:o + BANK], qk[r0:r0 + DH, h // 2, i * P:(i + 1) * P],
                              qk[r0:r0 + DH, 4 + h // 2, q * BANK:(q + 1) * BANK], start=True, stop=True)
                last.then_inc(s_full, 1)

            def turn(b, u):
                pe.wait_ge(p_full, b * UNITS + u + 1)
                if u >= 1:
                    pe.wait_ge(pt_dve, b * UNITS + u)
                    pe.wait_ge(pt_act, b * UNITS + u)
                for m in range(NB):
                    last = mm(bank[:, 4 * BANK + m * P:4 * BANK + (m + 1) * P], prob[:, u % 2, m * P:(m + 1) * P],
                              ident[:], start=(m % 4 == 0), stop=(m % 4 == 3), is_transpose=True)
                last.then_inc(pt_full, 1)

            def weigh(b, u):
                i, h = u // HEADS, u % HEADS
                pe.wait_ge(pt_dve, b * UNITS + u + 1)
                pe.wait_ge(pt_act, b * UNITS + u + 1)
                if h == 0 and i > 0:
                    pe.wait_ge(vn_done, b * NB + i)
                for m in range(NB):
                    last = mm(bank[:, 6 * BANK + h * DH:6 * BANK + (h + 1) * DH], pt[:, u % 2, m * P:(m + 1) * P],
                              vt[:, m, h * DH:(h + 1) * DH], start=(m == 0), stop=(m == NB - 1))
                last.then_inc(o_full, 1)

            def back(b, i):
                pe.wait_ge(vn_done, b * NB + i + 1)
                if i > 0:
                    pe.wait_ge(vals_done, b * NB + i)
                for k in range(KC):
                    last = mm(bank[:, 7 * BANK + k * P:7 * BANK + (k + 1) * P], vn[:, k * P:(k + 1) * P], ident[:],
                              start=(k == 0), stop=(k == KC - 1), is_transpose=True)
                last.then_inc(vtr_full, 1)

            with pe.Fori(0, batches) as b:
                g0 = b * STEPS
                tile_wait(b, 0)
                pe.wait_ge(gn_step, g0 + 12)
                mm(bk(0)[:, 0:2 * KC], group[:], gmv[:].rearrange("p k s -> p (k s)"), start=True, stop=True).then_inc(tile_full, 1)
                pe.wait_ge(gn_step, g0 + 14)
                mm(bk(1)[:, 0:KC], group[:], gd2[:], start=True, stop=True).then_inc(tile_full, 1)
                pe.wait_ge(gn_step, g0 + 18)
                for k in range(KC):
                    last = mm(bk(2)[:, 0:2], mean[:], st[:, k, :], start=(k == 0), stop=(k == KC - 1))
                last.then_inc(tile_full, 1)
                pe.wait_ge(gn_step, g0 + 20)
                for k in range(KC):
                    last = mm(bk(3)[:, 0:1], mean[:], ld2[:, k:k + 1], start=(k == 0), stop=(k == KC - 1))
                last.then_inc(tile_full, 1)
                pe.wait_ge(xf_done, b * KC + KC)
                for m in range(8):
                    for q in range(2):
                        t = T_QK + 2 * m + q
                        tile_wait(b, t)
                        for k in range(KC):
                            last = mm(bk(t % 8), wqkv[:, k, m * P:(m + 1) * P], xf[:, k, q * BANK:(q + 1) * BANK],
                                      start=(k == 0), stop=(k == KC - 1))
                        last.then_inc(tile_full, 1)
                for i in range(NB):
                    t = T_V + i
                    tile_wait(b, t)
                    for k in range(KC):
                        last = mm(bk(t % 8), xf[:, k, i * P:(i + 1) * P], wqkv[:, k, 2 * C:3 * C],
                                  start=(k == 0), stop=(k == KC - 1))
                    last.then_inc(tile_full, 1)
                pe.wait_ge(tile_act, b * PER_A + PER_A)
                pe.wait_ge(tile_dve, b * PER_D + left(T_V + 7) + 1)
                for u in range(UNITS + 2):
                    if u < UNITS:
                        scores(b, u)
                    if 1 <= u <= UNITS:
                        turn(b, u - 1)
                    if u >= 2:
                        weigh(b, u - 2)
                        if u - 2 > 7 and (u - 2) % HEADS == 1:
                            back(b, (u - 2) // HEADS - 1)
                back(b, NB - 1)
                pe.wait_ge(vals_done, b * NB + NB)
                for m in range(KC):
                    for q in range(2):
                        t = T_O + 2 * m + q
                        if t >= T_O + 8:
                            tile_wait(b, t)
                        for k in range(KC):
                            last = mm(bk(t % 8), wproj[:, k, m * P:(m + 1) * P], vals[:, k, q * BANK:(q + 1) * BANK],
                                      start=(k == 0), stop=(k == KC - 1))
                        last.then_inc(tile_full, 1)

        @block.scalar
        def _(act):
            A = nc.scalar.activation
            act.wait_ge(const_in, 96)

            def exps(b, u):
                act.wait_ge(bias_done, b * UNITS + u + 1)
                i, h = u // HEADS, u % HEADS
                if u >= 2:
                    act.wait_ge(pt_full, b * UNITS + u - 1)
                if h == 0 and i >= 2:
                    act.wait_ge(rr_done, b * NB + i - 1)
                A(prob[:, u % 2, :], bank[:, (u % 2) * 2 * BANK:(u % 2) * 2 * BANK + L1], ACT.Exp,
                  bias=nbias[:, u % 2:u % 2 + 1], scale=SCALE, accum_out=rs[:, i % 2, h:h + 1]).then_inc(p_full, 1)

            def half(b, u):
                act.wait_ge(pt_full, b * UNITS + u + 1)
                if u >= 2:
                    act.wait_ge(o_full, b * UNITS + u - 1)
                A(pt[:, u % 2, BANK:], bank[:, 5 * BANK:6 * BANK], ACT.Copy).then_inc(pt_act, 1)

            def values(b, i):
                act.wait_ge(vtr_full, b * NB + i + 1)
                for k in range(KC):
                    last = A(vals[:, k, i * P:(i + 1) * P], bank[:, 7 * BANK + k * P:7 * BANK + (k + 1) * P],
                             ACT.Identity, bias=bv[:, k:k + 1])
                last.then_inc(vals_done, 1)

            with act.Fori(0, batches) as b:
                for t in sorted(BY_ACT):
                    act.wait_ge(tile_full, b * TILES + t + 1)
                    if t < T_V:
                        m, q = (t - T_QK) // 2, (t - T_QK) % 2
                        A(qk[:, m, q * BANK:(q + 1) * BANK], bk(t % 8), ACT.Identity, bias=bq[:, m:m + 1]).then_inc(tile_act, 1)
                    else:
                        A(vt[:, t - T_V, :], bk(t % 8), ACT.Copy).then_inc(tile_act, 1)
                for u in range(UNITS + 1):
                    if u < UNITS:
                        exps(b, u)
                    if u >= 1:
                        half(b, u - 1)
                        if u - 1 > 10 and (u - 1) % HEADS == 3:
                            values(b, (u - 1) // HEADS - 1)
                values(b, NB - 1)

        @block.gpsimd
        def _(pool):
            nc.gpsimd.memset(mhalf[:], -0.5).then_inc(mhalf_set, 1)
            pool.wait_ge(mhalf_set, 1)
            with pool.Fori(0, batches) as b:
                g0 = b * STEPS
                pool.wait_ge(gn_step, g0 + 15)
                nc.gpsimd.tensor_tensor(gr[:], gve[:], mhalf[:], ALU.pow).then_inc(rstd, 1)
                pool.wait_ge(gn_step, g0 + 21)
                nc.gpsimd.tensor_tensor(lr[:], lve[:], mhalf[:, 0:1], ALU.pow).then_inc(rstd, 1)

        @block.vector
        def _(dve):
            dve.sem_inc(tile_dve, 1)
            V = nc.vector
            dve.wait_ge(const_in, 96)

            def maximum(b, u):
                dve.wait_ge(s_full, b * UNITS + u + 1)
                if u >= 2:
                    dve.wait_ge(p_full, b * UNITS + u - 1)
                V.reduce_max(mx[:, u % 2:u % 2 + 1], bank[:, (u % 2) * 2 * BANK:(u % 2) * 2 * BANK + L1], AX.X).then_inc(max_done, 1)
                dve.wait_ge(max_done, b * UNITS + u + 1)
                V.tensor_scalar(nbias[:, u % 2:u % 2 + 1], mx[:, u % 2:u % 2 + 1], -SCALE, None, ALU.mult).then_inc(bias_done, 1)

            def half(b, u):
                dve.wait_ge(pt_full, b * UNITS + u + 1)
                if u >= 2:
                    dve.wait_ge(o_full, b * UNITS + u - 1)
                V.tensor_copy(pt[:, u % 2, 0:BANK], bank[:, 4 * BANK:5 * BANK]).then_inc(pt_dve, 1)

            def normalise(b, i):
                dve.wait_ge(p_full, b * UNITS + (i + 1) * HEADS)
                V.reciprocal(rr[:], rs[:, i % 2, :]).then_inc(rr_done, 1)
                dve.wait_ge(rr_done, b * NB + i + 1)
                dve.wait_ge(o_full, b * UNITS + (i + 1) * HEADS)
                if i > 0:
                    dve.wait_ge(vtr_full, b * NB + i)
                V.tensor_tensor(vn[:].rearrange("p (h d) -> p h d", d=DH),
                                bk(6).rearrange("p (h d) -> p h d", d=DH),
                                rr[:].unsqueeze(2).broadcast_to([P, HEADS, DH]), ALU.mult).then_inc(vn_done, 1)

            with dve.Fori(0, batches) as b:
                n = [0]
                g0 = b * STEPS

                def step(ins, wait=True):
                    n[0] += 1
                    ins.then_inc(gn_step, 1)
                    if wait:
                        dve.wait_ge(gn_step, g0 + n[0])

                dve.wait_ge(x_arrived, b * 16 + 16)
                for k in range(KC):
                    for q in range(2):
                        step(V.bn_stats(gst[:, k, 6 * q:6 * q + 6], xin[:, k, q * BANK:(q + 1) * BANK]), False)
                dve.wait_ge(gn_step, g0 + 8)
                hold(dve)
                for k in range(KC):
                    step(V.bn_aggr(gmv[:, k, :], gst[:, k, :]), False)
                dve.wait_ge(tile_full, b * TILES + 1)
                V.tensor_copy(ggm[:].rearrange("p k s -> p (k s)"), bk(0)[:, 0:2 * KC]).then_inc(tile_dve, 1)
                dve.wait_ge(tile_dve, b * PER_D + 1 + 1)
                step(V.tensor_tensor(gd[:], gmv[:, :, 0], ggm[:, :, 0], ALU.subtract))
                step(V.tensor_tensor(gd2[:], gd[:], gd[:], ALU.mult))
                dve.wait_ge(tile_full, b * TILES + 2)
                V.tensor_tensor(gve[:], bk(1)[:, 0:KC], ggm[:, :, 1], ALU.add).then_inc(tile_dve, 1)
                dve.wait_ge(tile_dve, b * PER_D + 2 + 1)
                step(V.tensor_scalar(gve[:], gve[:], EPS, None, ALU.add))
                dve.wait_ge(rstd, b * 2 + 1)
                step(V.tensor_tensor(st2[:], gmv[:, :, 1], gr[:], ALU.mult))
                step(V.tensor_tensor(st[:, :, 0], gd[:], gr[:], ALU.mult))
                step(V.tensor_tensor(st[:, :, 1], st2[:], gr[:], ALU.mult))
                dve.wait_ge(tile_full, b * TILES + 3)
                V.tensor_copy(lm[:], bk(2)[:, 0:2]).then_inc(tile_dve, 1)
                dve.wait_ge(tile_dve, b * PER_D + 3 + 1)
                step(V.tensor_scalar(ld[:], st[:, :, 0], lm[:, 0:1], None, ALU.subtract))
                step(V.tensor_tensor(ld2[:], ld[:], ld[:], ALU.mult))
                dve.wait_ge(tile_full, b * TILES + 4)
                V.tensor_tensor(lve[:], bk(3)[:, 0:1], lm[:, 1:2], ALU.add).then_inc(tile_dve, 1)
                dve.wait_ge(tile_dve, b * PER_D + 4 + 1)
                step(V.tensor_scalar(lve[:], lve[:], EPS, None, ALU.add))
                dve.wait_ge(rstd, b * 2 + 2)
                step(V.tensor_scalar(sc[:], gamma, lr[:, 0:1], None, ALU.mult))
                step(V.tensor_tensor(aa[:], sc[:], gr[:], ALU.mult))
                step(V.tensor_tensor(bb[:], ggm[:, :, 0], gr[:], ALU.mult))
                step(V.scalar_tensor_tensor(cc[:], bb[:], lm[:, 0:1], sc[:], ALU.add, ALU.mult))
                step(V.tensor_tensor(bb[:], beta, cc[:], ALU.subtract))
                assert n[0] == STEPS
                for k in range(KC):
                    V.tensor_scalar(xf[:, k, :], xin[:, k, :], aa[:, k:k + 1], bb[:, k:k + 1], ALU.mult, ALU.add).then_inc(xf_done, 1)
                for t in range(T_QK, T_O):
                    if t in BY_ACT:
                        continue
                    dve.wait_ge(tile_full, b * TILES + t + 1)
                    if t < T_V:
                        m, q = (t - T_QK) // 2, (t - T_QK) % 2
                        V.tensor_scalar(qk[:, m, q * BANK:(q + 1) * BANK], bk(t % 8), bq[:, m:m + 1], None, ALU.add).then_inc(tile_dve, 1)
                    else:
                        V.tensor_copy(vt[:, t - T_V, :], bk(t % 8)).then_inc(tile_dve, 1)
                for u in range(UNITS + 2):
                    if u < UNITS:
                        maximum(b, u)
                    if 1 <= u <= UNITS:
                        half(b, u - 1)
                    if u >= 2 and (u - 2) % HEADS == HEADS - 1:
                        normalise(b, (u - 2) // HEADS)
                for m in range(KC):
                    for q in range(2):
                        t = T_O + 2 * m + q
                        dve.wait_ge(tile_full, b * TILES + t + 1)
                        dve.wait_ge(stored[m % 2], b * 32 + 16 * (m // 2) + 1)
                        V.scalar_tensor_tensor(y[:, m % 2, q * BANK:(q + 1) * BANK], bk(t % 8), bo[:, m:m + 1],
                                               xin[:, m, q * BANK:(q + 1) * BANK], ALU.add, ALU.add).then_inc(tile_dve, 1)


def build_program(nc, a, batches):
    shape = (batches, C, L1)
    between = [nc.dram_tensor(f"x_after_{i}", shape, F32, kind="Internal").ap() for i in range(3)]
    ssm_layer(nc, "l0", a["x"], between[0], a["w0"], a["nat0"], a["low0"], a["ident"], a["group"], batches)
    conv_layer(nc, "l1", between[0], between[1], a["taps"], a["masks"], a["ident"], a["group"], batches)
    ssm_layer(nc, "l2", between[1], between[2], a["w2"], a["nat2"], a["low2"], a["ident"], a["group"], batches)
    attention_layer(nc, "l3", between[2], a["out"], a["wqkv"], a["wproj"], a["vec"], a["ident"], a["group"],
                    a["mean"], batches)


def chunks(m):
    return np.ascontiguousarray(m.reshape(m.shape[0] // P, P, -1).transpose(1, 0, 2))


def ssm_weights(g):
    parts = [g("in_w")[D:].T] + [g(n).transpose(1, 2, 3, 0).reshape(D, 4 * D) for n in ("c2_w", "c3_w")]
    parts += [g("out_w").T] + [g(f"xw{i}")[R:].T for i in (1, 2, 3)] + [g(f"Al{i}") for i in (1, 2, 3)]
    parts += [g(n)[:, None] for n in ("in_b", "c1_b", "c2_b", "c3_b", "out_b")]
    parts += [g(f"{n}{i}")[:, None] for n in ("dtb", "Dv", "g", "be") for i in (1, 2, 3)]
    w = np.concatenate([chunks(m).reshape(P, -1) for m in parts], axis=1)
    assert w.shape[1] == W_TOTAL
    nat = chunks(np.concatenate([g("in_w")[:D], g("c1_w").T], axis=1))
    low = np.stack([np.stack([g(f"xw{i}")[:R] for i in (1, 2, 3)], axis=1),
                    np.stack([g(f"dtw{i}").T for i in (1, 2, 3)], axis=1)], axis=1)
    return np.ascontiguousarray(w), nat, np.ascontiguousarray(low)


def band_masks():
    m = np.zeros((4, WIDTH, TAPS, ROWS, WIDTH), np.float32)
    for a in range(4):
        for b in range(4):
            for s in range(4):
                for w in range(WIDTH):
                    if 0 <= w + b - 1 < WIDTH:
                        m[s, w, 4 * a + b, s + a, w + b - 1] = 1.0
    return m.reshape(P, TAPS, ROWS * WIDTH)


def kernel(**inputs):
    import concourse.bacc as bacc
    from concourse.bass_utils import run_bass_kernel_spmd

    def layer(i):
        return lambda name: np.asarray(inputs[f"L{i}_conv_{name}"])

    x = np.asarray(inputs["x"])
    batches = x.shape[0]
    same_group = np.arange(P)[:, None] // 16 == np.arange(P)[None, :] // 16
    arrays = {"x": np.ascontiguousarray(x.reshape(batches, C, L1)),
              "ident": np.eye(P, dtype=np.float32),
              "group": np.where(same_group, np.float32(1 / 16), np.float32(0)),
              "mean": np.full((P, P), 1 / C, np.float32),
              "masks": band_masks(),
              "taps": np.ascontiguousarray(np.asarray(inputs["L1_conv_kernel"]).reshape(TAPS)),
              "wqkv": chunks(layer(3)("w_qkv").T), "wproj": chunks(layer(3)("w_proj").T),
              "vec": np.concatenate([chunks(layer(3)(n)[:, None])[:, :, 0]
                                     for n in ("gn_gamma", "gn_beta", "b_qkv", "b_proj")], axis=1)}
    for i in (0, 2):
        arrays[f"w{i}"], arrays[f"nat{i}"], arrays[f"low{i}"] = ssm_weights(layer(i))

    nc = bacc.Bacc("TRN2", target_bir_lowering=False, num_devices=1)
    aps = {n: nc.dram_tensor(f"in_{n}", a.shape, mybir.dt.from_np(a.dtype), kind="ExternalInput").ap()
           for n, a in arrays.items()}
    aps["out"] = nc.dram_tensor("out", arrays["x"].shape, F32, kind="ExternalOutput").ap()
    build_program(nc, aps, batches)
    r = run_bass_kernel_spmd(nc, [{f"in_{n}": np.ascontiguousarray(a) for n, a in arrays.items()}], core_ids=[0])
    return r.results[0]["out"].reshape(x.shape)
```

```python
import concourse.bass as bass
import numpy as np
from concourse import mybir
from contextlib import ExitStack

F32 = mybir.dt.float32
ALU = mybir.AluOpType
ACT = mybir.ActivationFunctionType
AX = mybir.AxisListType

P = 128
C = 512
KC = C // P
L1, L2, L3 = 1024, 256, 64
D = 256
NH = D // P
N = 16
R = 8
BANK = 512
EPS = 1e-5
TAPS, ROWS, WIDTH = 16, 7, 32
HEADS, DH = 8, 64
NB = L1 // P
SCALE = float(C) ** -0.5

W_COLS = {}
_at = 0
for _name, _n in (("inz", KC * D), ("c2", NH * 4 * D), ("c3", NH * 4 * D), ("out", NH * C),
                  ("xw1", NH * 2 * N), ("xw2", NH * 2 * N), ("xw3", NH * 2 * N),
                  ("Al1", NH * N), ("Al2", NH * N), ("Al3", NH * N),
                  ("in_b", KC), ("c1_b", NH), ("c2_b", NH), ("c3_b", NH), ("out_b", KC),
                  ("dtb1", NH), ("dtb2", NH), ("dtb3", NH), ("Dv1", NH), ("Dv2", NH), ("Dv3", NH),
                  ("g1", NH), ("g2", NH), ("g3", NH), ("be1", NH), ("be2", NH), ("be3", NH)):
    W_COLS[_name] = (_at, _n)
    _at += _n
W_TOTAL = _at


def ssm_layer(nc, tag, x_in, x_out, w_dram, nat_dram, low_dram, ident_dram, group_dram, batches):
    ctx = ExitStack()
    with ctx:
        def sb(name, shape):
            return ctx.enter_context(nc.sbuf_tensor(f"{tag}_{name}", shape, F32))

        def sem(name):
            return ctx.enter_context(nc.semaphore(f"{tag}_{name}"))

        PITCH = max(NH * (L1 + 1), 4 * NH * (L2 + 1), N * NH * (L3 + 1))
        NA, NU = 2, 4
        W = sb("W", [P, W_TOTAL])
        wc = sb("wc", [P, KC, D])
        wd = sb("wd", [P, 3, NH, D])
        f1_b = sb("f1_b", [P, NH])
        ident = sb("ident", [P, P])
        group = sb("group", [P, P])
        xin = sb("xin", [P, KC, L1])
        z = sb("z", [P, NH, L1])
        f1 = sb("f1", [P, NH, L1])
        f2 = sb("f2", [P, NH, L2])
        f3 = sb("f3", [P, NH, L3])
        dA_ring = sb("dA", [P, NA, PITCH])
        u_ring = sb("u", [P, NU, PITCH])
        b_sb = sb("b_sb", [P, 3, 1024])
        delta = {"3": sb("dl3", [P, NH, L3]), "2": sb("dl2", [P, NH, L2]),
                 "1f": sb("dl1f", [P, NH, L1]), "1b": sb("dl1b", [P, NH, L1])}
        dx = {"3": sb("dx3", [P, NH, L3]), "2": sb("dx2", [P, NH, L2]),
              "1f": sb("dx1f", [P, NH, L1]), "1b": sb("dx1b", [P, NH, L1])}
        bct = {"3": sb("bct3", [P, 1, 2 * N]), "2": sb("bct2", [P, 2, 2 * N]),
               "1f": sb("bct1f", [P, NB, 2 * N]), "1b": sb("bct1b", [P, NB, 2 * N])}
        hn_buf = sb("hn", [P, 8, D])
        hn = {"3": hn_buf[:, 0:2, :], "2": hn_buf[:, 2:6, :], "1f": hn_buf[:], "1b": hn_buf[:]}
        out1 = sb("out1", [P, NH, L1])
        xres = sb("xres", [P, 2, BANK])
        y3s = sb("y3s", [P, NH, L3])
        y2s = sb("y2s", [P, NH, L2])
        T_u = sb("T_u", [P, 4, BANK])
        T_c = sb("T_c", [P, BANK])
        diag = sb("diag", [P, 3, NH, P])
        negA = sb("negA", [P, 3 * NH * N])
        bt = sb("bt", [P, 4 * NH])
        gst = sb("gst", [P, KC, 12])
        gmv = sb("gmv", [P, KC, 2])
        ggm = sb("ggm", [P, KC, 2])
        gd = sb("gd", [P, KC])
        gd2 = sb("gd2", [P, KC])
        gve = sb("gve", [P, KC])
        gr = sb("gr", [P, KC])
        lst = sb("lst", [P, 8, 6])
        lmv = sb("lmv", [P, 8, 2])
        lve = sb("lve", [P, 8])
        lr = sb("lr", [P, 8])
        mhalf = sb("mhalf", [P, 8])
        zero = sb("zero", [P, 2 * N])
        nat = u_ring[:, 0, 0:NH * 768].rearrange("p (k o) -> p k o", k=NH)
        low = u_ring[0:R, 1, 0:6 * D].rearrange("p (a s o) -> p a s o", a=2, s=3)
        bank = ctx.enter_context(nc.psum_tensor(f"{tag}_bank", [P, 8 * BANK], F32))
        BANK_B, BANK_T, BANK_C, BANK_X = 4, 5, 6, 3

        def bk(i, n=BANK):
            return bank[:, i * BANK:i * BANK + n]

        def w(name):
            a, n = W_COLS[name]
            return W[:, a:a + n]

        inz = w("inz").rearrange("p (k o) -> p k o", k=KC)
        c2T = w("c2").rearrange("p (k t o) -> p k t o", k=NH, t=4)
        c3T = w("c3").rearrange("p (k t o) -> p k t o", k=NH, t=4)
        outT = w("out").rearrange("p (k o) -> p k o", k=NH)
        xwT = {s: w(f"xw{s}").rearrange("p (k o) -> p k o", k=NH) for s in "123"}

        PASSES = [("3", f3, L3, "fb", "3"), ("2", f2, L2, "fb", "2"), ("1f", f1, L1, "f", "1"), ("1b", f1, L1, "b", "2")]
        LN_BLOCKS = [2, 4, 8, 8]
        CH, FIRST, END = [], [], []
        ITEMS = 0
        for pi, (key, f, L, dirs, s) in enumerate(PASSES):
            FIRST.append(len(CH))
            for n0 in range(0, N, 1024 // L):
                CH.append(dict(key=key, L=L, dirs=dirs, n0=n0, ns=1024 // L, pi=pi, item=ITEMS, wset=s,
                               in_item=ITEMS + len(dirs) - 1))
                ITEMS += len(dirs)
            END.append(ITEMS)
        NCH = len(CH)
        round_of_4, round_of_3 = [0, 1, 2, 3], [1, 2, 3]
        SLOT = [2, 3] + [0, 1, 2, 3] * 2 + 2 * (round_of_4 * 2 + round_of_3) + round_of_4 * 2 + [0, 1]
        assert len(SLOT) == ITEMS
        served = {}
        for i, c in enumerate(CH):
            c["scan0"] = sum(len(q["dirs"]) for q in CH[:i])
            c["pad_a"] = i - FIRST[c["pi"]] < NA and c["pi"] != 3
            c["pad_u"] = served.get(SLOT[c["in_item"]]) != c["L"]
            for it in range(c["item"], c["in_item"] + 1):
                served[SLOT[it]] = c["L"]
        for i, c in enumerate(CH):
            c["a_done"] = sum(q["pad_a"] + q["ns"] * NH for q in CH[:i + 1])
            c["u_done"] = sum(q["pad_u"] + 1 for q in CH[:i + 1])
            c["b_buf"] = i % 3 if i < NCH - 1 else 1
        SCANS = sum(len(c["dirs"]) for c in CH)
        PER_DA, PER_DBX = CH[-1]["a_done"], CH[-1]["u_done"]

        A_TILES = ["gm", "gd", "f1_0", "f1_1", "f1_2", "f1_3", "f2", "f3", "x23", "p2",
                   "p1f_0", "p1f_1", "p1f_2"]
        P_TILES = ["p1f_3", "z_0", "z_1", "z_2", "z_3", "p1b_0", "p1b_1", "p1b_2", "p1b_3", "xd1b"]
        OUTS = (0, 2, 4, 6, 1, 3, 5, 7)
        Z_TILES = ["n2", "n3", "nf_0", "nf_1", "nf_2", "nf_3", "nb_0", "nb_2", "nb_1", "nb_3"] + [f"out_{j}" for j in OUTS]
        PIECES = {"x23": 0, "p2": 1} | {f"p1f_{i}": 2 + i for i in range(4)} | {f"p1b_{i}": 6 + i for i in range(4)}
        NPC = len(PIECES)

        const_in = sem("const_in")
        const_set = sem("const_set")
        expA = sem("expA")
        bias_step = sem("bias_step")
        comp_full = sem("comp_full")
        x_arrived = sem("x_arrived")
        res_in = [sem(f"res_in{i}") for i in range(2)]
        stored = [sem(f"stored{i}") for i in range(2)]
        gn_step = sem("gn_step")
        gn_rstd = sem("gn_rstd")
        xn_done = sem("xn_done")
        a_full, p_full, z_full = sem("a_full"), sem("p_full"), sem("z_full")
        a_act, p_act, z_act = sem("a_act"), sem("p_act"), sem("z_act")
        a_dve, z_dve = sem("a_dve"), sem("z_dve")
        sp_exp = sem("sp_exp")
        sp_ln = sem("sp_ln")
        sp_step = sem("sp_step")
        delta_done = sem("delta_done")
        dx_done = sem("dx_done")
        silu_done = sem("silu_done")
        bb_full = sem("bb_full")
        bsb_full = sem("bsb_full")
        cb_full = sem("cb_full")
        da_full = sem("da_full")
        dbx_full = sem("dbx_full")
        xd_done = sem("xd_done")
        scan_done = sem("scan_done")
        hc_full = sem("hc_full")
        tr_done = sem("tr_done")
        ln_st = sem("ln_st")
        ln_mv = sem("ln_mv")
        ln_ve = sem("ln_ve")
        ln_r = sem("ln_r")
        ln_done = sem("ln_done")
        up2_done = sem("up2_done")
        up1_done = sem("up1_done")
        gate_done = sem("gate_done")
        held = {e: sem(f"held_{e}") for e in ("pe", "dve", "pool", "act")}

        def hold(engine, name):
            engine.sem_inc(held[name], 1)

        def wait(engine, s, per, b, k):
            if isinstance(b, int):
                if b * per + k > 0:
                    engine.wait_ge(s, b * per + k)
            else:
                engine.wait_ge(s, b * per + k)

        FAM = {"a": (A_TILES, a_full, {"gm": "dve", "gd": "dve"}, a_act, a_dve),
               "p": (P_TILES, p_full, {}, p_act, None),
               "z": (Z_TILES, z_full, {t: "dve" for t in Z_TILES[6:]}, z_act, z_dve)}

        def family(t):
            return next(v for v in FAM.values() if t in v[0])

        def wait_full(engine, b, t):
            tiles, full, _, _, _ = family(t)
            wait(engine, full, len(tiles), b, tiles.index(t) + 1)

        def wait_empty(engine, b, t):
            tiles, _, by, s_act, s_dve = family(t)
            who = by.get(t, "act")
            mine = [q for q in tiles if by.get(q, "act") == who]
            wait(engine, s_act if who == "act" else s_dve, len(mine), b, mine.index(t) + 1)

        def full_sem(t):
            return family(t)[1]

        def empty_sem(t):
            _, _, by, s_act, s_dve = family(t)
            return s_act if by.get(t, "act") == "act" else s_dve

        def wait_slot(engine, b, it):
            earlier = [j for j in range(it) if SLOT[j] == SLOT[it]]
            if earlier:
                wait(engine, tr_done, ITEMS, b, earlier[-1] + 1)
            else:
                wait(engine, tr_done, ITEMS, b, max(j for j in range(ITEMS) if SLOT[j] == SLOT[it]) + 1 - ITEMS)

        def seg(buf, ns, L):
            return buf[:, 0:ns * NH * (L + 1)].rearrange("p (n h l) -> p n h l", h=NH, l=L + 1)

        def piece(t):
            if t == "x23":
                return "3", [(3 * 2 * N + h * L3, h, 0, L3) for h in range(NH)]
            if t == "p2":
                return "2", [(h * L2, h, 0, L2) for h in range(NH)]
            i = int(t[-1])
            return t[1:3], [(0, i // 2, (i % 2) * BANK, BANK)]

        U_BUF = [0, 1, 2, 3, 0, 1, 2, 3, 0, 1]

        def piece_view(a, t):
            key, parts = piece(t)
            if len(parts) == 2:
                return a[key][:].rearrange("p h l -> p (h l)")
            return a[key][:, parts[0][1], parts[0][2]:parts[0][2] + BANK]

        def fillers(z_before, a_next):
            at = {c: [] for c in range(NCH)}
            if z_before:
                at[1] += ["nb_0", "nb_2"]
                at[2] += ["nb_1", "nb_3"]
                at[3] += [f"out_{j}" for j in OUTS[:2]]
                at[4] += [f"out_{j}" for j in OUTS[2:6]]
                at[5] += [f"out_{j}" for j in OUTS[6:]]
            for i in range(4):
                at[7 + i] += [f"z_{i}"]
                at[11 + i] += [f"p1b_{i}"]
            at[6] += ["n2"]
            at[16] += ["xd1b"]
            at[19] += ["n3"]
            if a_next:
                at[15] += ["gm"]
                at[17] += ["gd"]
                for i in range(4):
                    at[21 + i] += [f"f1_{i}"]
                at[25] += ["f2/0"]
                at[26] += ["f2/1"]
                at[27] += ["f3"]
                at[29] += ["x23"]
                at[31] += ["p2"]
                for i in range(3):
                    at[34 + i] += [f"p1f_{i}"]
            at[0] += ["p1f_3"]
            for i, c in enumerate((28, 30, 32, 33)):
                at[c] += [f"nf_{i}"]
            return at

        def bank_of(t, ci):
            kind = t.split("_")[0]
            if kind == "nb":
                return BANK_T if t in ("nb_0", "nb_1") else BANK_X
            if kind == "out":
                return BANK_X - OUTS.index(int(t[-1])) % 2
            return BANK_T

        OFFSET = {t: 1 for t in A_TILES} | {t: 0 for t in P_TILES} | {t: 0 for t in Z_TILES[:6]} | {t: -1 for t in Z_TILES[6:]}

        def emptied_by(who, at, c):
            out = []
            for t in at.get(c, []):
                name, _, part = t.partition("/")
                if part != "0" and (family(name)[2].get(name, "act") == who):
                    out.append(name)
            return out

        def following(b, ci, a_next):
            if ci < NCH:
                return b, ci
            return (b + 1, ci - NCH) if a_next else None

        def program(engine, prologue, body, epilogue):
            prologue()
            body(0, False, batches > 1)
            if batches > 2:
                with engine.Fori(1, batches - 1) as b:
                    body(b, True, True)
            if batches > 1:
                body(batches - 1, True, False)
            epilogue()

        block = ctx.enter_context(nc.Block())

        @block.sync
        def _(sp):
            for dst, src in ((nat, nat_dram), (low, low_dram), (W[:], w_dram), (ident[:], ident_dram), (group[:], group_dram)):
                sp.dma_start(dst, src).then_inc(const_in, 16)

            def load_x(b):
                sp.dma_start(xin[:], x_in[bass.ds(b, 1)].rearrange("a (k p) l -> p (a k) l", p=P)).then_inc(x_arrived, 16)

            def tile_of(x, b, j):
                return x[bass.ds(b, 1), (j // 2) * P:(j // 2 + 1) * P, (j % 2) * BANK:(j % 2 + 1) * BANK].rearrange("a p l -> (a p) l")

            def load_res(b, i):
                wait(sp, stored[i % 2], 64, b, 16 * (i // 2))
                sp.dma_start(xres[:, i % 2, :], tile_of(x_in, b, OUTS[i])).then_inc(res_in[i % 2], 16)

            def results(b):
                load_res(b, 0)
                load_res(b, 1)
                for i, j in enumerate(OUTS):
                    wait_empty(sp, b, f"out_{j}")
                    sp.dma_start(tile_of(x_out, b, j), xres[:, i % 2, :]).then_inc(stored[i % 2], 16)
                    if i < 6:
                        load_res(b, i + 2)

            def body(b, z_before, a_next):
                if z_before:
                    results(b - 1)
                if a_next:
                    wait_full(sp, b, "z_3")
                    load_x(b + 1)

            program(sp, lambda: load_x(0), body, lambda: results(batches - 1))
            for i in range(2):
                sp.wait_ge(stored[i], batches * 64)

        @block.tensor
        def _(pe):
            mm = nc.tensor.matmul
            pe.wait_ge(const_in, 80)
            for ic in range(KC):
                for k in range(NH):
                    mm(bk(ic, D), nat[:, k, ic * P:(ic + 1) * P], nat[:, k, C:C + D], start=(k == 0), stop=(k == NH - 1))
            for s in range(3):
                for k in range(NH):
                    mm(bk(4 + s)[:, k * D:(k + 1) * D], low[:, 0, s, k * P:(k + 1) * P], low[:, 1, s, :], start=True, stop=True)
            for m in range(NH):
                for k in range(NH):
                    last = mm(bk(7)[:, m:m + 1], nat[:, k, C + m * P:C + (m + 1) * P], w("in_b")[:, k:k + 1],
                              start=(k == 0), stop=(k == NH - 1))
            last.then_inc(comp_full, 1)
            pe.wait_ge(const_set, 4)

            def x_blocks(ps, s):
                for lb in range(NB):
                    for k in range(NH):
                        last = mm(ps[:, lb * 2 * N:(lb + 1) * 2 * N], f1[:, k, lb * P:(lb + 1) * P], xwT[s][:, k, :],
                                  start=(k == 0), stop=(k == NH - 1))
                return last

            before = {}

            def tile(b, t, bi=BANK_T):
                name, _, part = t.partition("/")
                tb = b + OFFSET[name]
                if part in ("", "0"):
                    if before.get(bi) is not None:
                        wait_empty(pe, *before[bi])
                    before[bi] = (tb, name)
                    needs(tb, name)
                ps = bk(bi)
                last = None
                kind = name.split("_")[0]
                i = int(name.split("_")[1]) if "_" in name else 0
                h, q = i // 2, i % 2
                if name == "gm":
                    last = mm(ps[:, 0:2 * KC], group[:], gmv[:].rearrange("p k s -> p (k s)"), start=True, stop=True)
                elif name == "gd":
                    last = mm(ps[:, 0:KC], group[:], gd2[:], start=True, stop=True)
                elif kind in ("f1", "z"):
                    ks = {"": range(KC), "0": range(0, 2), "1": range(2, KC)}[part]
                    wt = wc if kind == "f1" else inz
                    for k in ks:
                        last = mm(ps, wt[:, k, h * P:(h + 1) * P], xin[:, k, q * BANK:(q + 1) * BANK],
                                  start=(k == 0), stop=(k == KC - 1))
                elif kind in ("f2", "f3"):
                    src, wT, width = (f1, c2T, 32) if kind == "f2" else (f2, c3T, 16)
                    half = width // 2
                    for m in {"": range(NH), "0": range(1), "1": range(1, NH)}[part]:
                        j = 0
                        for k in range(NH):
                            v = src[:, k, :].rearrange("p (h y w x) -> p y x h w", y=2, x=2, w=half)
                            for tap in range(4):
                                last = mm(ps[:, m * half * half:(m + 1) * half * half].rearrange("p (h w) -> p h w", w=half),
                                          wT[:, k, tap, m * P:(m + 1) * P], v[:, tap // 2, tap % 2], start=(j == 0), stop=(j == 7))
                                j += 1
                elif name == "x23":
                    x_blocks(ps[:, 3 * 2 * N + NH * L3:], "1")
                    for k in range(NH):
                        mm(ps[0:L3, 0:2 * N], f3[:, k, :], xwT["3"][:, k, :], start=(k == 0), stop=(k == NH - 1))
                    for lb in range(2):
                        for k in range(NH):
                            mm(ps[:, (1 + lb) * 2 * N:(2 + lb) * 2 * N], f2[:, k, lb * P:(lb + 1) * P], xwT["2"][:, k, :],
                               start=(k == 0), stop=(k == NH - 1))
                    for m in range(NH):
                        for k in range(NH):
                            last = mm(ps[:, 3 * 2 * N + m * L3:3 * 2 * N + (m + 1) * L3], wd[:, 2, k, m * P:(m + 1) * P], f3[:, k, :],
                                      start=(k == 0), stop=(k == NH - 1))
                elif name == "p2":
                    for m in range(NH):
                        for k in range(NH):
                            last = mm(ps[:, m * L2:(m + 1) * L2], wd[:, 1, k, m * P:(m + 1) * P], f2[:, k, :],
                                      start=(k == 0), stop=(k == NH - 1))
                elif kind == "xd1b":
                    last = x_blocks(ps, "2")
                elif kind in ("p1f", "p1b"):
                    for k in range(NH):
                        last = mm(ps, wd[:, 0 if kind == "p1f" else 1, k, h * P:(h + 1) * P], f1[:, k, q * BANK:(q + 1) * BANK],
                                  start=(k == 0), stop=(k == NH - 1))
                elif name in ("n3", "n2"):
                    L, key = (L3, "3") if name == "n3" else (L2, "2")
                    rows, nlb = min(L, P), max(1, L // P)
                    if name == "n3":
                        hold(pe, "pe")
                    for m in range(NH):
                        for lb in range(nlb):
                            for d in range(2):
                                last = mm(ps[:, m * L + lb * rows:m * L + (lb + 1) * rows],
                                          hn[key][0:rows, d * nlb + lb, m * P:(m + 1) * P], ident[0:rows, 0:rows],
                                          start=(m == 0 and lb == 0 and d == 0),
                                          stop=(m == NH - 1 and lb == nlb - 1 and d == 1), is_transpose=True)
                elif kind in ("nf", "nb"):
                    for j in range(4):
                        last = mm(ps[:, j * P:(j + 1) * P], hn_buf[:, 4 * q + j, h * P:(h + 1) * P], ident[:],
                                  start=(j == 0), stop=(j == 3), is_transpose=True)
                elif kind == "out":
                    for k in range(NH):
                        last = mm(ps, outT[:, k, h * P:(h + 1) * P], out1[:, k, q * BANK:(q + 1) * BANK],
                                  start=(k == 0), stop=(k == NH - 1))
                if part in ("", "1"):
                    last.then_inc(full_sem(name), 1)

            def needs(tb, name):
                kind = name.split("_")[0]
                if name == "gm":
                    wait(pe, gn_step, 15, tb, 12)
                elif name == "gd":
                    wait(pe, gn_step, 15, tb, 14)
                elif kind == "f1":
                    wait(pe, xn_done, KC, tb, KC)
                elif name == "f2":
                    wait_empty(pe, tb, "f1_3")
                elif name == "f3":
                    wait_empty(pe, tb, "f2")
                elif name == "x23":
                    wait_empty(pe, tb, "f3")
                elif name in ("n3", "n2"):
                    wait(pe, ln_done, 4, tb, 2)
                elif kind == "nf":
                    wait(pe, ln_done, 4, tb, 3)
                elif kind == "nb":
                    wait(pe, ln_done, 4, tb, 4)
                elif kind == "out":
                    wait(pe, gate_done, 4, tb, 2 + 2 * (int(name[-1]) % 2))

            def broadcast(c, bi, col, halves):
                key, L = c["key"], c["L"]
                rows = min(L, P)
                if rows < P:
                    hold(pe, "pe")
                for hf in halves:
                    for o in range(0, BANK, rows):
                        at = hf * BANK + o
                        i, lb = at // L, (at % L) // rows
                        src = bct[key][0:rows, lb, col + c["n0"] + i:col + c["n0"] + i + 1].broadcast_to([rows, P])
                        oo = bi * BANK + (at if len(halves) == 2 else o)
                        last = mm(bank[:, oo:oo + rows], src, ident[0:rows, 0:rows],
                                  start=(o == 0), stop=(o == BANK - rows), is_transpose=True)
                return last

            def b_half(b, ci, hf):
                c = CH[ci]
                if hf == 0 and ci == FIRST[c["pi"]]:
                    wait_empty(pe, b, {"3": "x23", "2": "x23", "1f": "x23", "1b": "xd1b"}[c["key"]])
                wait(pe, bsb_full, 2 * NCH, b, 2 * ci + hf)
                broadcast(c, BANK_B, 0, [hf]).then_inc(bb_full, 1)

            def y_place(L, d, lb, h):
                if L == L1:
                    bi, col, first, last = lb // 2, (lb % 2) * D, lb % 2 == 0, lb % 2 == 1
                elif L == L2:
                    bi, col, first, last = int(d == "b"), lb * D, lb == 0, lb == L2 // P - 1
                else:
                    bi, col, first, last = 2, int(d == "b") * D, d == "f", d == "b"
                return bi * BANK + col + h * P, first and h == 0, last and h == NH - 1

            def add_item(src, L, d, final):
                rows, nlb = min(L, P), max(1, L // P)
                for i in range(src.shape[1]):
                    for h in range(NH):
                        for lb in range(nlb):
                            o, _, end = y_place(L, d, lb, h)
                            last = mm(bank[0:rows, o:o + P], src[:, i, h, 1 + lb * rows:1 + (lb + 1) * rows], ident[:, :],
                                      start=False, stop=final and i == src.shape[1] - 1 and end, is_transpose=True)
                return last

            def items(b, ci):
                c = CH[ci]
                for j, d in enumerate(c["dirs"]):
                    wait(pe, hc_full, SCANS, b, c["scan0"] + j + 1)
                    if c["L"] == L3:
                        hold(pe, "pe")
                    add_item(seg(u_ring[:, SLOT[c["item"] + j], :], c["ns"], c["L"]), c["L"], d,
                             c["n0"] + c["ns"] == N).then_inc(tr_done, 1)

            def skip(b, pi):
                wait(pe, ln_done, 4, b, pi if pi > 1 else 0)
                for bi in (BANK_X - 1, BANK_X):
                    if pi == 2 and before.get(bi) is not None:
                        wait_empty(pe, *before[bi])
                        before[bi] = None
                _, f, L, dirs, s = PASSES[pi]
                rows, nlb = min(L, P), max(1, L // P)
                for d in dirs:
                    for lb in range(nlb):
                        for h in range(NH):
                            o, first, _ = y_place(L, d, lb, h)
                            last = mm(bank[0:rows, o:o + P], f[:, h, lb * rows:(lb + 1) * rows], diag[:, int(s) - 1, h, :],
                                      start=first, stop=False)
                last.then_inc(xd_done, 1)

            def body(b, z_before, a_next):
                before.clear()
                before[BANK_T] = (b, "p1f_2")
                at = fillers(z_before, a_next)
                for ci in range(NCH):
                    wait(pe, hc_full, SCANS, b, CH[ci]["scan0"])
                    broadcast(CH[ci], BANK_C, N, [0, 1]).then_inc(cb_full, 1)
                    ahead = following(b, ci + 3, a_next)
                    late = ci <= FIRST[2]
                    if ahead and not late:
                        b_half(*ahead, 0)
                    if ci:
                        if ci - 1 in FIRST:
                            skip(b, CH[ci - 1]["pi"])
                        items(b, ci - 1)
                    if ahead:
                        if late:
                            b_half(*ahead, 0)
                        b_half(*ahead, 1)
                    for t in at[ci]:
                        tile(b, t, bank_of(t, ci))
                items(b, NCH - 1)

            def prologue():
                for t in A_TILES:
                    tile(-1, t)
                for ci in range(3):
                    for hf in range(2):
                        b_half(0, ci, hf)

            def epilogue():
                before.clear()
                for t in Z_TILES[6:]:
                    tile(batches, t, bank_of(t, NCH))

            program(pe, prologue, body, epilogue)

        @block.scalar
        def _(act):
            A = nc.scalar.activation
            act.wait_ge(const_in, 80)
            a0 = W_COLS["Al1"][0]
            A(negA[:], W[:, a0:a0 + 3 * NH * N], ACT.Exp).then_inc(expA, 1)
            act.wait_ge(const_set, 4)

            def softplus(b, t):
                key, parts = piece(t)
                s = {"3": "3", "2": "2", "1f": "1", "1b": "2"}[key]
                k = PIECES[t]
                u = T_u[:, U_BUF[k], :]
                used = [q for q in range(k) if U_BUF[q] == U_BUF[k]]
                wait(act, sp_step, 4 * NPC, b, 4 * (used[-1] + 1) if used else 0)
                n = 0
                for col, h, p0, m in parts:
                    bias = w(f"dtb{s}")[:, h:h + 1]
                    A(u[:, n:n + m], bk(BANK_T)[:, col:col + m], ACT.Abs, bias=bias)
                    last = A(delta[key][:, h, p0:p0 + m], bk(BANK_T)[:, col:col + m], ACT.Relu, bias=bias)
                    n += m
                last.then_inc(empty_sem(t), 1)
                wait_empty(act, b, t)
                A(u[:, 0:n], u[:, 0:n], ACT.Exp, scale=-1.0).then_inc(sp_exp, 1)

            def logs(b, t):
                k = PIECES[t]
                wait(act, sp_exp, NPC, b, k + 1)
                for q, tq in ((k - 1, list(PIECES)[k - 1]), (k, t)):
                    dst = piece_view(dx, tq)
                    A(dst, T_u[:, U_BUF[q], 0:dst.shape[1]], ACT.Ln, bias=1.0).then_inc(sp_ln, 1)

            def after_empty(b, name):
                if name == "z_3":
                    wait_empty(act, b, name)
                    A(z[:].rearrange("p h l -> p (h l)"), z[:].rearrange("p h l -> p (h l)"), ACT.Silu).then_inc(silu_done, 1)
                elif name in PIECES and PIECES[name] % 2 == 1:
                    logs(b, name)

            def empty(b, name):
                wait_full(act, b, name)
                kind = name.split("_")[0]
                i = int(name.split("_")[1]) if "_" in name else 0
                h, q = i // 2, i % 2
                ps = bk(BANK_T)
                if name == "f1_0":
                    wait(act, dx_done, NPC, b, 0)
                    wait(act, xd_done, 4, b, 0)
                if name == "z_0":
                    wait(act, gate_done, 4, b, 0)
                if kind == "f1":
                    A(f1[:, h, q * BANK:(q + 1) * BANK], ps, ACT.Identity, bias=f1_b[:, h:h + 1]).then_inc(a_act, 1)
                elif kind == "z":
                    A(z[:, h, q * BANK:(q + 1) * BANK], ps, ACT.Identity, bias=w("in_b")[:, NH + h:NH + h + 1]).then_inc(p_act, 1)
                elif kind in ("f2", "f3"):
                    dst, L, bias = (f2, L2, w("c2_b")) if kind == "f2" else (f3, L3, w("c3_b"))
                    for m in range(NH):
                        last = A(dst[:, m, :], ps[:, m * L:(m + 1) * L], ACT.Identity, bias=bias[:, m:m + 1])
                    last.then_inc(a_act, 1)
                elif name == "x23":
                    A(bct["3"][0:L3, 0, :], ps[0:L3, 0:2 * N], ACT.Copy)
                    A(bct["2"][:].rearrange("p a n -> p (a n)"), ps[:, 2 * N:6 * N], ACT.Copy)
                    x1 = 3 * 2 * N + NH * L3
                    A(bct["1f"][:].rearrange("p a n -> p (a n)"), ps[:, x1:x1 + NB * 2 * N], ACT.Copy)
                    softplus(b, name)
                elif kind == "xd1b":
                    A(bct["1b"][:].rearrange("p a n -> p (a n)"), ps[:, 0:NB * 2 * N], ACT.Copy).then_inc(empty_sem(name), 1)
                elif kind in ("p2", "p1f", "p1b"):
                    softplus(b, name)
                elif name == "n3":
                    wait(act, up2_done, 1, b, 0)
                    for m in range(NH):
                        last = A(y3s[:, m, :], ps[:, m * L3:(m + 1) * L3], ACT.Identity, scale=w("g3")[:, m:m + 1], bias=bt[:, m:m + 1])
                    last.then_inc(z_act, 1)
                elif name == "n2":
                    wait(act, up1_done, 4, b, 0)
                    for m in range(NH):
                        last = A(y2s[:, m, :], ps[:, m * L2:(m + 1) * L2], ACT.Copy, scale=w("g2")[:, m:m + 1])
                    last.then_inc(z_act, 1)
                elif kind == "nf":
                    A(out1[:, h, q * BANK:(q + 1) * BANK], ps, ACT.Copy, scale=w("g1")[:, h:h + 1]).then_inc(z_act, 1)

            def copy_b(b, ci, halves):
                buf = CH[ci]["b_buf"]
                used = [q for q in range(ci) if CH[q]["b_buf"] == buf]
                last = used[-1] if used else max(q for q in range(NCH) if CH[q]["b_buf"] == buf)
                for hf in halves:
                    wait(act, bb_full, 2 * NCH, b, 2 * ci + hf + 1)
                    if hf == 0:
                        wait(act, dbx_full, PER_DBX, b, CH[last]["u_done"] - (0 if used else PER_DBX))
                    A(b_sb[:, buf, hf * BANK:(hf + 1) * BANK], bk(BANK_B), ACT.Copy).then_inc(bsb_full, 1)

            def decays(b, ci):
                c = CH[ci]
                wait(act, delta_done, NPC, b, {"3": 1, "2": 2, "1f": 6, "1b": 10}[c["key"]])
                wait(act, scan_done, SCANS, b, CH[ci - NA]["scan0"] + len(CH[ci - NA]["dirs"]) if ci >= NA else 0)
                slot = seg(dA_ring[:, ci % NA, :], c["ns"], c["L"])
                if c["pad_a"]:
                    A(slot[:, :, :, 0], zero[:, 0:c["ns"] * NH].rearrange("p (n h) -> p n h", h=NH), ACT.Copy).then_inc(da_full, 1)
                for i in range(c["ns"]):
                    for h in range(NH):
                        col = (int(c["wset"]) - 1) * NH * N + h * N + c["n0"] + i
                        A(slot[:, i, h, 1:], delta[c["key"]][:, h, :], ACT.Exp, scale=negA[:, col:col + 1]).then_inc(da_full, 1)

            def body(b, z_before, a_next):
                at = fillers(z_before, a_next)
                if z_before:
                    empty(b, "p1f_1")
                for ci in range(NCH):
                    decays(b, ci)
                    ahead = following(b, ci + 2, a_next)
                    if ahead:
                        copy_b(*ahead, (0,))
                    for t in emptied_by("act", at, ci - 2):
                        empty(b + OFFSET[t], t)
                    if ci == 0 and z_before:
                        empty(b, "p1f_2")
                    if ahead:
                        copy_b(*ahead, (1,))
                    for t in emptied_by("act", at, ci - 3):
                        after_empty(b + OFFSET[t], t)
                    if ci == 0 and z_before:
                        logs(b, "p1f_1")

            def prologue():
                for t in A_TILES[2:]:
                    empty(0, t)
                    after_empty(0, t)
                copy_b(0, 0, (0, 1))
                copy_b(0, 1, (0, 1))

            program(act, prologue, body, lambda: None)

        @block.gpsimd
        def _(pool):
            G = nc.gpsimd
            G.memset(mhalf[:], -0.5).then_inc(const_set, 1)
            pool.wait_ge(const_set, 4)

            def group_rstd(b):
                wait(pool, gn_step, 15, b, 15)
                G.tensor_tensor(gr[:], gve[:], mhalf[:, 0:KC], ALU.pow).then_inc(gn_rstd, 1)

            def norm_rstd(b, pi):
                wait(pool, ln_ve, 4, b, pi + 1)
                rows, nb = min(PASSES[pi][2], P), LN_BLOCKS[pi]
                G.tensor_tensor(lr[0:rows, 0:nb], lve[0:rows, 0:nb], mhalf[0:rows, 0:nb], ALU.pow).then_inc(ln_r, 1)

            def step_sizes(b, t):
                key, parts = piece(t)
                f = {"3": f3, "2": f2}.get(key, f1)
                k = PIECES[t]
                d, x_ = piece_view(delta, t), piece_view(dx, t)
                parts_f = f[:].rearrange("p h l -> p (h l)") if len(parts) == 2 else f[:, parts[0][1], parts[0][2]:parts[0][2] + BANK]
                wait(pool, sp_step, 4 * NPC, b, 4 * k + 4)
                G.tensor_tensor(d, x_, d, ALU.add).then_inc(delta_done, 1)
                wait(pool, delta_done, NPC, b, k + 1)
                G.tensor_tensor(x_, d, parts_f, ALU.mult).then_inc(dx_done, 1)

            def inputs(b, ci):
                c = CH[ci]
                key, L, ns = c["key"], c["L"], c["ns"]
                wait(pool, dx_done, NPC, b, {"3": 1, "2": 2, "1f": 6, "1b": 10}[key])
                wait_slot(pool, b, c["in_item"])
                slot = seg(u_ring[:, SLOT[c["in_item"]], :], ns, L)
                if c["pad_u"]:
                    hold(pool, "pool")
                    G.memset(slot[:, :, :, 0], 0.0).then_inc(dbx_full, 1)
                wait(pool, bsb_full, 2 * NCH, b, 2 * ci + 2)
                shape = [P, ns, NH, L]
                G.tensor_tensor(slot[:, :, :, 1:], dx[key][:].unsqueeze(1).broadcast_to(shape),
                                b_sb[:, c["b_buf"], :].rearrange("p (n l) -> p n l", l=L).unsqueeze(2).broadcast_to(shape),
                                ALU.mult).then_inc(dbx_full, 1)

            def enlarge(dst, src, width, y0, y1):
                for dy in range(2):
                    v = dst.rearrange("p (h y w x) -> p h y w x", y=2, x=2, w=width)[:, y0:y1, dy]
                    s_ = src.rearrange("p (h w) -> p h w", w=width)[:, y0:y1]
                    last = G.tensor_tensor(v, v, s_.unsqueeze(3).broadcast_to([P, y1 - y0, width, 2]), ALU.add)
                return last

            def add_and_gate(b, q):
                wait(pool, up2_done, 1, b, 1)
                wait(pool, silu_done, 1, b, 1)
                for h in range(NH):
                    wait_empty(pool, b, f"nb_{2 * h + q}")
                    enlarge(out1[:, h, :], y2s[:, h, :], 16, 8 * q, 8 * q + 8).then_inc(up1_done, 1)
                wait(pool, up1_done, 4, b, 2 * q + 2)
                for h in range(NH):
                    o = out1[:, h, q * BANK:(q + 1) * BANK]
                    G.tensor_tensor(o, o, z[:, h, q * BANK:(q + 1) * BANK], ALU.mult).then_inc(gate_done, 1)

            def body(b, z_before, a_next):
                for ci in range(NCH):
                    inputs(b, ci)
                    if ci in (2, 4):
                        step_sizes(b, f"p1f_{ci - 2}")
                        step_sizes(b, f"p1f_{ci - 1}")
                    if ci == 1 and z_before:
                        norm_rstd(b - 1, 3)
                    if ci in (2, FIRST[2] + 1, FIRST[3] + 1):
                        norm_rstd(b, {2: 0, FIRST[2] + 1: 1, FIRST[3] + 1: 2}[ci])
                    if ci in (3, 4) and z_before:
                        add_and_gate(b - 1, ci - 3)
                    if ci == 23:
                        wait_empty(pool, b, "n3")
                        for h in range(NH):
                            last = enlarge(y2s[:, h, :], y3s[:, h, :], 8, 0, 8)
                        last.then_inc(up2_done, 1)
                    if ci == 16:
                        step_sizes(b, "p1b_0")
                        step_sizes(b, "p1b_1")
                    if ci == 19:
                        step_sizes(b, "p1b_2")
                        step_sizes(b, "p1b_3")
                    if a_next:
                        if ci == 19:
                            group_rstd(b + 1)
                        if ci == 36:
                            step_sizes(b + 1, "x23")
                            step_sizes(b + 1, "p2")

            def prologue():
                group_rstd(0)
                step_sizes(0, "x23")
                step_sizes(0, "p2")

            def epilogue():
                norm_rstd(batches - 1, 3)
                add_and_gate(batches - 1, 0)
                add_and_gate(batches - 1, 1)

            program(pool, prologue, body, epilogue)

        @block.vector
        def _(dve):
            V = nc.vector
            V.memset(zero[:], 0.0).then_inc(const_set, 1)
            dve.wait_ge(const_in, 80)
            dve.wait_ge(comp_full, 1)
            for k in range(KC):
                V.tensor_copy(wc[:, k, :], bk(k, D))
            for s in range(3):
                V.tensor_copy(wd[:, s].rearrange("p k o -> p (k o)"), bk(4 + s))
            V.tensor_tensor(f1_b[:], bk(7)[:, 0:NH], w("c1_b"), ALU.add)
            for s in range(3):
                for h in range(NH):
                    V.tensor_scalar(diag[:, s, h, :], ident[:], w(f"Dv{s + 1}")[:, h:h + 1], None, ALU.mult)
            dve.wait_ge(expA, 1)
            V.tensor_scalar(negA[:], negA[:], -1.0, None, ALU.mult).then_inc(const_set, 1)
            t_ = [bt[:, NH * i:NH * i + NH] for i in range(4)]
            V.tensor_scalar(t_[1], w("be2"), 3.0, None, ALU.mult).then_inc(bias_step, 1)
            V.tensor_scalar(t_[2], w("be3"), 2.0, None, ALU.mult).then_inc(bias_step, 1)
            dve.wait_ge(bias_step, 2)
            V.tensor_tensor(t_[3], t_[1], t_[2], ALU.add).then_inc(bias_step, 1)
            dve.wait_ge(bias_step, 3)
            V.tensor_tensor(t_[0], t_[3], w("be1"), ALU.add).then_inc(const_set, 1)

            def group_stats(b, k):
                wait(dve, x_arrived, 16, b, 16)
                for q in range(2):
                    V.bn_stats(gst[:, k, 6 * q:6 * q + 6], xin[:, k, q * BANK:(q + 1) * BANK]).then_inc(gn_step, 1)

            def group_aggregate(b):
                wait(dve, gn_step, 15, b, 8)
                hold(dve, "dve")
                for k in range(KC):
                    V.bn_aggr(gmv[:, k, :], gst[:, k, :]).then_inc(gn_step, 1)

            def group_mean(b):
                wait_full(dve, b, "gm")
                V.tensor_copy(ggm[:].rearrange("p k s -> p (k s)"), bk(BANK_T)[:, 0:2 * KC]).then_inc(a_dve, 1)
                wait_empty(dve, b, "gm")
                V.tensor_tensor(gd[:], gmv[:, :, 0], ggm[:, :, 0], ALU.subtract).then_inc(gn_step, 1)
                wait(dve, gn_step, 15, b, 13)
                V.tensor_tensor(gd2[:], gd[:], gd[:], ALU.mult).then_inc(gn_step, 1)

            def group_var(b):
                wait_full(dve, b, "gd")
                V.tensor_tensor(gve[:], bk(BANK_T)[:, 0:KC], ggm[:, :, 1], ALU.add).then_inc(a_dve, 1)
                wait_empty(dve, b, "gd")
                V.tensor_scalar(gve[:], gve[:], EPS, None, ALU.add).then_inc(gn_step, 1)

            def normalise(b, k):
                wait(dve, gn_rstd, 1, b, 1)
                V.tensor_scalar(xin[:, k, :], xin[:, k, :], ggm[:, k, 0:1], gr[:, k:k + 1],
                                ALU.subtract, ALU.mult).then_inc(xn_done, 1)

            def log1p(b, t):
                k = PIECES[t]
                ln = piece_view(dx, t)
                n = ln.shape[1]
                u = T_u[:, U_BUF[k], 0:n]
                wait(dve, sp_exp, NPC, b, k + 1)
                wait(dve, sp_step, 4 * NPC, b, 4 * k)
                V.tensor_scalar(T_c[:, 0:n], u, 1.0, 1.0, ALU.add, ALU.subtract).then_inc(sp_step, 1)
                wait(dve, sp_step, 4 * NPC, b, 4 * k + 1)
                V.tensor_tensor(T_c[:, 0:n], u, T_c[:, 0:n], ALU.subtract).then_inc(sp_step, 1)
                wait(dve, sp_step, 4 * NPC, b, 4 * k + 2)
                wait(dve, sp_ln, NPC, b, k + 1)
                V.tensor_tensor(ln, ln, T_c[:, 0:n], ALU.add).then_inc(sp_step, 1)
                wait(dve, sp_step, 4 * NPC, b, 4 * k + 3)
                V.tensor_tensor(ln, ln, u, ALU.min).then_inc(sp_step, 1)

            def norm_blocks(pi):
                rows, first = min(PASSES[pi][2], P), 2 * BANK if PASSES[pi][2] == L3 else 0
                return rows, [bank[0:rows, first + j * D:first + (j + 1) * D] for j in range(LN_BLOCKS[pi])]

            def norm_stats(b, pi):
                rows, blocks = norm_blocks(pi)
                nb, at, total = LN_BLOCKS[pi], sum(LN_BLOCKS[:pi]), sum(LN_BLOCKS)
                wait(dve, tr_done, ITEMS, b, END[pi])
                for j in range(nb):
                    V.bn_stats(lst[0:rows, j, :], blocks[j]).then_inc(ln_st, 1)
                wait(dve, ln_st, total, b, at + nb)
                hold(dve, "dve")
                for j in range(nb):
                    V.bn_aggr(lmv[0:rows, j, :], lst[0:rows, j, :]).then_inc(ln_mv, 1)
                wait(dve, ln_mv, total, b, at + nb)
                V.tensor_scalar(lve[0:rows, 0:nb], lmv[0:rows, 0:nb, 1], EPS, None, ALU.add).then_inc(ln_ve, 1)

            def norm_apply(b, pi):
                rows, blocks = norm_blocks(pi)
                key = PASSES[pi][0]
                wait(dve, ln_r, 4, b, pi + 1)
                if pi == 0:
                    wait_full(dve, b - 1, "nb_2")
                if pi == 2:
                    wait_full(dve, b, "n3")
                if pi == 3:
                    wait_full(dve, b, "nf_3")
                for j, blk in enumerate(blocks):
                    last = V.tensor_scalar(hn[key][0:rows, j, :], blk, lmv[0:rows, j, 0:1], lr[0:rows, j:j + 1],
                                           ALU.subtract, ALU.mult)
                last.then_inc(ln_done, 1)

            def empty(b, name, bi):
                wait_full(dve, b, name)
                j = int(name[-1])
                h, q = j // 2, j % 2
                if name[:2] == "nb":
                    wait_empty(dve, b, "nf_3")
                    o = out1[:, h, q * BANK:(q + 1) * BANK]
                    V.scalar_tensor_tensor(o, bk(bi), w("g2")[:, h:h + 1], o, ALU.mult, ALU.add).then_inc(z_dve, 1)
                else:
                    i = OUTS.index(j)
                    wait(dve, res_in[i % 2], 64, b, 16 * (i // 2) + 16)
                    o = xres[:, i % 2, :]
                    V.scalar_tensor_tensor(o, bk(bi), w("out_b")[:, h:h + 1], o, ALU.add, ALU.add).then_inc(z_dve, 1)

            def scan(b, ci):
                c = CH[ci]
                n = c["ns"] * NH * (c["L"] + 1)
                a = dA_ring[:, ci % NA, 0:n]
                src = u_ring[:, SLOT[c["in_item"]], 0:n]
                wait(dve, da_full, PER_DA, b, c["a_done"])
                wait(dve, dbx_full, PER_DBX, b, c["u_done"])
                for j, d in enumerate(c["dirs"]):
                    dst = u_ring[:, SLOT[c["item"] + j], 0:n]
                    if len(c["dirs"]) == 2:
                        if j == 0:
                            wait_slot(dve, b, c["item"])
                        else:
                            wait(dve, scan_done, SCANS, b, c["scan0"] + 1)
                    if d == "f":
                        V.tensor_tensor_scan(dst, a, src, 0.0, ALU.mult, ALU.add).then_inc(scan_done, 1)
                    else:
                        V.tensor_tensor_scan(dst[:, ::-1], a[:, ::-1], src[:, ::-1], 0.0, ALU.mult, ALU.add).then_inc(scan_done, 1)

            def times_c(b, ci):
                c = CH[ci]
                wait(dve, cb_full, NCH, b, ci + 1)
                for j in range(len(c["dirs"])):
                    wait(dve, scan_done, SCANS, b, c["scan0"] + j + 1)
                    v = seg(u_ring[:, SLOT[c["item"] + j], :], c["ns"], c["L"])[:, :, :, 1:]
                    cc = bank[:, BANK_C * BANK:(BANK_C + 2) * BANK].rearrange("p (n l) -> p n l", l=c["L"])
                    V.tensor_tensor(v, v, cc.unsqueeze(2).broadcast_to([P, c["ns"], NH, c["L"]]), ALU.mult).then_inc(hc_full, 1)

            def body(b, z_before, a_next):
                at = fillers(z_before, a_next)
                for ci in range(NCH):
                    ended = {2: 0, FIRST[2]: 1, FIRST[3]: 2}.get(ci)
                    if ci == 0:
                        ended = 3 if z_before else None
                    eb = b if ci else b - 1
                    scan(b, ci)
                    if ended is not None:
                        norm_stats(eb, ended)
                    late = [f"out_{OUTS[i]}" for i in (0, 1, 4, 5, 6, 7)]
                    for t in (at[ci - 1] if ci else []):
                        if t[:2] == "nb" or t in late:
                            empty(b - 1, t, bank_of(t, ci))
                    if a_next and ci == 16:
                        group_mean(b + 1)
                    if a_next and ci == 18:
                        group_var(b + 1)
                    times_c(b, ci)
                    if ended is not None:
                        norm_apply(eb, ended)
                    for t in at[ci]:
                        if t[:3] == "out" and t not in late:
                            empty(b - 1, t, bank_of(t, ci))
                    if ci in (1, 3):
                        log1p(b, f"p1f_{ci - 1}")
                        log1p(b, f"p1f_{ci}")
                    if ci in (15, 17):
                        log1p(b, f"p1b_{ci - 15}")
                        log1p(b, f"p1b_{ci - 14}")
                    if a_next:
                        if ci in (13, 14):
                            group_stats(b + 1, 2 * (ci - 13))
                            group_stats(b + 1, 2 * (ci - 13) + 1)
                        if ci == 14:
                            group_aggregate(b + 1)
                        if ci in (19, 20):
                            for k in range(2):
                                normalise(b + 1, 2 * (ci - 19) + k)
                        if ci == 34:
                            log1p(b + 1, "x23")
                        if ci == 35:
                            log1p(b + 1, "p2")

            def prologue():
                for k in range(KC):
                    group_stats(0, k)
                group_aggregate(0)
                group_mean(0)
                group_var(0)
                for k in range(KC):
                    normalise(0, k)
                log1p(0, "x23")
                log1p(0, "p2")

            def epilogue():
                norm_stats(batches - 1, 3)
                norm_apply(batches - 1, 3)
                for t in Z_TILES[6:]:
                    empty(batches - 1, t, bank_of(t, NCH))

            program(dve, prologue, body, epilogue)


def conv_layer(nc, tag, x_in, x_out, taps_dram, masks_dram, ident_dram, group_dram, batches):
    ctx = ExitStack()
    with ctx:
        def sb(name, shape):
            return ctx.enter_context(nc.sbuf_tensor(f"{tag}_{name}", shape, F32))

        def sem(name):
            return ctx.enter_context(nc.semaphore(f"{tag}_{name}"))

        ident = sb("ident", [P, P])
        group = sb("group", [P, P])
        taps = sb("taps", [P, TAPS])
        masks = sb("masks", [P, TAPS, ROWS * WIDTH])
        band = sb("band", [P, ROWS * WIDTH])
        xin = sb("xin", [P, 2, KC, L1])
        xn = sb("xn", [P, KC, L1])
        xt = sb("xt", [P, 8, C])
        y = sb("y", [P, 2, L1])
        gst = sb("gst", [P, KC, 12])
        gmv = sb("gmv", [P, KC, 2])
        ggm = sb("ggm", [P, KC, 2])
        gd = sb("gd", [P, KC])
        gd2 = sb("gd2", [P, KC])
        gve = sb("gve", [P, KC])
        gr = sb("gr", [P, KC])
        mhalf = sb("mhalf", [P, KC])
        bank = ctx.enter_context(nc.psum_tensor(f"{tag}_bank", [P, 8 * BANK], F32))

        const_in = sem("const_in")
        band_step = sem("band_step")
        mhalf_set = sem("mhalf_set")
        x_arrived = [sem(f"x_arrived{i}") for i in range(2)]
        gn_step = sem("gn_step")
        gm_full = sem("gm_full")
        gm_read = sem("gm_read")
        gn_rstd = sem("gn_rstd")
        xn_done = sem("xn_done")
        xt_full = sem("xt_full")
        xt_done = sem("xt_done")
        y_full = sem("y_full")
        y_done = sem("y_done")
        stored = [sem(f"stored{i}") for i in range(2)]
        held = sem("held")

        def hold(engine):
            engine.sem_inc(held, 1)

        block = ctx.enter_context(nc.Block())

        @block.sync
        def _(sp):
            sp.sem_inc(stored[0], 1)
            sp.sem_inc(stored[1], 1)
            for dst, src in ((ident[:], ident_dram), (group[:], group_dram), (masks[:], masks_dram),
                             (taps[:], taps_dram.partition_broadcast(P))):
                sp.dma_start(dst, src).then_inc(const_in, 16)

            def load(b, j):
                src = x_in[bass.ds(b, 1)].rearrange("a (k p) l -> p (a k) l", p=P)
                sp.dma_start(xin[:, j], src).then_inc(x_arrived[j], 16)

            def stores(b, bb, j):
                for k in range(KC):
                    sp.wait_ge(y_done, (b + j) * KC + k + 1 + 1)
                    sp.dma_start(x_out[bass.ds(b + j, 1), k * P:(k + 1) * P, :].rearrange("a p l -> (a p) l"),
                                 y[:, k % 2, :]).then_inc(stored[k % 2], 16)

            load(0, 0)

            def pair(b, last):
                load(b + 1, 1)
                stores(b, None, 0)
                if not last:
                    load(b + 2, 0)
                stores(b, None, 1)

            if batches > 2:
                with sp.Fori(0, batches - 2, 2) as b:
                    pair(b, False)
            pair(batches - 2, True)
            for i in range(2):
                sp.wait_ge(stored[i], batches * 32 + 1)

        @block.tensor
        def _(pe):
            pe.sem_inc(y_full, 1)
            mm = nc.tensor.matmul
            pe.wait_ge(const_in, 64)
            pe.wait_ge(band_step, TAPS)
            with pe.Fori(0, batches) as b:
                pe.wait_ge(gn_step, b * 15 + 12)
                mm(bank[:, 0:2 * KC], group[:], gmv[:].rearrange("p k s -> p (k s)"), start=True, stop=True).then_inc(gm_full, 1)
                pe.wait_ge(gn_step, b * 15 + 14)
                mm(bank[:, BANK:BANK + KC], group[:], gd2[:], start=True, stop=True).then_inc(gm_full, 1)
                pe.wait_ge(xn_done, b * KC + KC)
                for lb in range(8):
                    if lb >= 2:
                        pe.wait_ge(xt_done, b * 8 + lb - 1)
                    for k in range(KC):
                        o = (2 + lb % 2) * BANK + k * P
                        last = mm(bank[:, o:o + P], xn[:, k, lb * P:(lb + 1) * P], ident[:],
                                  start=(k == 0), stop=(k == KC - 1), is_transpose=True)
                    last.then_inc(xt_full, 1)
                pe.wait_ge(xt_done, b * 8 + 8)
                for k in range(KC):
                    if k < 2:
                        pe.wait_ge(y_done, b * KC + 1)
                    else:
                        pe.wait_ge(y_done, b * KC + k - 1 + 1)
                    started = set()
                    for j in range(8):
                        lo, hi = max(0, (4 * j - 1) * WIDTH), min(L1, (4 * j + 6) * WIDTH)
                        for q in range(2):
                            a, e = max(lo, q * BANK), min(hi, (q + 1) * BANK)
                            if a >= e:
                                continue
                            base = (4 + 2 * (k % 2)) * BANK
                            off = (4 * j - 1) * WIDTH
                            last = mm(bank[:, base + a:base + e], xt[:, j, k * P:(k + 1) * P], band[:, a - off:e - off],
                                      start=q not in started, stop=(j == (4 if q == 0 else 7)), skip_group_check=True)
                            started.add(q)
                    last.then_inc(y_full, 1)

        @block.scalar
        def _(act):
            with act.Fori(0, batches) as b:
                for lb in range(8):
                    act.wait_ge(xt_full, b * 8 + lb + 1)
                    act.wait_ge(y_full, b * KC + 1)
                    nc.scalar.activation(xt[:, lb, :], bank[:, (2 + lb % 2) * BANK:(3 + lb % 2) * BANK],
                                         ACT.Copy).then_inc(xt_done, 1)

        @block.gpsimd
        def _(pool):
            nc.gpsimd.memset(mhalf[:], -0.5).then_inc(mhalf_set, 1)
            pool.wait_ge(mhalf_set, 1)
            with pool.Fori(0, batches) as b:
                pool.wait_ge(gn_step, b * 15 + 15)
                nc.gpsimd.tensor_tensor(gr[:], gve[:], mhalf[:], ALU.pow).then_inc(gn_rstd, 1)

        @block.vector
        def _(dve):
            dve.sem_inc(y_done, 1)
            V = nc.vector
            dve.wait_ge(const_in, 64)
            V.tensor_scalar(band[:], masks[:, 0, :], taps[:, 0:1], None, ALU.mult).then_inc(band_step, 1)
            for t in range(1, TAPS):
                dve.wait_ge(band_step, t)
                V.scalar_tensor_tensor(band[:], masks[:, t, :], taps[:, t:t + 1], band[:], ALU.mult, ALU.add).then_inc(band_step, 1)

            def batch(b, bj, j, half):
                dve.wait_ge(x_arrived[j], half * 16 + 16)
                g0 = b * 15
                for k in range(KC):
                    for q in range(2):
                        V.bn_stats(gst[:, k, 6 * q:6 * q + 6], xin[:, j, k, q * BANK:(q + 1) * BANK]).then_inc(gn_step, 1)
                for k in range(KC):
                    dve.wait_ge(gn_step, g0 + 2 * k + 2)
                    hold(dve)
                    V.bn_aggr(gmv[:, k, :], gst[:, k, :]).then_inc(gn_step, 1)
                dve.wait_ge(gm_full, b * 2 + 1)
                V.tensor_copy(ggm[:].rearrange("p k s -> p (k s)"), bank[:, 0:2 * KC]).then_inc(gm_read, 1)
                dve.wait_ge(gm_read, b * 2 + 1)
                V.tensor_tensor(gd[:], gmv[:, :, 0], ggm[:, :, 0], ALU.subtract).then_inc(gn_step, 1)
                dve.wait_ge(gn_step, g0 + 13)
                V.tensor_tensor(gd2[:], gd[:], gd[:], ALU.mult).then_inc(gn_step, 1)
                dve.wait_ge(gm_full, b * 2 + 2)
                V.tensor_tensor(gve[:], bank[:, BANK:BANK + KC], ggm[:, :, 1], ALU.add).then_inc(gm_read, 1)
                dve.wait_ge(gm_read, b * 2 + 2)
                V.tensor_scalar(gve[:], gve[:], EPS, None, ALU.add).then_inc(gn_step, 1)
                dve.wait_ge(gn_rstd, b + 1)
                for k in range(KC):
                    V.tensor_scalar(xn[:, k, :], xin[:, j, k, :], ggm[:, k, 0:1], gr[:, k:k + 1],
                                    ALU.subtract, ALU.mult).then_inc(xn_done, 1)
                for k in range(KC):
                    dve.wait_ge(y_full, b * KC + k + 1 + 1)
                    if k >= 2:
                        dve.wait_ge(stored[k % 2], b * 32 + 16 + 1)
                    else:
                        dve.wait_ge(stored[k % 2], b * 32 + 1)
                    base = (4 + 2 * (k % 2)) * BANK
                    V.tensor_tensor(y[:, k % 2, :], bank[:, base:base + L1], xin[:, j, k, :], ALU.add).then_inc(y_done, 1)

            with dve.Fori(0, batches // 2) as pair:
                for j in range(2):
                    batch(pair * 2 + j, None, j, pair)


def attention_layer(nc, tag, x_in, x_out, wqkv_dram, wproj_dram, vec_dram, ident_dram, group_dram, mean_dram, batches):
    ctx = ExitStack()
    with ctx:
        def sb(name, shape):
            return ctx.enter_context(nc.sbuf_tensor(f"{tag}_{name}", shape, F32))

        def sem(name):
            return ctx.enter_context(nc.semaphore(f"{tag}_{name}"))

        ident = sb("ident", [P, P])
        group = sb("group", [P, P])
        mean = sb("mean", [P, P])
        wqkv = sb("wqkv", [P, KC, 3 * C])
        wproj = sb("wproj", [P, KC, C])
        vec = sb("vec", [P, 24])
        gamma, beta, bq, bv, bo = vec[:, 0:4], vec[:, 4:8], vec[:, 8:16], vec[:, 16:20], vec[:, 20:24]
        xin = sb("xin", [P, KC, L1])
        xf = sb("xf", [P, KC, L1])
        qk = sb("qk", [P, 8, L1])
        vt = sb("vt", [P, NB, C])
        vals = sb("vals", [P, KC, L1])
        prob = sb("prob", [P, 2, L1])
        pt = sb("pt", [P, 2, L1])
        vn = sb("vn", [P, C])
        y = sb("y", [P, 2, L1])
        mx = sb("mx", [P, 2])
        nbias = sb("nbias", [P, 2])
        rs = sb("rs", [P, 2, HEADS])
        rr = sb("rr", [P, HEADS])
        gst = sb("gst", [P, KC, 12])
        gmv = sb("gmv", [P, KC, 2])
        ggm = sb("ggm", [P, KC, 2])
        gd = sb("gd", [P, KC])
        gd2 = sb("gd2", [P, KC])
        gve = sb("gve", [P, KC])
        gr = sb("gr", [P, KC])
        st = sb("st", [P, KC, 2])
        st2 = sb("st2", [P, KC])
        lm = sb("lm", [P, 2])
        ld = sb("ld", [P, KC])
        ld2 = sb("ld2", [P, KC])
        lve = sb("lve", [P, 1])
        lr = sb("lr", [P, 1])
        sc = sb("sc", [P, KC])
        aa = sb("aa", [P, KC])
        bb = sb("bb", [P, KC])
        cc = sb("cc", [P, KC])
        mhalf = sb("mhalf", [P, KC])
        bank = ctx.enter_context(nc.psum_tensor(f"{tag}_bank", [P, 8 * BANK], F32))

        def bk(i, n=BANK):
            return bank[:, i * BANK:i * BANK + n]

        T_QK, T_V, T_O, TILES = 0, 16, 24, 32
        BY_ACT = {t for t in range(T_QK, T_O) if t % 2 == 0}
        PER_A, PER_D = len(BY_ACT), TILES - len(BY_ACT)

        def left(t):
            return sum((i in BY_ACT) == (t in BY_ACT) for i in range(t + 1))

        UNITS = NB * HEADS
        STAT_BLOCKS = (2, 3, 4, 5)
        STEPS = 8 + 4 + 2 + 1 + 3 + 2 + 1 + 5

        const_in = sem("const_in")
        mhalf_set = sem("mhalf_set")
        x_arrived = sem("x_arrived")
        res_in = [sem(f"res_in{i}") for i in range(2)]
        stat_full = sem("stat_full")
        stat_dve = sem("stat_dve")
        gn_step = sem("gn_step")
        rstd = sem("rstd")
        xf_done = sem("xf_done")
        tile_full = sem("tile_full")
        tile_act = sem("tile_act")
        tile_dve = sem("tile_dve")
        s_full = sem("s_full")
        max_done = sem("max_done")
        bias_done = sem("bias_done")
        p_full = sem("p_full")
        pt_full = sem("pt_full")
        pt_dve = sem("pt_dve")
        pt_act = sem("pt_act")
        o_full = sem("o_full")
        rr_done = sem("rr_done")
        vn_done = sem("vn_done")
        vtr_full = sem("vtr_full")
        vals_done = sem("vals_done")
        stored = [sem(f"stored{i}") for i in range(2)]
        held = sem("held")

        def hold(engine):
            engine.sem_inc(held, 1)

        block = ctx.enter_context(nc.Block())

        @block.sync
        def _(sp):
            sp.sem_inc(stored[0], 1)
            sp.sem_inc(stored[1], 1)
            for dst, src in ((wqkv[:], wqkv_dram), (wproj[:], wproj_dram), (vec[:], vec_dram),
                             (ident[:], ident_dram), (group[:], group_dram), (mean[:], mean_dram)):
                sp.dma_start(dst, src).then_inc(const_in, 16)
            def load_x(b):
                sp.dma_start(xin[:], x_in[bass.ds(b, 1)].rearrange("a (k p) l -> p (a k) l", p=P)).then_inc(x_arrived, 16)

            def rows(x, b, m):
                return x[bass.ds(b, 1), m * P:(m + 1) * P, :].rearrange("a p l -> (a p) l")

            def load_res(b, m):
                sp.wait_ge(stored[m % 2], b * 32 + 16 * (m // 2) + 1)
                sp.dma_start(y[:, m % 2, :], rows(x_in, b, m)).then_inc(res_in[m % 2], 16)

            def body(b, ahead):
                load_res(b, 0)
                load_res(b, 1)
                if ahead:
                    sp.wait_ge(xf_done, b * KC + KC)
                    load_x(b + 1)
                for m in range(KC):
                    sp.wait_ge(tile_dve, b * PER_D + left(T_O + 2 * m + 1) + 1)
                    sp.dma_start(rows(x_out, b, m), y[:, m % 2, :]).then_inc(stored[m % 2], 16)
                    if m < 2:
                        load_res(b, m + 2)

            load_x(0)
            with sp.Fori(0, batches - 1) as b:
                body(b, True)
            body(batches - 1, False)
            for i in range(2):
                sp.wait_ge(stored[i], batches * 32 + 1)

        @block.tensor
        def _(pe):
            mm = nc.tensor.matmul
            pe.wait_ge(const_in, 96)

            def tile_wait(b, t):
                if t < 8:
                    pe.wait_ge(tile_dve, b * PER_D + 1)
                elif t - 8 in BY_ACT:
                    pe.wait_ge(tile_act, b * PER_A + left(t - 8))
                else:
                    pe.wait_ge(tile_dve, b * PER_D + left(t - 8) + 1)

            def scores(b, u):
                i, h = u // HEADS, u % HEADS
                if u >= 2:
                    pe.wait_ge(p_full, b * UNITS + u - 1)
                r0 = (h % 2) * DH
                for q in range(2):
                    o = (u % 2) * 2 * BANK + q * BANK
                    last = mm(bank[:, o:o + BANK], qk[r0:r0 + DH, h // 2, i * P:(i + 1) * P],
                              qk[r0:r0 + DH, 4 + h // 2, q * BANK:(q + 1) * BANK], start=True, stop=True)
                last.then_inc(s_full, 1)

            def turn(b, u):
                pe.wait_ge(p_full, b * UNITS + u + 1)
                if u >= 1:
                    pe.wait_ge(pt_dve, b * UNITS + u)
                    pe.wait_ge(pt_act, b * UNITS + u)
                for m in range(NB):
                    last = mm(bank[:, 4 * BANK + m * P:4 * BANK + (m + 1) * P], prob[:, u % 2, m * P:(m + 1) * P],
                              ident[:], start=(m % 4 == 0), stop=(m % 4 == 3), is_transpose=True)
                last.then_inc(pt_full, 1)

            def weigh(b, u):
                i, h = u // HEADS, u % HEADS
                pe.wait_ge(pt_dve, b * UNITS + u + 1)
                pe.wait_ge(pt_act, b * UNITS + u + 1)
                if h == 0 and i > 0:
                    pe.wait_ge(vn_done, b * NB + i)
                for m in range(NB):
                    last = mm(bank[:, 6 * BANK + h * DH:6 * BANK + (h + 1) * DH], pt[:, u % 2, m * P:(m + 1) * P],
                              vt[:, m, h * DH:(h + 1) * DH], start=(m == 0), stop=(m == NB - 1))
                last.then_inc(o_full, 1)

            def back(b, i, ahead):
                pe.wait_ge(vn_done, b * NB + i + 1)
                if i > 0:
                    pe.wait_ge(vals_done, b * NB + i)
                if ahead and i in STAT_BLOCKS:
                    pe.wait_ge(stat_dve, b * 4 + 4 + STAT_BLOCKS.index(i) + 1)
                for k in range(KC):
                    last = mm(bank[:, 7 * BANK + k * P:7 * BANK + (k + 1) * P], vn[:, k * P:(k + 1) * P], ident[:],
                              start=(k == 0), stop=(k == KC - 1), is_transpose=True)
                last.then_inc(vtr_full, 1)

            def statistic(b, n):
                pe.wait_ge(gn_step, b * STEPS + (12, 14, 18, 20)[n])
                ps = bk(7)
                if n == 0:
                    last = mm(ps[:, 0:2 * KC], group[:], gmv[:].rearrange("p k s -> p (k s)"), start=True, stop=True)
                elif n == 1:
                    last = mm(ps[:, 0:KC], group[:], gd2[:], start=True, stop=True)
                else:
                    for k in range(KC):
                        rhs = st[:, k, :] if n == 2 else ld2[:, k:k + 1]
                        last = mm(ps[:, 0:4 - n], mean[:], rhs, start=(k == 0), stop=(k == KC - 1))
                last.then_inc(stat_full, 1)

            def body(b, ahead):
                pe.wait_ge(xf_done, b * KC + KC)
                for m in range(8):
                    for q in range(2):
                        t = T_QK + 2 * m + q
                        tile_wait(b, t)
                        for k in range(KC):
                            last = mm(bk(t % 8), wqkv[:, k, m * P:(m + 1) * P], xf[:, k, q * BANK:(q + 1) * BANK],
                                      start=(k == 0), stop=(k == KC - 1))
                        last.then_inc(tile_full, 1)
                for i in range(NB):
                    t = T_V + i
                    tile_wait(b, t)
                    for k in range(KC):
                        last = mm(bk(t % 8), xf[:, k, i * P:(i + 1) * P], wqkv[:, k, 2 * C:3 * C],
                                  start=(k == 0), stop=(k == KC - 1))
                    last.then_inc(tile_full, 1)
                pe.wait_ge(tile_act, b * PER_A + PER_A)
                pe.wait_ge(tile_dve, b * PER_D + left(T_V + 7) + 1)
                for u in range(UNITS + 2):
                    if u < UNITS:
                        scores(b, u)
                    if 1 <= u <= UNITS:
                        turn(b, u - 1)
                    if u >= 2:
                        weigh(b, u - 2)
                        i, h = (u - 2) // HEADS, (u - 2) % HEADS
                        if i > 0 and h == 1:
                            back(b, i - 1, ahead)
                        if ahead and h == 6 and i in STAT_BLOCKS:
                            pe.wait_ge(vals_done, b * NB + i)
                            statistic(b + 1, STAT_BLOCKS.index(i))
                back(b, NB - 1, ahead)
                pe.wait_ge(vals_done, b * NB + NB)
                for m in range(KC):
                    for q in range(2):
                        t = T_O + 2 * m + q
                        if t >= T_O + 8:
                            tile_wait(b, t)
                        for k in range(KC):
                            last = mm(bk(t % 8), wproj[:, k, m * P:(m + 1) * P], vals[:, k, q * BANK:(q + 1) * BANK],
                                      start=(k == 0), stop=(k == KC - 1))
                        last.then_inc(tile_full, 1)

            for n in range(4):
                if n > 0:
                    pe.wait_ge(stat_dve, n)
                statistic(0, n)
            with pe.Fori(0, batches - 1) as b:
                body(b, True)
            body(batches - 1, False)

        @block.scalar
        def _(act):
            A = nc.scalar.activation
            act.wait_ge(const_in, 96)

            def exps(b, u):
                act.wait_ge(bias_done, b * UNITS + u + 1)
                i, h = u // HEADS, u % HEADS
                if u >= 2:
                    act.wait_ge(pt_full, b * UNITS + u - 1)
                if h == 0 and i >= 2:
                    act.wait_ge(rr_done, b * NB + i - 1)
                A(prob[:, u % 2, :], bank[:, (u % 2) * 2 * BANK:(u % 2) * 2 * BANK + L1], ACT.Exp,
                  bias=nbias[:, u % 2:u % 2 + 1], scale=SCALE, accum_out=rs[:, i % 2, h:h + 1]).then_inc(p_full, 1)

            def half(b, u):
                act.wait_ge(pt_full, b * UNITS + u + 1)
                if u >= 2:
                    act.wait_ge(o_full, b * UNITS + u - 1)
                A(pt[:, u % 2, BANK:], bank[:, 5 * BANK:6 * BANK], ACT.Copy).then_inc(pt_act, 1)

            def values(b, i):
                act.wait_ge(vtr_full, b * NB + i + 1)
                for k in range(KC):
                    last = A(vals[:, k, i * P:(i + 1) * P], bank[:, 7 * BANK + k * P:7 * BANK + (k + 1) * P],
                             ACT.Identity, bias=bv[:, k:k + 1])
                last.then_inc(vals_done, 1)

            with act.Fori(0, batches) as b:
                for t in sorted(BY_ACT):
                    act.wait_ge(tile_full, b * TILES + t + 1)
                    if t < T_V:
                        m, q = (t - T_QK) // 2, (t - T_QK) % 2
                        A(qk[:, m, q * BANK:(q + 1) * BANK], bk(t % 8), ACT.Identity, bias=bq[:, m:m + 1]).then_inc(tile_act, 1)
                    else:
                        A(vt[:, t - T_V, :], bk(t % 8), ACT.Copy).then_inc(tile_act, 1)
                for u in range(UNITS + 1):
                    if u < UNITS:
                        exps(b, u)
                    if u >= 1:
                        half(b, u - 1)
                        if u - 1 > 10 and (u - 1) % HEADS == 3:
                            values(b, (u - 1) // HEADS - 1)
                values(b, NB - 1)

        @block.gpsimd
        def _(pool):
            nc.gpsimd.memset(mhalf[:], -0.5).then_inc(mhalf_set, 1)
            pool.wait_ge(mhalf_set, 1)
            with pool.Fori(0, batches) as b:
                g0 = b * STEPS
                pool.wait_ge(gn_step, g0 + 15)
                nc.gpsimd.tensor_tensor(gr[:], gve[:], mhalf[:], ALU.pow).then_inc(rstd, 1)
                pool.wait_ge(gn_step, g0 + 21)
                nc.gpsimd.tensor_tensor(lr[:], lve[:], mhalf[:, 0:1], ALU.pow).then_inc(rstd, 1)

        @block.vector
        def _(dve):
            dve.sem_inc(tile_dve, 1)
            V = nc.vector
            dve.wait_ge(const_in, 96)

            def maximum(b, u):
                dve.wait_ge(s_full, b * UNITS + u + 1)
                if u >= 2:
                    dve.wait_ge(p_full, b * UNITS + u - 1)
                V.reduce_max(mx[:, u % 2:u % 2 + 1], bank[:, (u % 2) * 2 * BANK:(u % 2) * 2 * BANK + L1], AX.X).then_inc(max_done, 1)
                dve.wait_ge(max_done, b * UNITS + u + 1)
                V.tensor_scalar(nbias[:, u % 2:u % 2 + 1], mx[:, u % 2:u % 2 + 1], -SCALE, None, ALU.mult).then_inc(bias_done, 1)

            def half(b, u):
                dve.wait_ge(pt_full, b * UNITS + u + 1)
                if u >= 2:
                    dve.wait_ge(o_full, b * UNITS + u - 1)
                V.tensor_copy(pt[:, u % 2, 0:BANK], bank[:, 4 * BANK:5 * BANK]).then_inc(pt_dve, 1)

            def normalise(b, i):
                dve.wait_ge(p_full, b * UNITS + (i + 1) * HEADS)
                V.reciprocal(rr[:], rs[:, i % 2, :]).then_inc(rr_done, 1)
                dve.wait_ge(rr_done, b * NB + i + 1)
                dve.wait_ge(o_full, b * UNITS + (i + 1) * HEADS)
                if i > 0:
                    dve.wait_ge(vtr_full, b * NB + i)
                V.tensor_tensor(vn[:].rearrange("p (h d) -> p h d", d=DH),
                                bk(6).rearrange("p (h d) -> p h d", d=DH),
                                rr[:].unsqueeze(2).broadcast_to([P, HEADS, DH]), ALU.mult).then_inc(vn_done, 1)

            def norm_piece(b, j):
                done = [b * STEPS + (0, 2, 4, 6, 8, 12, 14, 15, 18, 20, 21)[min(j, 10)]]

                def step(ins, wait=True):
                    done[0] = done[0] + 1
                    ins.then_inc(gn_step, 1)
                    if wait:
                        dve.wait_ge(gn_step, done[0])

                def read(ins, i):
                    ins.then_inc(stat_dve, 1)
                    dve.wait_ge(stat_dve, b * 4 + i + 1)

                if j < KC:
                    dve.wait_ge(x_arrived, b * 16 + 16)
                    for q in range(2):
                        step(V.bn_stats(gst[:, j, 6 * q:6 * q + 6], xin[:, j, q * BANK:(q + 1) * BANK]), False)
                elif j == 4:
                    dve.wait_ge(gn_step, b * STEPS + 8)
                    hold(dve)
                    for k in range(KC):
                        step(V.bn_aggr(gmv[:, k, :], gst[:, k, :]), False)
                elif j == 5:
                    dve.wait_ge(stat_full, b * 4 + 1)
                    read(V.tensor_copy(ggm[:].rearrange("p k s -> p (k s)"), bk(7)[:, 0:2 * KC]), 0)
                    step(V.tensor_tensor(gd[:], gmv[:, :, 0], ggm[:, :, 0], ALU.subtract))
                    step(V.tensor_tensor(gd2[:], gd[:], gd[:], ALU.mult))
                elif j == 6:
                    dve.wait_ge(stat_full, b * 4 + 2)
                    read(V.tensor_tensor(gve[:], bk(7)[:, 0:KC], ggm[:, :, 1], ALU.add), 1)
                    step(V.tensor_scalar(gve[:], gve[:], EPS, None, ALU.add))
                elif j == 7:
                    dve.wait_ge(rstd, b * 2 + 1)
                    step(V.tensor_tensor(st2[:], gmv[:, :, 1], gr[:], ALU.mult))
                    step(V.tensor_tensor(st[:, :, 0], gd[:], gr[:], ALU.mult))
                    step(V.tensor_tensor(st[:, :, 1], st2[:], gr[:], ALU.mult))
                elif j == 8:
                    dve.wait_ge(stat_full, b * 4 + 3)
                    read(V.tensor_copy(lm[:], bk(7)[:, 0:2]), 2)
                    step(V.tensor_scalar(ld[:], st[:, :, 0], lm[:, 0:1], None, ALU.subtract))
                    step(V.tensor_tensor(ld2[:], ld[:], ld[:], ALU.mult))
                elif j == 9:
                    dve.wait_ge(stat_full, b * 4 + 4)
                    read(V.tensor_tensor(lve[:], bk(7)[:, 0:1], lm[:, 1:2], ALU.add), 3)
                    step(V.tensor_scalar(lve[:], lve[:], EPS, None, ALU.add))
                elif j == 10:
                    dve.wait_ge(rstd, b * 2 + 2)
                    step(V.tensor_scalar(sc[:], gamma, lr[:, 0:1], None, ALU.mult))
                    step(V.tensor_tensor(aa[:], sc[:], gr[:], ALU.mult))
                    step(V.tensor_tensor(bb[:], ggm[:, :, 0], gr[:], ALU.mult))
                    step(V.scalar_tensor_tensor(cc[:], bb[:], lm[:, 0:1], sc[:], ALU.add, ALU.mult))
                    step(V.tensor_tensor(bb[:], beta, cc[:], ALU.subtract))
                else:
                    k = j - 11
                    V.tensor_scalar(xf[:, k, :], xin[:, k, :], aa[:, k:k + 1], bb[:, k:k + 1], ALU.mult, ALU.add).then_inc(xf_done, 1)

            NORM_UNITS = [4, 6, 8, 10, 12] + [26, 34, 37, 42, 50, 54] + [56, 58, 60, 62]

            def body(b, ahead):
                for t in range(T_QK, T_O):
                    if t in BY_ACT:
                        continue
                    dve.wait_ge(tile_full, b * TILES + t + 1)
                    if t < T_V:
                        m, q = (t - T_QK) // 2, (t - T_QK) % 2
                        V.tensor_scalar(qk[:, m, q * BANK:(q + 1) * BANK], bk(t % 8), bq[:, m:m + 1], None, ALU.add).then_inc(tile_dve, 1)
                    else:
                        V.tensor_copy(vt[:, t - T_V, :], bk(t % 8)).then_inc(tile_dve, 1)
                for u in range(UNITS + 2):
                    if u < UNITS:
                        maximum(b, u)
                    if 1 <= u <= UNITS:
                        half(b, u - 1)
                    if u >= 2 and (u - 2) % HEADS == HEADS - 1:
                        normalise(b, (u - 2) // HEADS)
                    if ahead and u in NORM_UNITS:
                        norm_piece(b + 1, NORM_UNITS.index(u))
                for m in range(KC):
                    for q in range(2):
                        t = T_O + 2 * m + q
                        dve.wait_ge(tile_full, b * TILES + t + 1)
                        dve.wait_ge(res_in[m % 2], b * 32 + 16 * (m // 2) + 16)
                        o = y[:, m % 2, q * BANK:(q + 1) * BANK]
                        V.scalar_tensor_tensor(o, bk(t % 8), bo[:, m:m + 1], o, ALU.add, ALU.add).then_inc(tile_dve, 1)

            for j in range(len(NORM_UNITS)):
                norm_piece(0, j)
            with dve.Fori(0, batches - 1) as b:
                body(b, True)
            body(batches - 1, False)


def build_program(nc, a, batches):
    shape = (batches, C, L1)
    between = [nc.dram_tensor(f"x_after_{i}", shape, F32, kind="Internal").ap() for i in range(3)]
    ssm_layer(nc, "l0", a["x"], between[0], a["w0"], a["nat0"], a["low0"], a["ident"], a["group"], batches)
    conv_layer(nc, "l1", between[0], between[1], a["taps"], a["masks"], a["ident"], a["group"], batches)
    ssm_layer(nc, "l2", between[1], between[2], a["w2"], a["nat2"], a["low2"], a["ident"], a["group"], batches)
    attention_layer(nc, "l3", between[2], a["out"], a["wqkv"], a["wproj"], a["vec"], a["ident"], a["group"],
                    a["mean"], batches)


def chunks(m):
    return np.ascontiguousarray(m.reshape(m.shape[0] // P, P, -1).transpose(1, 0, 2))


def ssm_weights(g):
    parts = [g("in_w")[D:].T] + [g(n).transpose(1, 2, 3, 0).reshape(D, 4 * D) for n in ("c2_w", "c3_w")]
    parts += [g("out_w").T] + [g(f"xw{i}")[R:].T for i in (1, 2, 3)] + [g(f"Al{i}") for i in (1, 2, 3)]
    parts += [g(n)[:, None] for n in ("in_b", "c1_b", "c2_b", "c3_b", "out_b")]
    parts += [g(f"{n}{i}")[:, None] for n in ("dtb", "Dv", "g", "be") for i in (1, 2, 3)]
    w = np.concatenate([chunks(m).reshape(P, -1) for m in parts], axis=1)
    assert w.shape[1] == W_TOTAL
    nat = chunks(np.concatenate([g("in_w")[:D], g("c1_w").T], axis=1))
    low = np.stack([np.stack([g(f"xw{i}")[:R] for i in (1, 2, 3)], axis=1),
                    np.stack([g(f"dtw{i}").T for i in (1, 2, 3)], axis=1)], axis=1)
    return np.ascontiguousarray(w), nat, np.ascontiguousarray(low)


def band_masks():
    m = np.zeros((4, WIDTH, TAPS, ROWS, WIDTH), np.float32)
    for a in range(4):
        for b in range(4):
            for s in range(4):
                for w in range(WIDTH):
                    if 0 <= w + b - 1 < WIDTH:
                        m[s, w, 4 * a + b, s + a, w + b - 1] = 1.0
    return m.reshape(P, TAPS, ROWS * WIDTH)


def kernel(**inputs):
    import concourse.bacc as bacc
    from concourse.bass_utils import run_bass_kernel_spmd

    def layer(i):
        return lambda name: np.asarray(inputs[f"L{i}_conv_{name}"])

    x = np.asarray(inputs["x"])
    batches = x.shape[0]
    same_group = np.arange(P)[:, None] // 16 == np.arange(P)[None, :] // 16
    arrays = {"x": np.ascontiguousarray(x.reshape(batches, C, L1)),
              "ident": np.eye(P, dtype=np.float32),
              "group": np.where(same_group, np.float32(1 / 16), np.float32(0)),
              "mean": np.full((P, P), 1 / C, np.float32),
              "masks": band_masks(),
              "taps": np.ascontiguousarray(np.asarray(inputs["L1_conv_kernel"]).reshape(TAPS)),
              "wqkv": chunks(layer(3)("w_qkv").T), "wproj": chunks(layer(3)("w_proj").T),
              "vec": np.concatenate([chunks(layer(3)(n)[:, None])[:, :, 0]
                                     for n in ("gn_gamma", "gn_beta", "b_qkv", "b_proj")], axis=1)}
    for i in (0, 2):
        arrays[f"w{i}"], arrays[f"nat{i}"], arrays[f"low{i}"] = ssm_weights(layer(i))

    nc = bacc.Bacc("TRN2", target_bir_lowering=False, num_devices=1)
    aps = {n: nc.dram_tensor(f"in_{n}", a.shape, mybir.dt.from_np(a.dtype), kind="ExternalInput").ap()
           for n, a in arrays.items()}
    aps["out"] = nc.dram_tensor("out", arrays["x"].shape, F32, kind="ExternalOutput").ap()
    build_program(nc, aps, batches)
    r = run_bass_kernel_spmd(nc, [{f"in_{n}": np.ascontiguousarray(a) for n, a in arrays.items()}], core_ids=[0])
    return r.results[0]["out"].reshape(x.shape)
```
